# Optimizing a Trainium2 kernel written in Bass

```python
import numpy as np
import jax
import jax.numpy as jnp

def _softmax(x, axis=-1):
    return jax.nn.softmax(x, axis=axis)

def _gelu(x):
    return jax.nn.gelu(x, approximate=True)

def _silu(x):
    return jax.nn.silu(x)

def _sigmoid(x):
    return jax.nn.sigmoid(x)

def _layernorm(x, axis=-1, eps=1e-05):
    m = jnp.mean(x, axis=axis, keepdims=True)
    v = jnp.var(x, axis=axis, keepdims=True)
    return (x - m) / jnp.sqrt(v + eps)

def _scatter_add(tgt, idx, src, axis=0):
    return tgt.at[idx].add(src)

def _segment_sum(src, seg, n):
    return jax.ops.segment_sum(src, seg, n)
kernel_name = 'mk_macaron_d2_jaxref_r8_7f5ae3'

def setup_inputs(seed: int=0):
    np.random.seed(seed)
    _w = jnp.asarray

    def _L0_attn_setup():
        import jax, jax.numpy as jnp
        import numpy as np
        B, T, DIM, H = (4, 128, 128, 16)
        D = DIM // H

        def _lin(x, Wt, bias):
            return x @ Wt.T + bias

        def _l2norm(x, eps=1e-12):
            n = jnp.sqrt(jnp.sum(x * x, axis=-1, keepdims=True))
            return x / jnp.maximum(n, eps)
        key = jax.random.key(seed)
        ks = jax.random.split(key, 18)
        W = lambda k: jax.random.normal(k, (DIM, DIM), jnp.float32) * 0.02
        b = lambda k: jax.random.normal(k, (DIM,), jnp.float32) * 0.02
        return {'x': jax.random.normal(ks[0], (B, T, DIM), jnp.float32), 'Wsq': W(ks[1]), 'bsq': b(ks[2]), 'Wsk': W(ks[3]), 'bsk': b(ks[4]), 'Wsv': W(ks[5]), 'bsv': b(ks[6]), 'Wg': jax.random.normal(ks[7], (H, DIM), jnp.float32) * 0.02, 'bg': jax.random.normal(ks[8], (H,), jnp.float32) * 0.02, 'Wq': W(ks[9]), 'bq': b(ks[10]), 'Wk': W(ks[11]), 'bk': b(ks[12]), 'Wv': W(ks[13]), 'bv': b(ks[14]), 'Wo': W(ks[15]), 'bo': b(ks[16]), 'temp': jnp.ones((1, H, 1, 1), jnp.float32)}
    _L0_attn_in = _L0_attn_setup()

    def _L0_ffn_setup():
        import jax, jax.numpy as jnp
        import numpy as np
        ALPHA = 1.0
        key = jax.random.key(seed)
        ks = jax.random.split(key, 7)
        B, S, IN, OUT = (8, 1024, 128, 128)
        RANK, DDIM, UDIM = (4, 100, 50)
        return {'hidden_states': jax.random.normal(ks[0], (B, S, IN), dtype=jnp.float32), 'W': jax.random.normal(ks[1], (OUT, IN), dtype=jnp.float32) * 0.02, 'b': jax.random.normal(ks[2], (OUT,), dtype=jnp.float32) * 0.02, 'lora_down': jax.random.normal(ks[3], (RANK, DDIM), dtype=jnp.float32) * 0.1, 'lora_up': jax.random.normal(ks[4], (UDIM, RANK), dtype=jnp.float32) * 0.1, 'down_aux': jax.random.normal(ks[5], (DDIM, IN), dtype=jnp.float32) * 0.03, 'up_aux': jax.random.normal(ks[6], (OUT, UDIM), dtype=jnp.float32) * 0.03}
    _L0_ffn_in = _L0_ffn_setup()

    def _L1_attn_setup():
        import jax, jax.numpy as jnp
        import numpy as np
        B, L, HID = (2, 256, 128)
        H = 16
        D = HID // H
        LR = 16
        EPS = 1e-05
        GLN = 16.0
        SCALE = D ** (-0.5)

        def _reference_tuple_inner(x, Wq, Wk, Wv, Wg1, Wg2, bg2, Wg, g_norm_w, Wo):
            Bb, Ll, Hid = x.shape
            q = (x @ Wq).reshape(Bb, Ll, H, D)
            k = (x @ Wk).reshape(Bb, Ll, H, D)
            v = (x @ Wv).reshape(Bb, Ll, H, D)
            gk = jax.nn.log_sigmoid(x @ Wg1 @ Wg2 + bg2).reshape(Bb, Ll, H, D) / GLN

            def step(S, inp):
                q_t, k_t, v_t, gk_t = inp
                S = jnp.exp(gk_t)[..., None] * S + k_t[..., None] * v_t[..., None, :]
                o_t = jnp.einsum('bhdv,bhd->bhv', S, q_t) * SCALE
                return (S, o_t)
            S0 = jnp.zeros((Bb, H, D, D), x.dtype)
            scan_in = tuple((jnp.moveaxis(t, 1, 0) for t in (q, k, v, gk)))
            S, o = jax.lax.scan(step, S0, scan_in)
            o = jnp.moveaxis(o, 0, 1)
            o = o * jax.lax.rsqrt(jnp.mean(o * o, axis=-1, keepdims=True) + EPS) * g_norm_w
            o = o.reshape(Bb, Ll, Hid)
            g = x @ Wg
            o = o * (g * jax.nn.sigmoid(g))
            o = o @ Wo
            return (o, S[:, None])
        key = jax.random.key(seed)
        ks = jax.random.split(key, 9)
        s = 0.02
        return {'x': jax.random.normal(ks[0], (B, L, HID), jnp.float32), 'Wq': jax.random.normal(ks[1], (HID, HID), jnp.float32) * s, 'Wk': jax.random.normal(ks[2], (HID, HID), jnp.float32) * s, 'Wv': jax.random.normal(ks[3], (HID, HID), jnp.float32) * s, 'Wg1': jax.random.normal(ks[4], (HID, LR), jnp.float32) * s, 'Wg2': jax.random.normal(ks[5], (LR, HID), jnp.float32) * s, 'bg2': jnp.zeros((HID,), jnp.float32), 'Wg': jax.random.normal(ks[6], (HID, HID), jnp.float32) * s, 'g_norm_w': jnp.ones((D,), jnp.float32), 'Wo': jax.random.normal(ks[7], (HID, HID), jnp.float32) * s}
    _L1_attn_in = _L1_attn_setup()

    def _L1_ffn_setup():
        import jax, jax.numpy as jnp
        import numpy as np
        B, N, DIM = (2, 256, 128)
        HEADS, DIM_HEAD, EXPERTS = (8, 64, 8)
        SCALE = DIM_HEAD ** (-0.5)
        key = jax.random.key(seed)
        ks = jax.random.split(key, 6)
        dim_inner = HEADS * DIM_HEAD
        return {'x': jax.random.normal(ks[0], (B, N, DIM), jnp.float32), 'w_q': jax.random.normal(ks[1], (DIM, dim_inner), jnp.float32) * 0.02, 'w_k': jax.random.normal(ks[2], (DIM, dim_inner), jnp.float32) * 0.02, 'w_gate': jax.random.normal(ks[3], (DIM, HEADS * EXPERTS), jnp.float32) * 0.02, 'value_experts': jax.random.normal(ks[4], (EXPERTS, HEADS, DIM, DIM_HEAD), jnp.float32) * 0.02, 'output_experts': jax.random.normal(ks[5], (EXPERTS, HEADS, DIM_HEAD, DIM), jnp.float32) * 0.02}
    _L1_ffn_in = _L1_ffn_setup()
    _d = {'L0_attn_x': _L0_attn_in['x'], 'L0_attn_Wsq': _L0_attn_in['Wsq'], 'L0_attn_bsq': _L0_attn_in['bsq'], 'L0_attn_Wsk': _L0_attn_in['Wsk'], 'L0_attn_bsk': _L0_attn_in['bsk'], 'L0_attn_Wsv': _L0_attn_in['Wsv'], 'L0_attn_bsv': _L0_attn_in['bsv'], 'L0_attn_Wg': _L0_attn_in['Wg'], 'L0_attn_bg': _L0_attn_in['bg'], 'L0_attn_Wq': _L0_attn_in['Wq'], 'L0_attn_bq': _L0_attn_in['bq'], 'L0_attn_Wk': _L0_attn_in['Wk'], 'L0_attn_bk': _L0_attn_in['bk'], 'L0_attn_Wv': _L0_attn_in['Wv'], 'L0_attn_bv': _L0_attn_in['bv'], 'L0_attn_Wo': _L0_attn_in['Wo'], 'L0_attn_bo': _L0_attn_in['bo'], 'L0_attn_temp': _L0_attn_in['temp'], 'L0_ffn_W': _L0_ffn_in['W'], 'L0_ffn_b': _L0_ffn_in['b'], 'L0_ffn_lora_down': _L0_ffn_in['lora_down'], 'L0_ffn_lora_up': _L0_ffn_in['lora_up'], 'L0_ffn_down_aux': _L0_ffn_in['down_aux'], 'L0_ffn_up_aux': _L0_ffn_in['up_aux'], 'L1_attn_Wq': _L1_attn_in['Wq'], 'L1_attn_Wk': _L1_attn_in['Wk'], 'L1_attn_Wv': _L1_attn_in['Wv'], 'L1_attn_Wg1': _L1_attn_in['Wg1'], 'L1_attn_Wg2': _L1_attn_in['Wg2'], 'L1_attn_bg2': _L1_attn_in['bg2'], 'L1_attn_Wg': _L1_attn_in['Wg'], 'L1_attn_g_norm_w': _L1_attn_in['g_norm_w'], 'L1_attn_Wo': _L1_attn_in['Wo'], 'L1_ffn_w_q': _L1_ffn_in['w_q'], 'L1_ffn_w_k': _L1_ffn_in['w_k'], 'L1_ffn_w_gate': _L1_ffn_in['w_gate'], 'L1_ffn_value_experts': _L1_ffn_in['value_experts'], 'L1_ffn_output_experts': _L1_ffn_in['output_experts']}
    _x0 = _d['L0_attn_x']
    _d['L0_attn_x'] = jax.random.normal(jax.random.fold_in(jax.random.key(seed), 1), (16, 256, 128), dtype=_x0.dtype)
    del _x0
    return _d

def reference(L0_attn_x, L0_attn_Wsq, L0_attn_bsq, L0_attn_Wsk, L0_attn_bsk, L0_attn_Wsv, L0_attn_bsv, L0_attn_Wg, L0_attn_bg, L0_attn_Wq, L0_attn_bq, L0_attn_Wk, L0_attn_bk, L0_attn_Wv, L0_attn_bv, L0_attn_Wo, L0_attn_bo, L0_attn_temp, L0_ffn_W, L0_ffn_b, L0_ffn_lora_down, L0_ffn_lora_up, L0_ffn_down_aux, L0_ffn_up_aux, L1_attn_Wq, L1_attn_Wk, L1_attn_Wv, L1_attn_Wg1, L1_attn_Wg2, L1_attn_bg2, L1_attn_Wg, L1_attn_g_norm_w, L1_attn_Wo, L1_ffn_w_q, L1_ffn_w_k, L1_ffn_w_gate, L1_ffn_value_experts, L1_ffn_output_experts):

    def _L0_attn_ref(x, Wsq, bsq, Wsk, bsk, Wsv, bsv, Wg, bg, Wq, bq, Wk, bk, Wv, bv, Wo, bo, temp):
        import jax, jax.numpy as jnp
        import numpy as np
        B, T, DIM, H = (4, 128, 128, 16)
        D = DIM // H

        def _lin(x, Wt, bias):
            return x @ Wt.T + bias

        def _l2norm(x, eps=1e-12):
            n = jnp.sqrt(jnp.sum(x * x, axis=-1, keepdims=True))
            return x / jnp.maximum(n, eps)
        Bx, Tx, C = x.shape
        nh, hd = (H, C // H)
        sq = _lin(x, Wsq, bsq).reshape(Bx, Tx, nh, hd)
        sk = _lin(x, Wsk, bsk).reshape(Bx, Tx, nh, hd)
        sv = _lin(x, Wsv, bsv).reshape(Bx, Tx, nh, hd)
        g = jnp.exp(-jax.nn.softplus(_lin(x, Wg, bg)))

        def step(M, inp):
            g_t, k_t, v_t, q_t = inp
            M = g_t[..., None, None] * M + k_t[..., None] * v_t[..., None, :]
            h = jnp.einsum('bhd,bhde->bhe', q_t, M)
            return (M, h)
        xs = (g.transpose(1, 0, 2), sk.transpose(1, 0, 2, 3), sv.transpose(1, 0, 2, 3), sq.transpose(1, 0, 2, 3))
        M0 = jnp.zeros((Bx, nh, hd, hd), x.dtype)
        _, hs = jax.lax.scan(step, M0, xs)
        Hseq = hs.transpose(1, 0, 2, 3).reshape(Bx, Tx, C)
        Q = _lin(Hseq, Wq, bq).reshape(Bx, Tx, nh, hd).transpose(0, 2, 1, 3)
        K = _lin(Hseq, Wk, bk).reshape(Bx, Tx, nh, hd).transpose(0, 2, 1, 3)
        V = _lin(x, Wv, bv).reshape(Bx, Tx, nh, hd).transpose(0, 2, 1, 3)
        Q = _l2norm(Q)
        K = _l2norm(K)
        scores = jnp.einsum('bhqd,bhkd->bhqk', Q, K) * jax.nn.softplus(temp)
        attn = jax.nn.softmax(scores, axis=-1)
        out = jnp.einsum('bhqk,bhkd->bhqd', attn, V).transpose(0, 2, 1, 3).reshape(Bx, Tx, C)
        return _lin(out, Wo, bo)

    def _L0_ffn_ref(hidden_states, W, b, lora_down, lora_up, down_aux, up_aux):
        import jax, jax.numpy as jnp
        import numpy as np
        ALPHA = 1.0
        lilora_weight = up_aux @ (lora_up @ (lora_down @ down_aux))
        base = jnp.einsum('bsi,oi->bso', hidden_states, W) + b
        delta = jnp.einsum('bsi,oi->bso', hidden_states, lilora_weight)
        return base + ALPHA * delta

    def _L1_attn_ref(x, Wq, Wk, Wv, Wg1, Wg2, bg2, Wg, g_norm_w, Wo):
        import jax, jax.numpy as jnp
        import numpy as np
        B, L, HID = (2, 256, 128)
        H = 16
        D = HID // H
        LR = 16
        EPS = 1e-05
        GLN = 16.0
        SCALE = D ** (-0.5)

        def _reference_tuple_inner(x, Wq, Wk, Wv, Wg1, Wg2, bg2, Wg, g_norm_w, Wo):
            Bb, Ll, Hid = x.shape
            q = (x @ Wq).reshape(Bb, Ll, H, D)
            k = (x @ Wk).reshape(Bb, Ll, H, D)
            v = (x @ Wv).reshape(Bb, Ll, H, D)
            gk = jax.nn.log_sigmoid(x @ Wg1 @ Wg2 + bg2).reshape(Bb, Ll, H, D) / GLN

            def step(S, inp):
                q_t, k_t, v_t, gk_t = inp
                S = jnp.exp(gk_t)[..., None] * S + k_t[..., None] * v_t[..., None, :]
                o_t = jnp.einsum('bhdv,bhd->bhv', S, q_t) * SCALE
                return (S, o_t)
            S0 = jnp.zeros((Bb, H, D, D), x.dtype)
            scan_in = tuple((jnp.moveaxis(t, 1, 0) for t in (q, k, v, gk)))
            S, o = jax.lax.scan(step, S0, scan_in)
            o = jnp.moveaxis(o, 0, 1)
            o = o * jax.lax.rsqrt(jnp.mean(o * o, axis=-1, keepdims=True) + EPS) * g_norm_w
            o = o.reshape(Bb, Ll, Hid)
            g = x @ Wg
            o = o * (g * jax.nn.sigmoid(g))
            o = o @ Wo
            return (o, S[:, None])
        return _reference_tuple_inner(x, Wq, Wk, Wv, Wg1, Wg2, bg2, Wg, g_norm_w, Wo)[0]

    def _L1_ffn_ref(x, w_q, w_k, w_gate, value_experts, output_experts):
        import jax, jax.numpy as jnp
        import numpy as np
        B, N, DIM = (2, 256, 128)
        HEADS, DIM_HEAD, EXPERTS = (8, 64, 8)
        SCALE = DIM_HEAD ** (-0.5)
        b, n, _ = x.shape
        q = (x @ w_q).reshape(b, n, HEADS, DIM_HEAD).transpose(0, 2, 1, 3)
        k = (x @ w_k).reshape(b, n, HEADS, DIM_HEAD).transpose(0, 2, 1, 3)
        gates = jax.nn.sigmoid((x @ w_gate).reshape(b, n, HEADS, EXPERTS).transpose(0, 2, 1, 3))
        sel = jnp.argmax(gates, axis=-1)
        gm = jax.nn.one_hot(sel, EXPERTS, dtype=x.dtype) * gates
        values = jnp.einsum('bhne,ehdk,bnd->bhnk', gm, value_experts, x)
        sim = jnp.einsum('bhid,bhjd->bhij', q * SCALE, k)
        causal_mask = jnp.triu(jnp.ones((n, n), dtype=bool), 1)
        sim = jnp.where(causal_mask, jnp.finfo(sim.dtype).min, sim)
        attn = jax.nn.softmax(sim, axis=-1)
        out = jnp.einsum('bhij,bhjk->bhik', attn, values)
        out = jnp.einsum('bhne,ehkd,bhnk->bhnd', gm, output_experts, out)
        return out.sum(axis=1)
    x = L0_attn_x
    x = x + 0.5 * _L0_ffn_ref(_layernorm(x, axis=-1), L0_ffn_W, L0_ffn_b, L0_ffn_lora_down, L0_ffn_lora_up, L0_ffn_down_aux, L0_ffn_up_aux)
    x = x + _L0_attn_ref(_layernorm(x, axis=-1), L0_attn_Wsq, L0_attn_bsq, L0_attn_Wsk, L0_attn_bsk, L0_attn_Wsv, L0_attn_bsv, L0_attn_Wg, L0_attn_bg, L0_attn_Wq, L0_attn_bq, L0_attn_Wk, L0_attn_bk, L0_attn_Wv, L0_attn_bv, L0_attn_Wo, L0_attn_bo, L0_attn_temp)
    x = x + 0.5 * _L0_ffn_ref(_layernorm(x, axis=-1), L0_ffn_W, L0_ffn_b, L0_ffn_lora_down, L0_ffn_lora_up, L0_ffn_down_aux, L0_ffn_up_aux)
    x = x + 0.5 * _L1_ffn_ref(_layernorm(x, axis=-1), L1_ffn_w_q, L1_ffn_w_k, L1_ffn_w_gate, L1_ffn_value_experts, L1_ffn_output_experts)
    x = x + _L1_attn_ref(_layernorm(x, axis=-1), L1_attn_Wq, L1_attn_Wk, L1_attn_Wv, L1_attn_Wg1, L1_attn_Wg2, L1_attn_bg2, L1_attn_Wg, L1_attn_g_norm_w, L1_attn_Wo)
    x = x + 0.5 * _L1_ffn_ref(_layernorm(x, axis=-1), L1_ffn_w_q, L1_ffn_w_k, L1_ffn_w_gate, L1_ffn_value_experts, L1_ffn_output_experts)
    return x

_drawn_inputs = setup_inputs


def setup_inputs(seed=0):
    import zlib

    import numpy as np

    out = dict(_drawn_inputs(seed))
    spreads = {'L0_attn_temp': (1.0, 0.6), 'L1_attn_bg2': (0.0, 2.0), 'L1_attn_g_norm_w': (1.0, 0.6)}
    factors = {'L0_attn_Wsq': 8.0,
     'L0_attn_bsq': 8.0,
     'L0_attn_Wsk': 8.0,
     'L0_attn_bsk': 8.0,
     'L0_attn_Wsv': 8.0,
     'L0_attn_bsv': 8.0,
     'L0_attn_Wg': 8.0,
     'L0_attn_bg': 8.0,
     'L0_attn_Wq': 8.0,
     'L0_attn_bq': 8.0,
     'L0_attn_Wk': 8.0,
     'L0_attn_bk': 36.109,
     'L0_attn_Wv': 8.0,
     'L0_attn_bv': 8.0,
     'L0_attn_Wo': 8.0,
     'L0_attn_bo': 2.771,
     'L0_ffn_b': 2.936,
     'L0_ffn_lora_down': 3.921,
     'L0_ffn_lora_up': 4.35,
     'L0_ffn_down_aux': 3.687,
     'L0_ffn_up_aux': 4.036,
     'L1_attn_Wg1': 27.886,
     'L1_attn_Wg2': 25.097,
     'L1_ffn_w_q': 8.0,
     'L1_ffn_w_k': 8.0,
     'L1_ffn_w_gate': 8.0,
     'L1_ffn_value_experts': 8.0,
     'L1_ffn_output_experts': 8.0}
    for name, (base, spread) in spreads.items():
        noise = np.random.default_rng([zlib.crc32(name.encode()), seed]).standard_normal(out[name].shape)
        drawn = base * np.exp(spread * noise) if base else spread * noise
        out[name] = jnp.asarray(drawn.astype(out[name].dtype))
    for name, factor in factors.items():
        out[name] = (out[name] * factor).astype(out[name].dtype)
    return out
```

```python
from contextlib import ExitStack

import numpy as np

import concourse.bass as bass
from concourse import mybir

ALU = mybir.AluOpType
ACT = mybir.ActivationFunctionType
F32 = mybir.dt.float32
BF16 = mybir.dt.bfloat16
U32 = mybir.dt.uint32
AX_X = mybir.AxisListType.X

P = 128
B, T, C = 16, 256, 128
TILES = T // P
LN_EPS = 1e-5

H, D = 16, 8
GLA_RANK = 16
GLA_NORM = 16.0
RMS_EPS = 1e-5
L2_FLOOR = 1e-24
EXP_SAFE = 80.0

EH, EK, NE = 8, 64, 8
PAIRS = EH // 2
BLOCKS = 3
MASKED = -1e30
PARTS = 3
OBANK = 6

FFN_TILES = 4


def wait(eng, sem, value):
    if not (isinstance(value, int) and value <= 0):
        eng.wait_ge(sem, value)


class Chain:

    def __init__(self, eng, sem):
        self.eng, self.sem, self.base, self.n = eng, sem, 0, 0

    def link(self, ins, static=False):
        self.n += 1
        ins.then_inc(self.sem, 1)
        self.eng.wait_ge(self.sem, self.base + self.n)
        if static is not False:
            self.eng.memset(static[:], 0.0)

    def start(self, base):
        self.base, self.n = base, 0



def of(i, n=1, per=1):
    return (i + 1) * per + n


def before(i, n=1, per=1):
    return i * per + n


def credit(eng, sem, per=1):
    for _ in range(per):
        eng.nop().then_inc(sem, 1)



def ln_stats(dve, chain, s, x_tiles, tiles):
    for t in range(tiles):
        ins = dve.bn_stats(s.stats[:, t, :], x_tiles(t))
    chain.link(ins, static=s.scratch)
    for t in range(tiles):
        ins = dve.bn_aggr(s.mean_var[:, t, :], s.stats[:, t, :])
    chain.link(ins)
    dve.tensor_scalar(s.var_eps[:, 0:tiles], s.mean_var[:, 0:tiles, 1], LN_EPS, None,
                      ALU.add).then_inc(s.var_ready, 1)


def ln_apply(dve, s, x_tiles, tiles, n):
    wait(dve, s.rstd_ready, n + 1)
    wait(dve, s.norm_used, n)
    for t in range(tiles):
        ins = dve.tensor_scalar(s.norm[:, t, :], x_tiles(t), s.mean_var[:, t, 0:1], s.rstd[:, t:t + 1],
                                ALU.subtract, ALU.mult)
    ins.then_inc(s.norm_ready, 1)


def ln_power(pool, s, tiles, n):
    wait(pool, s.var_ready, n + 1)
    wait(pool, s.norm_ready, n)
    pool.tensor_tensor(s.rstd[:, 0:tiles], s.var_eps[:, 0:tiles], s.minus_half[:, 0:tiles],
                       ALU.pow).then_inc(s.rstd_ready, 1)


def ln_buffers(s, c, tiles):
    s.stats = c.sb("stats", [P, tiles, 6])
    s.mean_var = c.sb("mean_var", [P, tiles, 2])
    s.var_eps = c.sb("var_eps", [P, tiles])
    s.rstd = c.sb("rstd", [P, tiles])
    s.norm = c.sb("norm", [P, tiles, C])
    s.scratch = c.sb("scratch", [P, 1])
    s.var_ready, s.rstd_ready, s.norm_ready, s.norm_used = c.sems(
        "var_ready", "rstd_ready", "norm_ready", "norm_used")


class Stage:
    pass


class Ctx:

    def __init__(self, nc, k, phase, kind=None):
        self.nc, self.k, self.phase, self.kind, self.stack = nc, k, phase, kind or phase, ExitStack()

    def __enter__(self):
        self.stack.__enter__()
        return self

    def __exit__(self, *a):
        return self.stack.__exit__(*a)

    def sb(self, name, shape, dt=F32):
        return self.stack.enter_context(self.nc.sbuf_tensor(f"{self.phase}_{name}", shape, dt))

    def sem(self, name):
        kept = self.k.sems.setdefault(self.kind, {})
        if name not in kept:
            kept[name] = self.k.stack.enter_context(self.nc.semaphore(f"{self.kind}_{name}"))
        return kept[name]

    def sems(self, *names):
        return [self.sem(name) for name in names]


def forget(pool, k, kind):
    for sem in k.sems[kind].values():
        pool.sem_clear(sem)



def phase_load(nc, k, dram):
    with Ctx(nc, k, "load") as c, nc.Block() as block:
        loaded = c.sem("loaded")
        made = c.sem("made")
        lora1 = c.sem("lora1")
        lora1_sb = c.sem("lora1_sb")
        lora2 = c.sem("lora2")
        lora2_sb = c.sem("lora2_sb")
        lora3 = c.sem("lora3")
        bias_rows = c.sem("bias_rows")
        temp_rows = c.sem("temp_rows")
        act_step = c.sem("act_step")
        dve_step = c.sem("dve_step")
        w = k.w
        a1 = c.sb("a1", [4, C])
        a2 = c.sb("a2", [50, C])
        t1 = c.sb("t1", [P, H])
        t2 = c.sb("t2", [P, H])
        t3 = c.sb("t3", [P, H])
        names = sorted(w)

        @block.sync
        def _(sp):
            sp.dma_start(k.x[:, 0:B * TILES, :], dram["x"].rearrange("b (t p) c -> p (b t) c", p=P)) \
              .then_inc(loaded, 16)
            for name in names:
                src = dram[name]
                sp.dma_start(w[name][:], src).then_inc(loaded, 16)
            sp.wait_ge(loaded, 16 * (len(names) + 1))

        @block.gpsimd
        def _(pool):
            pool.memset(k.minus_half[:], -0.5)
            pool.memset(k.x[:, B * TILES:, :], 0.0)
            pool.memset(k.vaug[:], 1.0)
            pool.memset(k.values[:], 1.0)
            pool.memset(k.qk_pad[:], 0.0)
            pool.memset(k.ones_row[:], 1.0).then_inc(made, 1)

        @block.tensor
        def _(pe):
            pe.wait_ge(loaded, 16 * (len(names) + 1))
            pe.wait_ge(made, 1)
            pe.matmul(k.bank[0][0:4, 0:C], w["lora_downT"][:], w["down_aux"][:], start=True, stop=True).then_inc(lora1, 1)
            pe.matmul(k.bank[3][:, 0:2 * C], k.ones_row[:], w["bqk"][:], start=True, stop=True)
            pe.matmul(k.bank[4][:, 0:C], k.ones_row[:], w["bv"][:], start=True, stop=True)
            pe.matmul(k.bank[5][:, 0:C], k.ones_row[:], w["gnorm"][:], start=True, stop=True).then_inc(bias_rows, 1)
            pe.matmul(k.bank[6][:, 0:H], k.ones_row[:], w["temp"][:], start=True, stop=True).then_inc(temp_rows, 1)
            pe.wait_ge(lora1_sb, 1)
            pe.matmul(k.bank[1][0:50, 0:C], w["lora_upT"][:], a1[:], start=True, stop=True).then_inc(lora2, 1)
            pe.wait_ge(lora2_sb, 1)
            pe.matmul(k.bank[2][:, 0:C], a2[:], w["up_auxT"][:], start=True, stop=True).then_inc(lora3, 1)

        @block.vector
        def _(dve):
            chain = Chain(dve, dve_step)
            dve.wait_ge(lora1, 1)
            dve.tensor_copy(a1[:], k.bank[0][0:4, 0:C]).then_inc(lora1_sb, 1)
            dve.wait_ge(bias_rows, 1)
            for t in range(TILES):
                dve.tensor_copy(k.bqk_rows[:, t, :], k.bank[3][:, 0:2 * C])
                dve.tensor_copy(k.bv_rows[:, t, :], k.bank[4][:, 0:C])
                dve.tensor_copy(k.gnorm_rows[:, t, :], k.bank[5][:, 0:C])
            dve.wait_ge(lora2, 1)
            dve.tensor_copy(a2[:], k.bank[1][0:50, 0:C]).then_inc(lora2_sb, 1)
            dve.wait_ge(lora3, 1)
            chain.link(dve.tensor_tensor(k.w_ffn[:], k.bank[2][:, 0:C], w["ffn_WT"][:], ALU.add))
            dve.tensor_scalar(k.w_ffn[:], k.w_ffn[:], 0.5, None, ALU.mult)
            dve.tensor_scalar(k.b_ffn[:], w["ffn_b"][:], 0.5, None, ALU.mult)
            dve.tensor_scalar(k.minus_bg[:], w["gla_bg"][:], -1.0, None, ALU.mult)
            dve.wait_ge(act_step, 4)
            chain.link(dve.tensor_tensor(t3[:], t2[:], t1[:], ALU.add))
            dve.tensor_scalar(k.exp_shift[:], t3[:], EXP_SAFE, 0.0, ALU.subtract, ALU.max)
            for t in range(TILES):
                dve.memset(k.l2_scale[:, t, H:2 * H], 1.0)
                ins = dve.tensor_copy(k.l2_scale[:, t, 0:H], t3[:])
            chain.link(ins)
            chain.link(dve.tensor_scalar(k.exp_shift[:], k.exp_shift[:], -1.0, None, ALU.mult))

        @block.scalar
        def _(act):
            act.wait_ge(temp_rows, 1)
            act.activation(t1[:], k.bank[6][:, 0:H], ACT.Relu).then_inc(act_step, 1)
            act.activation(t2[:], k.bank[6][:, 0:H], ACT.Abs).then_inc(act_step, 1)
            act.wait_ge(act_step, 2)
            act.activation(t2[:], t2[:], ACT.Exp, scale=-1.0).then_inc(act_step, 1)
            act.wait_ge(act_step, 3)
            act.activation(t2[:], t2[:], ACT.Ln, bias=1.0).then_inc(act_step, 1)



def phase_ffn(nc, k, name, kind="ffn"):
    steps = B * TILES // FFN_TILES
    with Ctx(nc, k, name, kind) as c, nc.Block() as block:
        s = Stage()
        s.minus_half = k.minus_half
        ln_buffers(s, c, FFN_TILES)
        nT = c.sb("nT", [P, FFN_TILES, P])
        nT_ready, y_ready, x_done = (c.sem(n) for n in ("nT_ready", "y_ready", "x_done"))
        dve_step = c.sem("dve_step")
        turned, y = k.bank[0], k.bank[1]

        def x_at(step):
            return lambda t: k.x[:, bass.ds(step * FFN_TILES + t, 1), :].rearrange("p a c -> p (a c)")

        @block.vector
        def _(dve):
            credit(dve, x_done)
            chain = Chain(dve, dve_step)
            ln_stats(dve, chain, s, x_at(0), FFN_TILES)
            ln_apply(dve, s, x_at(0), FFN_TILES, 0)
            with dve.Fori(0, steps) as i:
                chain.start(2 * i + 2)
                ln_stats(dve, chain, s, x_at(i + 1), FFN_TILES)
                ln_apply(dve, s, x_at(i + 1), FFN_TILES, i + 1)
                dve.wait_ge(y_ready, of(i))
                x_now = k.x[:, bass.ds(i * FFN_TILES, FFN_TILES), :].rearrange("p a c -> p (a c)")
                dve.tensor_tensor(x_now, x_now, y[:, :], ALU.add).then_inc(x_done, 1)

        @block.gpsimd
        def _(pool):
            ln_power(pool, s, FFN_TILES, 0)
            with pool.Fori(0, steps) as i:
                ln_power(pool, s, FFN_TILES, i + 1)

        @block.tensor
        def _(pe):
            credit(pe, y_ready)
            with pe.Fori(0, steps) as i:
                pe.wait_ge(s.norm_ready, i + 1)
                pe.wait_ge(nT_ready, before(i))
                for t in range(FFN_TILES):
                    ins = pe.transpose(turned[:, t * P:(t + 1) * P], s.norm[:, t, :], k.w["ident"][:])
                    if t == FFN_TILES - 1:
                        ins.then_inc(s.norm_used, 1)
                pe.wait_ge(nT_ready, of(i))
                pe.wait_ge(x_done, before(i))
                for t in range(FFN_TILES):
                    out = y[:, t * C:(t + 1) * C]
                    pe.matmul(out, nT[:, t, :], k.w_ffn[:], start=True, stop=False)
                    ins = pe.matmul(out, k.ones_row[:], k.b_ffn[:], start=False, stop=True)
                ins.then_inc(y_ready, 1)

        @block.scalar
        def _(act):
            credit(act, nT_ready)
            with act.Fori(0, steps) as i:
                act.wait_ge(s.norm_used, i + 1)
                act.wait_ge(y_ready, before(i))
                act.activation(nT[:].rearrange("p a c -> p (a c)"), turned[:, :], ACT.Copy).then_inc(nT_ready, 1)



def outer_and_scan(dve, s, v_banks, v_bias, n):
    dve.wait_ge(s.qkT_ready, of(n))
    dve.wait_ge(s.prod_ready, before(n, 2, 2))
    for chunk in range(D // 2):
        dve.wait_ge(s.v_ready, of(n, chunk + 1, D // 2))
        for e in (2 * chunk, 2 * chunk + 1):
            v = v_banks[chunk % 2][:, (e % 2) * T:(e % 2 + 1) * T]
            if v_bias is None:
                ins = dve.tensor_tensor(s.kv[:, e, :], v, s.kT[:], ALU.mult)
            else:
                ins = dve.scalar_tensor_tensor(s.kv[:, e, :], v, v_bias[:, e:e + 1], s.kT[:], ALU.add, ALU.mult)
            ins.then_inc(s.kv_done, 1)
        if chunk == 0:
            dve.wait_ge(s.decay_ready, of(n))
        for e in (2 * chunk, 2 * chunk + 1):
            dve.wait_ge(s.kv_done, of(n, e + 1, D))
            dve.tensor_tensor_scan(s.M[:, e, :], s.decay[:], s.kv[:, e, :], 0.0, ALU.mult, ALU.add) \
               .then_inc(s.scan_done, 1)


def query_states(pool, s, n):
    half = D // 2
    pool.wait_ge(s.sum_ready, before(n))
    for j in range(2):
        pool.wait_ge(s.scan_done, of(n, half * (j + 1), D))
        e = slice(half * j, half * (j + 1))
        pool.tensor_tensor(s.prod[:, e, :], s.M[:, e, :], s.qT[:].unsqueeze(1).broadcast_to([P, half, T]),
                           ALU.mult).then_inc(s.prod_ready, 1)


def spread_values(pe, s, v_banks, w_v, n, banks_free):
    for chunk in range(D // 2):
        if chunk < 2:
            banks_free(chunk)
        else:
            pe.wait_ge(s.kv_done, of(n, 2 * (chunk - 1), D))
        for e in (2 * chunk, 2 * chunk + 1):
            ins = pe.matmul(v_banks[chunk % 2][:, (e % 2) * T:(e % 2 + 1) * T], w_v[:, e, :], s.nT[:],
                            start=True, stop=True)
        ins.then_inc(s.v_ready, 1)


def recurrence_buffers(s, c):
    s.nT = c.sb("nT", [P, T])
    s.qT = c.sb("qT", [P, T])
    s.kT = c.sb("kT", [P, T])
    s.decay = c.sb("decay", [P, T])
    s.kv = c.sb("kv", [P, D, T])
    s.M = c.sb("M", [P, D, T])
    s.prod = c.sb("prod", [P, D, T])
    s.z_relu = c.sb("z_relu", [P, T])
    s.z_exp = c.sb("z_exp", [P, T])
    s.softplus = c.sb("softplus", [P, T])
    s.nT_ready, s.qkz_ready, s.qkT_ready, s.z_read, s.z_parts = c.sems(
        "nT_ready", "qkz_ready", "qkT_ready", "z_read", "z_parts")
    s.softplus_ready, s.decay_ready, s.v_ready, s.kv_done, s.scan_done = c.sems(
        "softplus_ready", "decay_ready", "v_ready", "kv_done", "scan_done")
    s.prod_ready, s.sum_ready, s.act_step, s.dve_step = c.sems(
        "prod_ready", "sum_ready", "act_step", "dve_step")


def x_tile(k, seq):
    return lambda t: k.x[:, bass.ds(seq * TILES + t, 1), :].rearrange("p a c -> p (a c)")


def x_seq(k, seq):
    return k.x[:, bass.ds(seq * TILES, TILES), :].rearrange("p a c -> p (a c)")



def phase_mixer(nc, k, name, kind="mixer"):
    w = k.w
    with Ctx(nc, k, name, kind) as c, nc.Block() as block:
        s = Stage()
        s.minus_half = k.minus_half
        ln_buffers(s, c, TILES)
        recurrence_buffers(s, c)
        s.hT = c.sb("hT", [P, T])
        s.qk = c.sb("qk", [P, TILES, 2 * H, D])
        s.qk_sq = c.sb("qk_sq", [P, TILES, 2 * H, D])
        s.ss = c.sb("ss", [P, TILES * 2 * H])
        s.rs = c.sb("rs", [P, TILES * 2 * H])
        s.qp = c.sb("qp", [P, H // 4, T])
        s.kp = c.sb("kp", [P, H // 4, T])
        s.probs = c.sb("probs", [P, 3, 2 * T])
        s.rden = c.sb("rden", [P, TILES, H, 1])
        s.on = c.sb("on", [P, TILES, C])
        s.onT = c.sb("onT", [P, T])
        s.hT_ready, s.qk_rows, s.v_rows, s.qk_sb, s.qk_sq_ready = c.sems(
            "hT_ready", "qk_rows", "v_rows", "qk_sb", "qk_sq_ready")
        s.ss_ready, s.rs_ready, s.vaug_ready, s.qk_pad_ready, s.q_turned = c.sems(
            "ss_ready", "rs_ready", "vaug_ready", "qk_pad_ready", "q_turned")
        s.k_turned, s.qp_ready, s.kp_ready, s.scores_ready, s.exp_done = c.sems(
            "k_turned", "qp_ready", "kp_ready", "scores_ready", "exp_done")
        s.pv_done, s.on_ready, s.on_turned, s.onT_ready, s.out_ready = c.sems(
            "pv_done", "on_ready", "on_turned", "onT_ready", "out_ready")
        s.x_done, s.pool_step = c.sems(
            "x_done", "pool_step")
        score_bank, o_bank, misc, proj, v_banks = k.bank[0:3], k.bank[3], k.bank[4], k.bank[5], k.bank[6:8]
        o_view = o_bank[:, 0:TILES * H * (D + 1)].rearrange("p (t h e) -> p t h e", t=TILES, h=H)

        @block.tensor
        def _(pe):
            for sem, per in ((s.v_ready, D // 2), (s.sum_ready, 1), (s.qkz_ready, 1), (s.qk_rows, 1), (s.v_rows, 1),
                             (s.q_turned, 1), (s.k_turned, 1), (s.scores_ready, H), (s.pv_done, H),
                             (s.on_turned, 1), (s.out_ready, 1)):
                credit(pe, sem, per)

            def project(n):
                pe.wait_ge(s.norm_ready, n + 1)
                pe.wait_ge(s.nT_ready, before(n))
                for t in range(TILES):
                    ins = pe.transpose(misc[:, t * P:(t + 1) * P], s.norm[:, t, :], w["ident"][:])
                ins.then_inc(s.norm_used, 1)
                pe.wait_ge(s.nT_ready, of(n))
                pe.wait_ge(s.qk_sb, before(n))
                pe.matmul(proj[:, 0:T], w["mix_q"][:], s.nT[:], start=True, stop=True)
                pe.matmul(proj[:, T:2 * T], w["mix_k"][:], s.nT[:], start=True, stop=True)
                pe.matmul(score_bank[2][:, 0:T], w["mix_g"][:], s.nT[:], start=True, stop=True).then_inc(s.qkz_ready, 1)
                spread_values(pe, s, v_banks, w["mix_v"], n,
                              lambda chunk: pe.wait_ge(s.kp_ready, before(n)))

            def rows(n):
                pe.wait_ge(s.prod_ready, of(n, 2, 2))
                for e in range(D):
                    ins = pe.matmul(v_banks[1][:, 0:T], w["sum_d"][:, e, :], s.prod[:, e, :], start=(e == 0), stop=(e == D - 1))
                ins.then_inc(s.sum_ready, 1)
                for t in range(TILES):
                    ins = pe.matmul(v_banks[0][:, t * C:(t + 1) * C], s.nT[:, t * P:(t + 1) * P], w["v"][:], start=True, stop=True)
                ins.then_inc(s.v_rows, 1)
                pe.wait_ge(s.hT_ready, of(n))
                for t in range(TILES):
                    ins = pe.matmul(proj[:, t * 2 * C:(t + 1) * 2 * C], s.hT[:, t * P:(t + 1) * P], w["qk"][:], start=True, stop=True)
                ins.then_inc(s.qk_rows, 1)

            def turn_qk(n):
                pe.wait_ge(s.qk_pad_ready, of(n))
                pe.wait_ge(s.vaug_ready, of(n))
                for banks, first, turned in ((score_bank, 0, s.q_turned), (v_banks, H, s.k_turned)):
                    for g in range(H // 4):
                        for t in range(TILES):
                            at = (g % 2) * T + t * P
                            ins = pe.transpose(banks[g // 2][:, at:at + P],
                                               k.qk_pad[:, t, first + 4 * g:first + 4 * g + 4, :].rearrange("p h e -> p (h e)"),
                                               w["ident"][:])
                    ins.then_inc(turned, 1)

            def scores(i, h):
                if h == 0:
                    pe.wait_ge(s.qp_ready, of(i))
                    pe.wait_ge(s.kp_ready, of(i))
                if h == 2:
                    pe.wait_ge(s.z_read, of(i + 1))
                if h >= 3:
                    pe.wait_ge(s.exp_done, of(i, h - 2, H))
                lane = slice(32 * (h % 4), 32 * (h % 4) + D)
                for kt in range(TILES):
                    ins = pe.matmul(score_bank[h % 3][:, kt * T:(kt + 1) * T], s.kp[lane, h // 4, kt * P:(kt + 1) * P],
                                    s.qp[lane, h // 4, :], start=True, stop=True)
                ins.then_inc(s.scores_ready, 1)

            def weigh(i, h):
                if h == 0:
                    pe.wait_ge(s.x_done, before(i))
                    pe.wait_ge(s.vaug_ready, of(i))
                pe.wait_ge(s.exp_done, of(i, h + 1, H))
                for qt in range(TILES):
                    for kt in range(TILES):
                        at = kt * T + qt * P
                        ins = pe.matmul(o_view[:, qt, h, :], s.probs[:, h % 3, at:at + P], k.vaug[:, kt, h, :],
                                        start=(kt == 0), stop=(kt == TILES - 1))
                ins.then_inc(s.pv_done, 1)

            def turn_o(i):
                pe.wait_ge(s.on_ready, of(i))
                for t in range(TILES):
                    ins = pe.transpose(misc[:, T + t * P:T + (t + 1) * P], s.on[:, t, :], w["ident"][:])
                ins.then_inc(s.on_turned, 1)

            def output(i):
                pe.wait_ge(s.onT_ready, of(i))
                for t in range(TILES):
                    out = o_bank[:, t * C:(t + 1) * C]
                    pe.matmul(out, s.onT[:, t * P:(t + 1) * P], w["o"][:], start=True, stop=False)
                    ins = pe.matmul(out, k.ones_row[:], w["bo"][:], start=False, stop=True)
                ins.then_inc(s.out_ready, 1)

            project(0)
            rows(0)
            turn_qk(0)
            with pe.Fori(0, B) as i:
                project(i + 1)
                for h in range(H + 2):
                    if h < H:
                        scores(i, h)
                    if h >= 2:
                        weigh(i, h - 2)
                rows(i + 1)
                turn_o(i)
                output(i)
                turn_qk(i + 1)

        @block.scalar
        def _(act):
            for sem, per in ((s.nT_ready, 1), (s.qkT_ready, 1), (s.z_read, 1), (s.z_parts, 1), (s.decay_ready, 1),
                             (s.exp_done, H), (s.hT_ready, 1), (s.onT_ready, 1), (s.qk_sq_ready, 1), (s.qp_ready, 1)):
                credit(act, sem, per)
            chain = Chain(act, s.act_step)

            def project(n):
                chain.start(n)
                act.wait_ge(s.norm_used, n + 1)
                act.activation(s.nT[:], misc[:, 0:T], ACT.Copy).then_inc(s.nT_ready, 1)
                act.wait_ge(s.qkz_ready, of(n))
                act.activation(s.kT[:], proj[:, T:2 * T], ACT.Identity, bias=w["mix_bk"][:])
                act.activation(s.qT[:], proj[:, 0:T], ACT.Identity, bias=w["mix_bq"][:]).then_inc(s.qkT_ready, 1)
                act.activation(s.z_relu[:], score_bank[2][:, 0:T], ACT.Relu, bias=w["mix_bg"][:])
                act.activation(s.z_exp[:], score_bank[2][:, 0:T], ACT.Abs, bias=w["mix_bg"][:]).then_inc(s.z_read, 1)
                act.wait_ge(s.z_read, of(n))
                chain.link(act.activation(s.z_exp[:], s.z_exp[:], ACT.Exp, scale=-1.0))
                act.activation(s.z_exp[:], s.z_exp[:], ACT.Ln, bias=1.0).then_inc(s.z_parts, 1)
                act.wait_ge(s.softplus_ready, of(n))
                act.activation(s.decay[:], s.softplus[:], ACT.Exp, scale=-1.0).then_inc(s.decay_ready, 1)

            def h_copy(n):
                act.wait_ge(s.sum_ready, of(n))
                act.activation(s.hT[:], v_banks[1][:, 0:T], ACT.Copy).then_inc(s.hT_ready, 1)

            def square(n):
                act.wait_ge(s.qk_sb, of(n))
                act.activation(s.qk_sq[:], s.qk[:], ACT.Square).then_inc(s.qk_sq_ready, 1)

            def q_copy(n):
                act.wait_ge(s.q_turned, of(n))
                for b in range(2):
                    ins = act.activation(s.qp[:, 2 * b:2 * b + 2, :].rearrange("p g t -> p (g t)"), score_bank[b][:, :], ACT.Copy)
                ins.then_inc(s.qp_ready, 1)

            project(0)
            h_copy(0)
            square(0)
            q_copy(0)
            with act.Fori(0, B) as i:
                project(i + 1)
                for h in range(H):
                    act.wait_ge(s.scores_ready, of(i, h + 1, H))
                    act.wait_ge(s.pv_done, of(i, h - 2, H))
                    act.activation(s.probs[:, h % 3, :], score_bank[h % 3][:, :], ACT.Exp,
                                   bias=k.exp_shift[:, h:h + 1]).then_inc(s.exp_done, 1)
                h_copy(i + 1)
                act.wait_ge(s.on_turned, of(i))
                act.activation(s.onT[:], misc[:, T:2 * T], ACT.Copy).then_inc(s.onT_ready, 1)
                square(i + 1)
                q_copy(i + 1)

        @block.gpsimd
        def _(pool):
            forget(pool, k, "ffn")
            for sem, per in ((s.softplus_ready, 1), (s.prod_ready, 2), (s.rs_ready, 1)):
                credit(pool, sem, per)

            def front(n):
                pool.wait_ge(s.z_parts, of(n))
                pool.tensor_tensor(s.softplus[:], s.z_relu[:], s.z_exp[:], ALU.add).then_inc(s.softplus_ready, 1)
                query_states(pool, s, n)

            def norms(n):
                pool.wait_ge(s.ss_ready, of(n))
                pool.tensor_tensor(s.rs[:], s.ss[:], s.minus_half[:, 0:TILES * 2 * H], ALU.pow).then_inc(s.pool_step, 1)
                pool.wait_ge(s.pool_step, n + 1)
                pool.tensor_tensor(s.rs[:], s.rs[:], k.l2_scale[:].rearrange("p t h -> p (t h)"), ALU.mult).then_inc(s.rs_ready, 1)

            ln_power(pool, s, TILES, 0)
            front(0)
            ln_power(pool, s, TILES, 1)
            norms(0)
            with pool.Fori(0, B) as i:
                front(i + 1)
                ln_power(pool, s, TILES, i + 2)
                norms(i + 1)

        @block.vector
        def _(dve):
            for sem, per in ((s.kv_done, D), (s.scan_done, D), (s.qk_sb, 1), (s.vaug_ready, 1), (s.ss_ready, 1),
                             (s.qk_pad_ready, 1), (s.kp_ready, 1), (s.on_ready, 1), (s.x_done, 1)):
                credit(dve, sem, per)
            chain = Chain(dve, s.dve_step)

            def norm_rows(n):
                ln_stats(dve, chain, s, x_tile(k, n), TILES)
                ln_apply(dve, s, x_tile(k, n), TILES, n)

            def qk_rows(n):
                dve.wait_ge(s.qk_rows, of(n))
                dve.tensor_tensor(s.qk[:].rearrange("p t h e -> p (t h e)"), proj[:, :],
                                  k.bqk_rows[:].rearrange("p t c -> p (t c)"), ALU.add).then_inc(s.qk_sb, 1)
                dve.wait_ge(s.v_rows, of(n))
                dve.tensor_tensor(k.vaug[:, :, :, 0:D].rearrange("p t h e -> p (t h) e"),
                                  v_banks[0][:, 0:TILES * C].rearrange("p (g e) -> p g e", e=D),
                                  k.bv_rows[:].rearrange("p t (h e) -> p (t h) e", e=D), ALU.add).then_inc(s.vaug_ready, 1)
                dve.wait_ge(s.qk_sq_ready, of(n))
                chain.link(dve.tensor_reduce(s.ss[:], s.qk_sq[:].rearrange("p t h e -> p (t h) e"), AX_X, ALU.add))
                dve.tensor_scalar(s.ss[:], s.ss[:], L2_FLOOR, None, ALU.max).then_inc(s.ss_ready, 1)
                dve.wait_ge(s.rs_ready, of(n))
                dve.tensor_tensor(k.qk_pad[:, :, :, 0:D].rearrange("p t h e -> p (t h) e"),
                                  s.qk[:].rearrange("p t h e -> p (t h) e"),
                                  s.rs[:].unsqueeze(2).broadcast_to([P, TILES * 2 * H, D]), ALU.mult).then_inc(s.qk_pad_ready, 1)

            def k_copy(n):
                dve.wait_ge(s.k_turned, of(n))
                for b in range(2):
                    ins = dve.tensor_copy(s.kp[:, 2 * b:2 * b + 2, :].rearrange("p g t -> p (g t)"), v_banks[b][:, :])
                ins.then_inc(s.kp_ready, 1)

            def weighted(i):
                dve.wait_ge(s.pv_done, of(i, H, H))
                chain.link(dve.reciprocal(s.rden[:], o_view[:, :, :, D:D + 1]))
                dve.tensor_tensor(s.on[:].rearrange("p t (h e) -> p (t h) e", e=D),
                                  o_view[:, :, :, 0:D].rearrange("p t h e -> p (t h) e"),
                                  s.rden[:].rearrange("p t h e -> p (t h) e").broadcast_to([P, TILES * H, D]),
                                  ALU.mult).then_inc(s.on_ready, 1)

            norm_rows(0)
            outer_and_scan(dve, s, v_banks, w["mix_bv"], 0)
            norm_rows(1)
            qk_rows(0)
            k_copy(0)
            first = chain.n
            with dve.Fori(0, B) as i:
                chain.start(4 * i + first)
                outer_and_scan(dve, s, v_banks, w["mix_bv"], i + 1)
                norm_rows(i + 2)
                weighted(i)
                qk_rows(i + 1)
                dve.wait_ge(s.out_ready, of(i))
                dve.tensor_tensor(x_seq(k, i), x_seq(k, i), o_bank[:, 0:TILES * C], ALU.add).then_inc(s.x_done, 1)
                k_copy(i + 1)
                assert chain.n == 4



def phase_moe(nc, k, name, kind="moe"):
    w = k.w
    CAUSAL = BLOCKS * P
    SEL = TILES * NE
    SPREADS = PAIRS * NE // 2
    with Ctx(nc, k, name, kind) as c, nc.Block() as block:
        s = Stage()
        s.minus_half = k.minus_half
        ln_buffers(s, c, TILES)
        s.nT = c.sb("nT", [P, T])
        s.qT = c.sb("qT", [P, PAIRS, T])
        s.kT = c.sb("kT", [P, PAIRS, T])
        s.gates = c.sb("gates", [P, TILES * EH, NE])
        s.ranked = c.sb("ranked", [P, TILES * EH, NE])
        s.best = c.sb("best", [P, TILES * EH])
        s.top_gate = c.sb("top_gate", [P, TILES * EH])
        s.onehot = c.sb("onehot", [P, TILES, EH, NE])
        s.block_max = c.sb("block_max", [P, EH, BLOCKS])
        s.max1 = c.sb("max1", [P, EH])
        s.shift = c.sb("shift", [P, TILES, EH])
        s.part_bf = c.sb("part_bf", [P, TILES, EH], BF16)
        s.parts = c.sb("parts", [P, TILES, PARTS * EH])
        s.partsT = c.sb("partsT", [PARTS * EH, T], BF16)
        s.onehotT = c.sb("onehotT", [EH * NE, T], BF16)
        s.probs = c.sb("probs", [P, EH, CAUSAL])
        s.coef = c.sb("coef", [P, TILES * EH])
        s.o = c.sb("o", [P, TILES * EH, EK])
        s.oT = c.sb("oT", [P, PAIRS, T])
        s.picked = c.sb("picked", [P, 3, 2, T])
        s.taken = c.sb("taken", [P, SEL])
        s.nT_ready, s.q_psum, s.q_ready, s.k_psum, s.k_ready = c.sems(
            "nT_ready", "q_psum", "q_ready", "k_psum", "k_ready")
        s.logits_psum, s.gate_exp_ready, s.onehot_ready, s.rows_ready, s.max_done = c.sems(
            "logits_psum", "gate_exp_ready", "onehot_ready", "rows_ready", "max_done")
        s.parts_ready, s.small_turned, s.small_ready, s.experts_ready, s.selected = c.sems(
            "parts_ready", "small_turned", "small_ready", "experts_ready", "selected")
        s.gated, s.scores_ready, s.exp_done, s.o_psum, s.o_ready = c.sems(
            "gated", "scores_ready", "exp_done", "o_psum", "o_ready")
        s.o_turned, s.oT_ready, s.spread_ready, s.picked_ready, s.picked_used = c.sems(
            "o_turned", "oT_ready", "spread_ready", "picked_ready", "picked_used")
        s.x_done, s.dve_step = c.sems(
            "x_done", "dve_step")
        two, experts, misc, o_banks = k.bank[0:2], k.bank[2:4], k.bank[4], k.bank[5:8]
        acc = [o_banks[t][:, 0:C] for t in range(TILES)]
        results = TILES * EH

        def o_of(r, last):
            return o_banks[r // OBANK][:, (r % OBANK) * (EK + 1):(r % OBANK) * (EK + 1) + last]

        def o_group(b):
            first, count = b * OBANK, min(OBANK, results - b * OBANK)
            return first, count, o_banks[b][:, 0:count * (EK + 1)].rearrange("p (r e) -> p r e", e=EK + 1)

        @block.tensor
        def _(pe):
            for sem, per in ((s.q_psum, 2), (s.k_psum, 2), (s.logits_psum, 1), (s.rows_ready, EH), (s.small_turned, 1),
                             (s.experts_ready, SEL), (s.scores_ready, EH), (s.o_psum, 1), (s.o_turned, 1),
                             (s.spread_ready, SPREADS), (s.picked_used, SPREADS)):
                credit(pe, sem, per)

            def turn_norm(n):
                pe.wait_ge(s.norm_ready, n + 1)
                for t in range(TILES):
                    ins = pe.transpose(misc[:, t * P:(t + 1) * P], s.norm[:, t, :], w["ident"][:])
                ins.then_inc(s.norm_used, 1)

            def project(n, weight, ready):
                for b in range(2):
                    for p in (2 * b, 2 * b + 1):
                        ins = pe.matmul(experts[b][:, (p % 2) * T:(p % 2 + 1) * T], weight[:, p * P:(p + 1) * P], s.nT[:],
                                        start=True, stop=True)
                    ins.then_inc(ready, 1)

            def project_q(n):
                pe.wait_ge(s.nT_ready, of(n))
                pe.wait_ge(s.selected, before(n, SEL, SEL))
                project(n, w["moe_q"], s.q_psum)

            def project_k(n):
                pe.wait_ge(s.q_ready, of(n, 2, 2))
                project(n, w["moe_k"], s.k_psum)

            def logits(n):
                for t in range(TILES):
                    ins = pe.matmul(misc[:, T + t * EH * NE:T + (t + 1) * EH * NE], s.nT[:, t * P:(t + 1) * P], w["moe_gate"][:],
                                    start=True, stop=True)
                ins.then_inc(s.logits_psum, 1)

            def head(tensor, h, at, size):
                return tensor[EK * (h % 2):EK * (h % 2 + 1), h // 2, at:at + size]

            def score_rows(i, h):
                if h == 0:
                    pe.wait_ge(s.q_ready, of(i, 2, 2))
                    pe.wait_ge(s.k_ready, of(i, 2, 2))
                if h >= 2:
                    pe.wait_ge(s.max_done, of(i, h - 1, EH))
                b = two[h % 2]
                pe.matmul(b[:, 0:P], head(s.qT, h, 0, P), head(s.kT, h, 0, P), start=True, stop=False)
                pe.matmul(b[:, 0:P], w["ident_bf"][:], w["mask_rows"][:], start=False, stop=True)
                pe.matmul(b[:, P:CAUSAL], head(s.qT, h, P, P), head(s.kT, h, 0, T), start=True, stop=False, skip_group_check=True)
                pe.matmul(b[:, 2 * P:CAUSAL], w["ident_bf"][:], w["mask_rows"][:], start=False, stop=True,
                          skip_group_check=True).then_inc(s.rows_ready, 1)

            def scores(i, h):
                if h == 0:
                    pe.wait_ge(s.small_ready, of(i))
                if h >= 2:
                    pe.wait_ge(s.exp_done, of(i, h - 1, EH))
                b = two[h % 2]
                for at, key, query, size in ((0, 0, 0, T), (T, P, P, P)):
                    pe.matmul(b[:, at:at + size], head(s.kT, h, key, P), head(s.qT, h, query, size), start=True, stop=False,
                              skip_group_check=True)
                    pe.matmul(b[:, at:at + size], w["shift_sel"][:, h, :], s.partsT[:, query:query + size], start=False, stop=False,
                              skip_group_check=True)
                    ins = pe.matmul(b[:, at:at + P], w["ident_bf"][:], w["mask_T"][:], start=False, stop=True,
                                    skip_group_check=True)
                ins.then_inc(s.scores_ready, 1)

            def expert_values(i, t):
                for e in range(NE):
                    j = t * NE + e
                    if j >= 2:
                        pe.wait_ge(s.selected, of(i, j - 1, SEL))
                    pe.matmul(experts[j % 2][:, :], s.nT[:, t * P:(t + 1) * P], w["moe_v"][:, e, :], start=True, stop=True) \
                      .then_inc(s.experts_ready, 1)

            def turn_small(i):
                pe.wait_ge(s.parts_ready, of(i))
                for t in range(TILES):
                    pe.transpose(misc[0:PARTS * EH, t * P:(t + 1) * P], s.parts[:, t, :], w["ident"][:])
                for t in range(TILES):
                    ins = pe.transpose(misc[0:EH * NE, T + t * P:T + (t + 1) * P],
                                       s.onehot[:, t, :, :].rearrange("p h e -> p (h e)"), w["ident"][:])
                ins.then_inc(s.small_turned, 1)

            def weigh(i):
                pe.wait_ge(s.gated, of(i, 2, 2))
                pe.wait_ge(s.exp_done, of(i, EH, EH))
                pe.wait_ge(s.x_done, before(i))
                for h in range(EH):
                    value = [k.values[:, t, h, :] for t in range(TILES)]
                    pe.matmul(o_of(h, EK + 1), s.probs[:, h, 0:P], value[0], start=True, stop=True)
                    pe.matmul(o_of(EH + h, EK + 1), s.probs[:, h, P:2 * P], value[0], start=True, stop=False)
                    ins = pe.matmul(o_of(EH + h, EK + 1), s.probs[:, h, 2 * P:3 * P], value[1], start=False, stop=True)
                ins.then_inc(s.o_psum, 1)

            def turn_o(i):
                pe.wait_ge(s.o_ready, of(i))
                pe.wait_ge(s.k_ready, of(i + 1, 2, 2))
                for p in range(PAIRS):
                    for t in range(TILES):
                        at = (p % 2) * T + t * P
                        r = t * EH + 2 * p
                        ins = pe.transpose(experts[p // 2][:, at:at + P], s.o[:, r:r + 2, :].rearrange("p r e -> p (r e)"),
                                           w["ident"][:])
                ins.then_inc(s.o_turned, 1)

            def spread(i, g):
                if g >= 2:
                    pe.wait_ge(s.picked_ready, of(i, g - 1, SPREADS))
                p, e = g // (NE // 2), 2 * (g % (NE // 2))
                for j in range(2):
                    ins = pe.matmul(two[g % 2][:, j * T:(j + 1) * T], w["spread"][:, p, e + j, :], s.onehotT[:], start=True, stop=True)
                ins.then_inc(s.spread_ready, 1)

            def expert_outputs(i, g):
                pe.wait_ge(s.picked_ready, of(i, g + 1, SPREADS))
                p, e = g // (NE // 2), 2 * (g % (NE // 2))
                for j in range(2):
                    for t in range(TILES):
                        ins = pe.matmul(acc[t], s.picked[:, g % 3, j, t * P:(t + 1) * P], w["moe_o"][:, p, e + j, :],
                                        start=(g == 0 and j == 0), stop=(g == SPREADS - 1 and j == 1))
                ins.then_inc(s.picked_used, 1)

            turn_norm(0)
            project_q(0)
            project_k(0)
            logits(0)
            with pe.Fori(0, B) as i:
                for h in range(EH):
                    score_rows(i, h)
                pe.wait_ge(s.onehot_ready, of(i))
                expert_values(i, 0)
                turn_small(i)
                for h in range(EH):
                    scores(i, h)
                expert_values(i, 1)
                turn_norm(i + 1)
                project_q(i + 1)
                weigh(i)
                project_k(i + 1)
                logits(i + 1)
                turn_o(i)
                for g in range(SPREADS + 1):
                    if g < SPREADS:
                        spread(i, g)
                    if g >= 1:
                        expert_outputs(i, g - 1)

        @block.scalar
        def _(act):
            for sem, per in ((s.nT_ready, 1), (s.q_ready, 2), (s.k_ready, 2), (s.gate_exp_ready, 1), (s.small_ready, 1),
                             (s.exp_done, EH), (s.oT_ready, 1)):
                credit(act, sem, per)

            def norm_copy(n):
                act.wait_ge(s.norm_used, n + 1)
                act.activation(s.nT[:], misc[:, 0:T], ACT.Copy).then_inc(s.nT_ready, 1)

            def projected(n, psum, dst, ready, scale):
                for b in range(2):
                    act.wait_ge(psum, of(n, b + 1, 2))
                    act.activation(dst[:, 2 * b:2 * b + 2, :].rearrange("p g t -> p (g t)"), experts[b][:, :], ACT.Copy,
                                   scale=scale).then_inc(ready, 1)

            def front(n):
                norm_copy(n)
                projected(n, s.q_psum, s.qT, s.q_ready, EK ** -0.5)
                projected(n, s.k_psum, s.kT, s.k_ready, 1.0)
                act.wait_ge(s.logits_psum, of(n))
                act.activation(s.gates[:].rearrange("p r e -> p (r e)"), misc[:, T:T + TILES * EH * NE], ACT.Exp,
                               scale=-1.0).then_inc(s.gate_exp_ready, 1)

            front(0)
            with act.Fori(0, B) as i:
                act.wait_ge(s.small_turned, of(i))
                act.activation(s.partsT[:], misc[0:PARTS * EH, 0:T], ACT.Copy)
                act.activation(s.onehotT[:], misc[0:EH * NE, T:2 * T], ACT.Copy).then_inc(s.small_ready, 1)
                for h in range(EH):
                    act.wait_ge(s.scores_ready, of(i, h + 1, EH))
                    act.activation(s.probs[:, h, :], two[h % 2][:, 0:CAUSAL], ACT.Exp).then_inc(s.exp_done, 1)
                front(i + 1)
                act.wait_ge(s.o_turned, of(i))
                for b in range(2):
                    ins = act.activation(s.oT[:, 2 * b:2 * b + 2, :].rearrange("p g t -> p (g t)"), experts[b][:, :], ACT.Copy)
                ins.then_inc(s.oT_ready, 1)

        @block.gpsimd
        def _(pool):
            credit(pool, s.gated, TILES)
            ln_power(pool, s, TILES, 0)
            with pool.Fori(0, B) as i:
                ln_power(pool, s, TILES, i + 1)
                for t in range(TILES):
                    pool.wait_ge(s.selected, of(i, NE * (t + 1), SEL))
                    pool.tensor_tensor(k.values[:, t, :, 0:EK], k.values[:, t, :, 0:EK],
                                       s.top_gate[:, t * EH:(t + 1) * EH].unsqueeze(2).broadcast_to([P, EH, EK]),
                                       ALU.mult).then_inc(s.gated, 1)

        @block.vector
        def _(dve):
            for sem, per in ((s.max_done, EH), (s.parts_ready, 1), (s.selected, SEL), (s.o_ready, 1), (s.picked_ready, SPREADS),
                             (s.x_done, 1), (s.onehot_ready, 1)):
                credit(dve, sem, per)
            chain = Chain(dve, s.dve_step)

            def norm_rows(n):
                ln_stats(dve, chain, s, x_tile(k, n), TILES)
                ln_apply(dve, s, x_tile(k, n), TILES, n)

            def route(n):
                wide = [P, TILES * EH, NE]
                dve.wait_ge(s.gate_exp_ready, of(n))
                chain.link(dve.tensor_scalar(s.gates[:], s.gates[:], 1.0, None, ALU.add))
                chain.link(dve.reciprocal(s.gates[:], s.gates[:]))
                chain.link(dve.tensor_reduce(s.top_gate[:], s.gates[:], AX_X, ALU.max))
                chain.link(dve.tensor_tensor(s.ranked[:], s.gates[:], s.top_gate[:].unsqueeze(2).broadcast_to(wide), ALU.is_equal))
                chain.link(dve.tensor_tensor(s.ranked[:], s.ranked[:], w["rank"][:], ALU.mult))
                chain.link(dve.tensor_reduce(s.best[:], s.ranked[:], AX_X, ALU.max))
                dve.tensor_tensor(s.onehot[:].rearrange("p t h e -> p (t h) e"), w["rank"][:],
                                  s.best[:].unsqueeze(2).broadcast_to(wide), ALU.is_equal).then_inc(s.onehot_ready, 1)

            def select(i, t):
                for e in range(NE):
                    dve.wait_ge(s.experts_ready, of(i, t * NE + e + 1, SEL))
                    if e > 0:
                        dve.wait_ge(s.selected, of(i, t * NE + e, SEL))
                    dve.memset(s.taken[:, t * NE + e:t * NE + e + 1], 0.0)
                    dve.copy_predicated(k.values[:, t, :, 0:EK],
                                        s.onehot[:, t, :, e:e + 1].bitcast(U32).broadcast_to([P, EH, EK]),
                                        experts[e % 2][:, :].rearrange("p (h e) -> p h e", e=EK)).then_inc(s.selected, 1)

            norm_rows(0)
            route(0)
            first = chain.n
            with dve.Fori(0, B) as i:
                chain.start(16 * i + first)
                for h in range(EH):
                    dve.wait_ge(s.rows_ready, of(i, h + 1, EH))
                    dve.tensor_reduce(s.block_max[:, h, :], two[h % 2][:, 0:CAUSAL].rearrange("p (b k) -> p b k", k=P), AX_X,
                                      ALU.max).then_inc(s.max_done, 1)
                dve.wait_ge(s.max_done, of(i, EH, EH))
                dve.tensor_scalar(s.shift[:, 0, :], s.block_max[:, :, 0], -1.0, None, ALU.mult)
                chain.link(dve.tensor_tensor(s.max1[:], s.block_max[:, :, 1], s.block_max[:, :, 2], ALU.max))
                chain.link(dve.tensor_scalar(s.shift[:, 1, :], s.max1[:], -1.0, None, ALU.mult))
                for part in range(PARTS - 1):
                    chain.link(dve.tensor_copy(s.part_bf[:], s.shift[:]))
                    dve.tensor_copy(s.parts[:, :, part * EH:(part + 1) * EH], s.part_bf[:])
                    chain.link(dve.tensor_tensor(s.shift[:], s.shift[:], s.part_bf[:], ALU.subtract))
                dve.tensor_copy(s.parts[:, :, (PARTS - 1) * EH:PARTS * EH], s.shift[:]).then_inc(s.parts_ready, 1)
                dve.wait_ge(s.onehot_ready, of(i))
                select(i, 0)
                norm_rows(i + 1)
                select(i, 1)
                dve.wait_ge(s.o_psum, of(i))
                for b in range(len(o_banks)):
                    first_r, count, view = o_group(b)
                    ins = dve.reciprocal(s.coef[:, first_r:first_r + count].unsqueeze(2), view[:, :, EK:EK + 1])
                chain.link(ins)
                chain.link(dve.tensor_tensor(s.coef[:], s.coef[:], s.top_gate[:], ALU.mult))
                for b in range(len(o_banks)):
                    first_r, count, view = o_group(b)
                    ins = dve.tensor_tensor(s.o[:, first_r:first_r + count, :], view[:, :, 0:EK],
                                            s.coef[:, first_r:first_r + count].unsqueeze(2).broadcast_to([P, count, EK]), ALU.mult)
                ins.then_inc(s.o_ready, 1)
                dve.wait_ge(s.oT_ready, of(i))
                for g in range(SPREADS):
                    dve.wait_ge(s.spread_ready, of(i, g + 1, SPREADS))
                    dve.wait_ge(s.picked_used, of(i, g - 2, SPREADS))
                    dve.tensor_tensor(s.picked[:, g % 3], two[g % 2][:, :].rearrange("p (j t) -> p j t", t=T),
                                      s.oT[:, g // (NE // 2), :].unsqueeze(1).broadcast_to([P, 2, T]), ALU.mult).then_inc(s.picked_ready, 1)
                route(i + 1)
                dve.wait_ge(s.picked_used, of(i, SPREADS, SPREADS))
                for t in range(TILES):
                    ins = dve.scalar_tensor_tensor(x_tile(k, i)(t), acc[t], 0.5, x_tile(k, i)(t), ALU.mult, ALU.add)
                ins.then_inc(s.x_done, 1)
                assert chain.n == 16, chain.n



def phase_gla(nc, k, name, kind="gla"):
    w = k.w
    with Ctx(nc, k, name, kind) as c, nc.Block() as block:
        s = Stage()
        s.minus_half = k.minus_half
        ln_buffers(s, c, TILES)
        recurrence_buffers(s, c)
        s.low = c.sb("low", [GLA_RANK, T])
        s.gate_exp = c.sb("gate_exp", [P, TILES * C])
        s.gate = c.sb("gate", [P, TILES * C])
        s.o_sq = c.sb("o_sq", [P, TILES, D, H])
        s.ms = c.sb("ms", [P, TILES * H])
        s.rs = c.sb("rs", [P, TILES * H])
        s.on = c.sb("on", [P, TILES, C])
        s.gated = c.sb("gated", [P, TILES, C])
        s.onT = c.sb("onT", [P, T])
        s.low_psum, s.low_ready, s.gate_psum, s.gate_exp_ready, s.gate_ready = c.sems(
            "low_psum", "low_ready", "gate_psum", "gate_exp_ready", "gate_ready")
        s.o_sq_ready, s.ms_ready, s.rs_ready, s.on_ready, s.gated_ready = c.sems(
            "o_sq_ready", "ms_ready", "rs_ready", "on_ready", "gated_ready")
        s.on_turned, s.onT_ready, s.out_ready, s.x_done = c.sems(
            "on_turned", "onT_ready", "out_ready", "x_done")
        o_bank, out_bank, gate_bank, z_bank, misc, proj, v_banks = *k.bank[0:6], k.bank[6:8]
        o_heads = o_bank[:, 0:TILES * C].rearrange("p (t e h) -> p t h e", t=TILES, e=D)

        @block.tensor
        def _(pe):
            for sem, per in ((s.v_ready, D // 2), (s.sum_ready, 1), (s.qkz_ready, 1), (s.low_psum, 1),
                             (s.gate_psum, 1), (s.on_turned, 1), (s.out_ready, 1)):
                credit(pe, sem, per)

            def project(n):
                pe.wait_ge(s.norm_ready, n + 1)
                pe.wait_ge(s.nT_ready, before(n))
                for t in range(TILES):
                    ins = pe.transpose(misc[:, t * P:(t + 1) * P], s.norm[:, t, :], w["ident"][:])
                ins.then_inc(s.norm_used, 1)
                pe.wait_ge(s.nT_ready, of(n))
                pe.wait_ge(s.qkT_ready, before(n))
                pe.wait_ge(s.z_read, before(n))
                pe.matmul(z_bank[0:GLA_RANK, 0:T], w["gla_g1"][:], s.nT[:], start=True, stop=True).then_inc(s.low_psum, 1)
                pe.matmul(proj[:, 0:T], w["gla_q"][:], s.nT[:], start=True, stop=True)
                pe.matmul(proj[:, T:2 * T], w["gla_k"][:], s.nT[:], start=True, stop=True)
                pe.wait_ge(s.low_ready, of(n))
                pe.matmul(z_bank[:, T:2 * T], w["gla_g2"][:], s.low[:], start=True, stop=True).then_inc(s.qkz_ready, 1)
                spread_values(pe, s, v_banks, w["gla_v"], n,
                              lambda chunk: pe.wait_ge(s.kv_done, before(n, D // 2 + 2 * (chunk + 1), D)))
                pe.wait_ge(s.gate_ready, before(n))
                for t in range(TILES):
                    ins = pe.matmul(gate_bank[:, t * C:(t + 1) * C], s.nT[:, t * P:(t + 1) * P], w["gla_gate"][:], start=True, stop=True)
                ins.then_inc(s.gate_psum, 1)

            def sum_states(n):
                pe.wait_ge(s.prod_ready, of(n, 2, 2))
                pe.wait_ge(s.on_ready, before(n))
                for t in range(TILES):
                    for e in range(D):
                        at = t * C + e * H
                        ins = pe.matmul(o_bank[:, at:at + H], s.prod[:, e, t * P:(t + 1) * P], w["sum_dh"][:], start=True, stop=True)
                ins.then_inc(s.sum_ready, 1)

            def output(i):
                pe.wait_ge(s.gated_ready, of(i))
                for t in range(TILES):
                    ins = pe.transpose(misc[:, T + t * P:T + (t + 1) * P], s.gated[:, t, :], w["ident"][:])
                ins.then_inc(s.on_turned, 1)
                pe.wait_ge(s.onT_ready, of(i))
                pe.wait_ge(s.x_done, before(i))
                for t in range(TILES):
                    ins = pe.matmul(out_bank[:, t * C:(t + 1) * C], s.onT[:, t * P:(t + 1) * P], w["gla_o"][:], start=True, stop=True)
                ins.then_inc(s.out_ready, 1)

            project(0)
            sum_states(0)
            with pe.Fori(0, B) as i:
                project(i + 1)
                output(i)
                sum_states(i + 1)

        @block.scalar
        def _(act):
            for sem, per in ((s.nT_ready, 1), (s.qkT_ready, 1), (s.z_read, 1), (s.z_parts, 1), (s.decay_ready, 1),
                             (s.low_ready, 1), (s.gate_exp_ready, 1), (s.o_sq_ready, 1), (s.onT_ready, 1)):
                credit(act, sem, per)
            chain = Chain(act, s.act_step)

            def project(n):
                chain.start(n)
                act.wait_ge(s.norm_used, n + 1)
                act.activation(s.nT[:], misc[:, 0:T], ACT.Copy).then_inc(s.nT_ready, 1)
                act.wait_ge(s.low_psum, of(n))
                act.activation(s.low[:], z_bank[0:GLA_RANK, 0:T], ACT.Copy).then_inc(s.low_ready, 1)
                act.wait_ge(s.qkz_ready, of(n))
                act.activation(s.kT[:], proj[:, T:2 * T], ACT.Copy)
                act.activation(s.qT[:], proj[:, 0:T], ACT.Copy).then_inc(s.qkT_ready, 1)
                act.activation(s.z_relu[:], z_bank[:, T:2 * T], ACT.Relu, bias=k.minus_bg[:], scale=-1.0)
                act.activation(s.z_exp[:], z_bank[:, T:2 * T], ACT.Abs, bias=w["gla_bg"][:]).then_inc(s.z_read, 1)
                act.wait_ge(s.z_read, of(n))
                chain.link(act.activation(s.z_exp[:], s.z_exp[:], ACT.Exp, scale=-1.0))
                act.activation(s.z_exp[:], s.z_exp[:], ACT.Ln, bias=1.0).then_inc(s.z_parts, 1)
                act.wait_ge(s.softplus_ready, of(n))
                act.activation(s.decay[:], s.softplus[:], ACT.Exp, scale=-1.0 / GLA_NORM).then_inc(s.decay_ready, 1)
                act.wait_ge(s.gate_psum, of(n))
                act.activation(s.gate_exp[:], gate_bank[:, 0:TILES * C], ACT.Exp, scale=-1.0).then_inc(s.gate_exp_ready, 1)

            def square(n):
                act.wait_ge(s.sum_ready, of(n))
                act.activation(s.o_sq[:].rearrange("p t e h -> p (t e h)"), o_bank[:, 0:TILES * C], ACT.Square).then_inc(s.o_sq_ready, 1)

            project(0)
            square(0)
            with act.Fori(0, B) as i:
                project(i + 1)
                act.wait_ge(s.on_turned, of(i))
                act.activation(s.onT[:], misc[:, T:2 * T], ACT.Copy).then_inc(s.onT_ready, 1)
                square(i + 1)

        @block.gpsimd
        def _(pool):
            forget(pool, k, "moe")
            for sem, per in ((s.softplus_ready, 1), (s.prod_ready, 2), (s.rs_ready, 1), (s.gated_ready, 1)):
                credit(pool, sem, per)

            def softplus(n):
                pool.wait_ge(s.z_parts, of(n))
                pool.tensor_tensor(s.softplus[:], s.z_relu[:], s.z_exp[:], ALU.add).then_inc(s.softplus_ready, 1)

            ln_power(pool, s, TILES, 0)
            softplus(0)
            query_states(pool, s, 0)
            ln_power(pool, s, TILES, 1)
            with pool.Fori(0, B) as i:
                pool.wait_ge(s.ms_ready, of(i))
                pool.tensor_tensor(s.rs[:], s.ms[:], s.minus_half[:, 0:TILES * H], ALU.pow).then_inc(s.rs_ready, 1)
                pool.wait_ge(s.on_ready, of(i))
                pool.tensor_tensor(s.gated[:].rearrange("p t c -> p (t c)"), s.on[:].rearrange("p t c -> p (t c)"), s.gate[:],
                                   ALU.mult).then_inc(s.gated_ready, 1)
                softplus(i + 1)
                query_states(pool, s, i + 1)
                ln_power(pool, s, TILES, i + 2)

        @block.vector
        def _(dve):
            for sem, per in ((s.kv_done, D), (s.scan_done, D), (s.gate_ready, 1), (s.ms_ready, 1), (s.on_ready, 1),
                             (s.x_done, 1)):
                credit(dve, sem, per)
            chain = Chain(dve, s.dve_step)

            def norm_rows(n):
                ln_stats(dve, chain, s, x_tile(k, n), TILES)
                ln_apply(dve, s, x_tile(k, n), TILES, n)

            norm_rows(0)
            outer_and_scan(dve, s, v_banks, None, 0)
            norm_rows(1)
            first = chain.n
            with dve.Fori(0, B) as i:
                chain.start(6 * i + first)
                dve.wait_ge(s.o_sq_ready, of(i))
                chain.link(dve.tensor_reduce(s.ms[:].rearrange("p (t h) -> p t h", h=H),
                                             s.o_sq[:].rearrange("p t e h -> p t h e"), AX_X, ALU.add))
                dve.tensor_scalar(s.ms[:], s.ms[:], 1.0 / D, RMS_EPS, ALU.mult, ALU.add).then_inc(s.ms_ready, 1)
                dve.wait_ge(s.gate_exp_ready, of(i))
                chain.link(dve.tensor_scalar(s.gate[:], s.gate_exp[:], 1.0, None, ALU.add))
                chain.link(dve.reciprocal(s.gate[:], s.gate[:]))
                chain.link(dve.tensor_tensor(s.gate[:], gate_bank[:, 0:TILES * C], s.gate[:], ALU.mult))
                dve.tensor_tensor(s.gate[:], s.gate[:], k.gnorm_rows[:].rearrange("p t c -> p (t c)"), ALU.mult).then_inc(s.gate_ready, 1)
                dve.wait_ge(s.rs_ready, of(i))
                for t in range(TILES):
                    ins = dve.tensor_tensor(s.on[:, t, :].rearrange("p (h e) -> p h e", e=D), o_heads[:, t],
                                            s.rs[:, t * H:(t + 1) * H].unsqueeze(2).broadcast_to([P, H, D]), ALU.mult)
                ins.then_inc(s.on_ready, 1)
                outer_and_scan(dve, s, v_banks, None, i + 1)
                norm_rows(i + 2)
                dve.wait_ge(s.out_ready, of(i))
                dve.tensor_tensor(x_seq(k, i), x_seq(k, i), out_bank[:, 0:TILES * C], ALU.add).then_inc(s.x_done, 1)
                assert chain.n == 6



def phase_store(nc, k, out):
    with Ctx(nc, k, "store") as c, nc.Block() as block:
        stored = c.sem("stored")

        @block.sync
        def _(sp):
            sp.dma_start(out.rearrange("b (t p) c -> p (b t) c", p=P), k.x[:, 0:B * TILES, :]).then_inc(stored, 16)
            sp.wait_ge(stored, 16)


def build(nc, dram, out):
    k = Stage()
    k.sems, k.stack = {}, ExitStack()
    with k.stack, Ctx(nc, k, "all") as c:
        k.bank = [c.stack.enter_context(nc.psum_tensor(f"bank{i}", [P, 512], F32)) for i in range(8)]
        k.x = c.sb("x", [P, B * TILES + FFN_TILES, C])
        k.w = {n: c.sb("w_" + n, list(a.shape), a.dtype) for n, a in dram.items() if n != "x"}
        k.minus_half = c.sb("minus_half", [P, 64])
        k.ones_row = c.sb("ones_row", [1, P])
        k.w_ffn = c.sb("w_ffn", [P, C])
        k.b_ffn = c.sb("b_ffn", [1, C])
        k.bqk_rows = c.sb("bqk_rows", [P, TILES, 2 * C])
        k.bv_rows = c.sb("bv_rows", [P, TILES, C])
        k.gnorm_rows = c.sb("gnorm_rows", [P, TILES, C])
        k.l2_scale = c.sb("l2_scale", [P, TILES, 2 * H])
        k.exp_shift = c.sb("exp_shift", [P, H])
        k.minus_bg = c.sb("minus_bg", [P, 1])
        k.vaug = c.sb("vaug", [P, TILES, H, D + 1])
        k.qk_pad = c.sb("qk_pad", [P, TILES, 2 * H, 32])
        k.values = c.sb("values", [P, TILES, EH, EK + 1])
        phase_load(nc, k, dram)
        phase_ffn(nc, k, "ffn_a")
        phase_mixer(nc, k, "mixer")
        phase_ffn(nc, k, "ffn_b")
        phase_moe(nc, k, "moe_a")
        phase_gla(nc, k, "gla")
        phase_moe(nc, k, "moe_b")
        phase_store(nc, k, out)


def layouts(a):
    def recur_v(w):
        return np.repeat(w.reshape(C, H, D).transpose(0, 2, 1), D, axis=2)

    w = {
        "ffn_WT": a["L0_ffn_W"].T, "ffn_b": a["L0_ffn_b"][None],
        "lora_downT": a["L0_ffn_lora_down"].T, "down_aux": a["L0_ffn_down_aux"],
        "lora_upT": a["L0_ffn_lora_up"].T, "up_auxT": a["L0_ffn_up_aux"].T,
        "mix_q": a["L0_attn_Wsq"].T, "mix_k": a["L0_attn_Wsk"].T,
        "mix_bq": a["L0_attn_bsq"][:, None], "mix_bk": a["L0_attn_bsk"][:, None],
        "mix_g": np.repeat(a["L0_attn_Wg"].T, D, axis=1), "mix_bg": np.repeat(a["L0_attn_bg"], D)[:, None],
        "mix_v": recur_v(a["L0_attn_Wsv"].T),
        "mix_bv": np.repeat(a["L0_attn_bsv"].reshape(H, D), D, axis=0),
        "qk": np.concatenate([a["L0_attn_Wq"].T, a["L0_attn_Wk"].T], axis=1),
        "bqk": np.concatenate([a["L0_attn_bq"], a["L0_attn_bk"]])[None],
        "v": a["L0_attn_Wv"].T, "bv": a["L0_attn_bv"][None],
        "o": a["L0_attn_Wo"].T, "bo": a["L0_attn_bo"][None],
        "temp": a["L0_attn_temp"].reshape(1, H),
        "gla_q": a["L1_attn_Wq"], "gla_k": a["L1_attn_Wk"], "gla_v": recur_v(a["L1_attn_Wv"]),
        "gla_g1": a["L1_attn_Wg1"], "gla_g2": a["L1_attn_Wg2"], "gla_bg": a["L1_attn_bg2"][:, None],
        "gla_gate": a["L1_attn_Wg"], "gnorm": np.tile(a["L1_attn_g_norm_w"], H)[None], "gla_o": a["L1_attn_Wo"],
        "moe_q": a["L1_ffn_w_q"], "moe_k": a["L1_ffn_w_k"], "moe_gate": a["L1_ffn_w_gate"],
        "moe_v": a["L1_ffn_value_experts"].transpose(2, 0, 1, 3).reshape(P, NE, EH * EK),
        "moe_o": a["L1_ffn_output_experts"].transpose(1, 2, 0, 3).reshape(PAIRS, P, NE, C).transpose(1, 0, 2, 3),
    }
    w = {n: np.ascontiguousarray(v) for n, v in w.items()}
    w["ident"] = np.eye(P, dtype=np.float32)
    ch = np.arange(P)
    same_head = ch[:, None] // D == ch[None, :] // D
    w["sum_d"] = np.stack([same_head & (ch[None, :] % D == e) for e in range(D)], 1).astype(np.float32)
    w["sum_dh"] = ((ch[:, None] // D == np.arange(H)[None]) * np.float32(D ** -0.5)).astype(np.float32)
    return w


def kernel(**inputs):
    import ml_dtypes
    import concourse.bacc as _bacc
    from concourse.bass_utils import run_bass_kernel_spmd as _run

    a = {n: np.asarray(v) for n, v in inputs.items()}
    w = layouts(a)
    bf = ml_dtypes.bfloat16
    w["ident_bf"] = np.eye(P, dtype=bf)
    i = np.arange(P)
    w["mask_rows"] = np.where(i[None, :] > i[:, None], MASKED, 0.0).astype(bf)
    w["mask_T"] = np.where(i[:, None] > i[None, :], MASKED, 0.0).astype(bf)
    part = np.arange(PARTS * EH)
    w["shift_sel"] = np.broadcast_to((part[:, None] % EH == np.arange(EH)[None])[:, :, None],
                                     (PARTS * EH, EH, P)).astype(bf)
    he = np.arange(EH * NE)
    pair, e, m = np.meshgrid(np.arange(PAIRS), np.arange(NE), np.arange(P), indexing="ij")
    w["spread"] = (he[:, None, None, None] == ((2 * pair + m // EK) * NE + e)[None]).astype(bf)
    w["rank"] = np.broadcast_to(NE - np.arange(NE, dtype=np.float32), (P, TILES * EH, NE))
    w = {n: np.ascontiguousarray(v) for n, v in w.items()}

    nc = _bacc.Bacc("TRN2", target_bir_lowering=False, num_devices=1)
    w["x"] = np.ascontiguousarray(a["L0_attn_x"])
    dram = {n: nc.dram_tensor("in_" + n, v.shape, mybir.dt.from_np(v.dtype), kind="ExternalInput").ap()
            for n, v in w.items()}
    out = nc.dram_tensor("out", (B, T, C), F32, kind="ExternalOutput").ap()
    build(nc, dram, out)
    r = _run(nc, [{"in_" + n: v for n, v in w.items()}], core_ids=[0])
    return r.results[0]["out"]
```

```python
from contextlib import ExitStack

import numpy as np

import concourse.bass as bass
from concourse import mybir

ALU = mybir.AluOpType
ACT = mybir.ActivationFunctionType
F32 = mybir.dt.float32
F32R = mybir.dt.float32r
BF16 = mybir.dt.bfloat16
U32 = mybir.dt.uint32
AX_X = mybir.AxisListType.X

P = 128
B, T, C = 16, 256, 128
TILES = T // P
LN_EPS = 1e-5

H, D = 16, 8
GLA_RANK = 16
GLA_NORM = 16.0
RMS_EPS = 1e-5
L2_FLOOR = 1e-24
ROOT_SCALE = 2.0 ** 18
LANES = P // 32
GROUPS = H // LANES
SPLIT = 4
EXP_SAFE = 80.0

EH, EK, NE = 8, 64, 8
PAIRS = EH // 2
BLOCKS = 3
MASKED = -1e30
PARTS = 3
OBANK = 6

FFN_TILES = 4

LOG_EXP_SET = "natural_log_exp_and_others"


def wait(eng, sem, value):
    if not (isinstance(value, int) and value <= 0):
        eng.wait_ge(sem, value)


class Chain:

    def __init__(self, eng, sem):
        self.eng, self.sem, self.base, self.n = eng, sem, 0, 0

    def link(self, ins, static=False):
        self.n += 1
        ins.then_inc(self.sem, 1)
        self.eng.wait_ge(self.sem, self.base + self.n)
        if static is not False:
            self.eng.memset(static[:], 0.0)

    def start(self, base):
        self.base, self.n = base, 0



def of(i, n=1, per=1):
    return (i + 1) * per + n


def before(i, n=1, per=1):
    return i * per + n


def credit(eng, sem, per=1):
    for _ in range(per):
        eng.nop().then_inc(sem, 1)



def ln_stats(dve, chain, s, x_tiles, tiles):
    for t in range(tiles):
        ins = dve.bn_stats(s.stats[:, t, :], x_tiles(t))
    chain.link(ins, static=s.scratch)
    for t in range(tiles):
        ins = dve.bn_aggr(s.mean_var[:, t, :], s.stats[:, t, :])
    chain.link(ins)
    dve.tensor_scalar(s.var_eps[:, 0:tiles], s.mean_var[:, 0:tiles, 1], LN_EPS, None,
                      ALU.add).then_inc(s.var_ready, 1)


def ln_apply(dve, s, x_tiles, tiles, n):
    wait(dve, s.rstd_ready, n + 1)
    wait(dve, s.norm_used, n)
    for t in range(tiles):
        ins = dve.tensor_scalar(s.norm[:, t, :], x_tiles(t), s.mean_var[:, t, 0:1], s.rstd[:, t:t + 1],
                                ALU.subtract, ALU.mult)
    ins.then_inc(s.norm_ready, 1)


def ln_power(pool, s, tiles, n):
    wait(pool, s.var_ready, n + 1)
    wait(pool, s.norm_ready, n)
    pool.tensor_tensor(s.rstd[:, 0:tiles], s.var_eps[:, 0:tiles], s.minus_half[:, 0:tiles],
                       ALU.pow).then_inc(s.rstd_ready, 1)


def root_guess(act, chain, s, z, n):
    act.wait_ge(s.z_ready, of(n))
    chain.link(act.activation(s.guess[:], z[:], ACT.Ln))
    act.activation(s.guess[:], s.guess[:], ACT.Exp, scale=-0.5).then_inc(s.guess_ready, 1)


def refine_root(dve, chain, s, z, n):
    dve.wait_ge(s.guess_ready, of(n))
    chain.link(dve.tensor_tensor(s.rs[:], s.guess[:], z[:], ALU.mult))
    chain.link(dve.scalar_tensor_tensor(s.rs[:], s.rs[:], -0.5, s.guess[:], ALU.mult, ALU.mult))
    return dve.scalar_tensor_tensor(s.rs[:], s.rs[:], 1.5, s.guess[:], ALU.add, ALU.mult)


def ln_buffers(s, c, tiles):
    s.stats = c.sb("stats", [P, tiles, 6])
    s.mean_var = c.sb("mean_var", [P, tiles, 2])
    s.var_eps = c.sb("var_eps", [P, tiles])
    s.rstd = c.sb("rstd", [P, tiles])
    s.norm = c.sb("norm", [P, tiles, C])
    s.scratch = c.sb("scratch", [P, 1])
    s.var_ready, s.rstd_ready, s.norm_ready, s.norm_used = c.sems(
        "var_ready", "rstd_ready", "norm_ready", "norm_used")


class Stage:
    pass


class Ctx:

    def __init__(self, nc, k, phase, kind=None):
        self.nc, self.k, self.phase, self.kind, self.stack = nc, k, phase, kind or phase, ExitStack()

    def __enter__(self):
        self.stack.__enter__()
        return self

    def __exit__(self, *a):
        return self.stack.__exit__(*a)

    def sb(self, name, shape, dt=F32):
        return self.stack.enter_context(self.nc.sbuf_tensor(f"{self.phase}_{name}", shape, dt))

    def sem(self, name):
        kept = self.k.sems.setdefault(self.kind, {})
        if name not in kept:
            kept[name] = self.k.stack.enter_context(self.nc.semaphore(f"{self.kind}_{name}"))
        return kept[name]

    def sems(self, *names):
        return [self.sem(name) for name in names]


def forget(pool, k, kind):
    for sem in k.sems[kind].values():
        pool.sem_clear(sem)



def phase_load(nc, k, dram):
    with Ctx(nc, k, "load") as c, nc.Block() as block:
        loaded = c.sem("loaded")
        made = c.sem("made")
        lora1 = c.sem("lora1")
        lora1_sb = c.sem("lora1_sb")
        lora2 = c.sem("lora2")
        lora2_sb = c.sem("lora2_sb")
        lora3 = c.sem("lora3")
        bias_rows = c.sem("bias_rows")
        temp_rows = c.sem("temp_rows")
        act_step = c.sem("act_step")
        dve_step = c.sem("dve_step")
        w = k.w
        a1 = c.sb("a1", [4, C])
        a2 = c.sb("a2", [50, C])
        t1 = c.sb("t1", [P, H])
        t2 = c.sb("t2", [P, H])
        t3 = c.sb("t3", [P, H])
        names = sorted(w)

        @block.sync
        def _(sp):
            sp.dma_start(k.x[:, 0:B * TILES, :], dram["x"].rearrange("b (t p) c -> p (b t) c", p=P)) \
              .then_inc(loaded, 16)
            for name in names:
                src = dram[name]
                sp.dma_start(w[name][:], src).then_inc(loaded, 16)
            sp.wait_ge(loaded, 16 * (len(names) + 1))

        @block.gpsimd
        def _(pool):
            pool.memset(k.minus_half[:], -0.5)
            pool.memset(k.x[:, B * TILES:, :], 0.0)
            pool.memset(k.vaug[:], 1.0)
            pool.memset(k.values[:], 1.0)
            pool.memset(k.ones_row[:], 1.0).then_inc(made, 1)

        @block.tensor
        def _(pe):
            pe.wait_ge(loaded, 16 * (len(names) + 1))
            pe.wait_ge(made, 1)
            pe.matmul(k.bank[0][0:4, 0:C], w["lora_downT"][:], w["down_aux"][:], start=True, stop=True).then_inc(lora1, 1)
            pe.matmul(k.bank[3][:, 0:2 * C], k.ones_row[:], w["bqk"][:], start=True, stop=True)
            pe.matmul(k.bank[4][:, 0:C], k.ones_row[:], w["bv"][:], start=True, stop=True)
            pe.matmul(k.bank[5][:, 0:C], k.ones_row[:], w["gnorm"][:], start=True, stop=True).then_inc(bias_rows, 1)
            pe.matmul(k.bank[6][:, 0:H], k.ones_row[:], w["temp"][:], start=True, stop=True).then_inc(temp_rows, 1)
            pe.wait_ge(lora1_sb, 1)
            pe.matmul(k.bank[1][0:50, 0:C], w["lora_upT"][:], a1[:], start=True, stop=True).then_inc(lora2, 1)
            pe.wait_ge(lora2_sb, 1)
            pe.matmul(k.bank[2][:, 0:C], a2[:], w["up_auxT"][:], start=True, stop=True).then_inc(lora3, 1)

        @block.vector
        def _(dve):
            chain = Chain(dve, dve_step)
            dve.wait_ge(lora1, 1)
            dve.tensor_copy(a1[:], k.bank[0][0:4, 0:C]).then_inc(lora1_sb, 1)
            dve.wait_ge(bias_rows, 1)
            for t in range(TILES):
                dve.tensor_copy(k.bqk_rows[:, t, :], k.bank[3][:, 0:2 * C])
                dve.tensor_copy(k.bv_rows[:, t, :], k.bank[4][:, 0:C])
                dve.tensor_copy(k.gnorm_rows[:, t, :], k.bank[5][:, 0:C])
            dve.wait_ge(lora2, 1)
            dve.tensor_copy(a2[:], k.bank[1][0:50, 0:C]).then_inc(lora2_sb, 1)
            dve.wait_ge(lora3, 1)
            chain.link(dve.tensor_tensor(k.w_ffn[:], k.bank[2][:, 0:C], w["ffn_WT"][:], ALU.add))
            dve.tensor_scalar(k.w_ffn[:], k.w_ffn[:], 0.5, None, ALU.mult)
            dve.tensor_scalar(k.b_ffn[:], w["ffn_b"][:], 0.5, None, ALU.mult)
            dve.tensor_scalar(k.minus_bg[:], w["gla_bg"][:], -1.0, None, ALU.mult)
            dve.wait_ge(act_step, 4)
            chain.link(dve.tensor_tensor(t3[:], t2[:], t1[:], ALU.add))
            dve.tensor_scalar(k.exp_shift[:], t3[:], EXP_SAFE, 0.0, ALU.subtract, ALU.max)
            for t in range(TILES):
                dve.memset(k.l2_scale[:, 1, t, :], ROOT_SCALE ** 0.5)
                ins = dve.tensor_scalar(k.l2_scale[:, 0, t, :], t3[:], ROOT_SCALE ** 0.5, None, ALU.mult)
            chain.link(ins)
            chain.link(dve.tensor_scalar(k.exp_shift[:], k.exp_shift[:], -1.0, None, ALU.mult))

        @block.scalar
        def _(act):
            act.wait_ge(temp_rows, 1)
            act.activation(t1[:], k.bank[6][:, 0:H], ACT.Relu).then_inc(act_step, 1)
            act.activation(t2[:], k.bank[6][:, 0:H], ACT.Abs).then_inc(act_step, 1)
            act.wait_ge(act_step, 2)
            act.activation(t2[:], t2[:], ACT.Exp, scale=-1.0).then_inc(act_step, 1)
            act.wait_ge(act_step, 3)
            act.activation(t2[:], t2[:], ACT.Ln, bias=1.0).then_inc(act_step, 1)



def phase_ffn(nc, k, name, kind="ffn"):
    steps = B * TILES // FFN_TILES
    with Ctx(nc, k, name, kind) as c, nc.Block() as block:
        s = Stage()
        s.minus_half = k.minus_half
        ln_buffers(s, c, FFN_TILES)
        nT = c.sb("nT", [P, FFN_TILES, P])
        nT_ready, y_ready, x_done = (c.sem(n) for n in ("nT_ready", "y_ready", "x_done"))
        dve_step = c.sem("dve_step")
        turned, y = k.bank[0], k.bank[1]

        def x_at(step):
            return lambda t: k.x[:, bass.ds(step * FFN_TILES + t, 1), :].rearrange("p a c -> p (a c)")

        @block.vector
        def _(dve):
            credit(dve, x_done)
            chain = Chain(dve, dve_step)
            ln_stats(dve, chain, s, x_at(0), FFN_TILES)
            ln_apply(dve, s, x_at(0), FFN_TILES, 0)
            with dve.Fori(0, steps) as i:
                chain.start(2 * i + 2)
                ln_stats(dve, chain, s, x_at(i + 1), FFN_TILES)
                ln_apply(dve, s, x_at(i + 1), FFN_TILES, i + 1)
                dve.wait_ge(y_ready, of(i))
                x_now = k.x[:, bass.ds(i * FFN_TILES, FFN_TILES), :].rearrange("p a c -> p (a c)")
                dve.tensor_tensor(x_now, x_now, y[:, :], ALU.add).then_inc(x_done, 1)

        @block.gpsimd
        def _(pool):
            ln_power(pool, s, FFN_TILES, 0)
            with pool.Fori(0, steps) as i:
                ln_power(pool, s, FFN_TILES, i + 1)

        @block.tensor
        def _(pe):
            credit(pe, y_ready)
            with pe.Fori(0, steps) as i:
                pe.wait_ge(s.norm_ready, i + 1)
                pe.wait_ge(nT_ready, before(i))
                for t in range(FFN_TILES):
                    ins = pe.transpose(turned[:, t * P:(t + 1) * P], s.norm[:, t, :], k.w["ident"][:])
                    if t == FFN_TILES - 1:
                        ins.then_inc(s.norm_used, 1)
                pe.wait_ge(nT_ready, of(i))
                pe.wait_ge(x_done, before(i))
                for t in range(FFN_TILES):
                    out = y[:, t * C:(t + 1) * C]
                    pe.matmul(out, nT[:, t, :], k.w_ffn[:], start=True, stop=False)
                    ins = pe.matmul(out, k.ones_row[:], k.b_ffn[:], start=False, stop=True)
                ins.then_inc(y_ready, 1)

        @block.scalar
        def _(act):
            credit(act, nT_ready)
            with act.Fori(0, steps) as i:
                act.wait_ge(s.norm_used, i + 1)
                act.wait_ge(y_ready, before(i))
                act.activation(nT[:].rearrange("p a c -> p (a c)"), turned[:, :], ACT.Copy).then_inc(nT_ready, 1)



def outer_and_scan(dve, s, v_banks, v_bias, n):
    dve.wait_ge(s.qkT_ready, of(n))
    dve.wait_ge(s.prod_ready, before(n, 2, 2))
    for chunk in range(D // 2):
        dve.wait_ge(s.v_ready, of(n, chunk + 1, D // 2))
        for e in (2 * chunk, 2 * chunk + 1):
            v = v_banks[chunk % 2][:, (e % 2) * T:(e % 2 + 1) * T]
            if v_bias is None:
                ins = dve.tensor_tensor(s.kv[:, e, :], v, s.kT[:], ALU.mult)
            else:
                ins = dve.scalar_tensor_tensor(s.kv[:, e, :], v, v_bias[:, e:e + 1], s.kT[:], ALU.add, ALU.mult)
            ins.then_inc(s.kv_done, 1)
        if chunk == 0:
            dve.wait_ge(s.decay_ready, of(n))
        for e in (2 * chunk, 2 * chunk + 1):
            dve.wait_ge(s.kv_done, of(n, e + 1, D))
            dve.tensor_tensor_scan(s.M[:, e, :], s.decay[:], s.kv[:, e, :], 0.0, ALU.mult, ALU.add) \
               .then_inc(s.scan_done, 1)


def query_states(pool, s, n):
    half = D // 2
    pool.wait_ge(s.sum_ready, before(n))
    for j in range(2):
        pool.wait_ge(s.scan_done, of(n, half * (j + 1), D))
        e = slice(half * j, half * (j + 1))
        pool.tensor_tensor(s.prod[:, e, :], s.M[:, e, :], s.qT[:].unsqueeze(1).broadcast_to([P, half, T]),
                           ALU.mult).then_inc(s.prod_ready, 1)


def spread_values(pe, s, v_banks, w_v, n, banks_free):
    for chunk in range(D // 2):
        if chunk < 2:
            banks_free(chunk)
        else:
            pe.wait_ge(s.kv_done, of(n, 2 * (chunk - 1), D))
        for e in (2 * chunk, 2 * chunk + 1):
            ins = pe.matmul(v_banks[chunk % 2][:, (e % 2) * T:(e % 2 + 1) * T], w_v[:, e, :], s.nT[:],
                            start=True, stop=True)
        ins.then_inc(s.v_ready, 1)


def recurrence_buffers(s, c):
    s.nT = c.sb("nT", [P, T])
    s.qT = c.sb("qT", [P, T])
    s.kT = c.sb("kT", [P, T])
    s.decay = c.sb("decay", [P, T])
    s.kv = c.sb("kv", [P, D, T])
    s.M = c.sb("M", [P, D, T])
    s.prod = c.sb("prod", [P, D, T])
    s.z_relu = c.sb("z_relu", [P, T])
    s.z_exp = c.sb("z_exp", [P, T])
    s.softplus = c.sb("softplus", [P, T])
    s.nT_ready, s.qkz_ready, s.qkT_ready, s.z_read, s.z_parts = c.sems(
        "nT_ready", "qkz_ready", "qkT_ready", "z_read", "z_parts")
    s.softplus_ready, s.decay_ready, s.v_ready, s.kv_done, s.scan_done = c.sems(
        "softplus_ready", "decay_ready", "v_ready", "kv_done", "scan_done")
    s.prod_ready, s.sum_ready, s.act_step, s.dve_step = c.sems(
        "prod_ready", "sum_ready", "act_step", "dve_step")


def x_tile(k, seq):
    return lambda t: k.x[:, bass.ds(seq * TILES + t, 1), :].rearrange("p a c -> p (a c)")


def x_seq(k, seq):
    return k.x[:, bass.ds(seq * TILES, TILES), :].rearrange("p a c -> p (a c)")



def phase_mixer(nc, k, name, kind="mixer"):
    w = k.w
    with Ctx(nc, k, name, kind) as c, nc.Block() as block:
        s = Stage()
        s.minus_half = k.minus_half
        ln_buffers(s, c, TILES)
        recurrence_buffers(s, c)
        s.hT = c.sb("hT", [P, T])
        s.qk = c.sb("qk", [P, 2, TILES, C])
        s.qk_sq = c.sb("qk_sq", [P, 2, TILES, C])
        s.ss = c.sb("ss", [P, 2 * TILES * H])
        s.guess = c.sb("guess", [P, 2 * TILES * H])
        s.rs = c.sb("rs", [P, 2 * TILES * H])
        s.parts = c.sb("parts", [P, 2, TILES * H, SPLIT, D], F32R)
        s.qp = c.sb("qp", [P, GROUPS, T], F32R)
        s.kp = c.sb("kp", [P, GROUPS, T], F32R)
        s.probs = c.sb("probs", [P, 2 * LANES, 2 * T])
        s.oT = c.sb("oT", [P, GROUPS, T])
        s.rden = c.sb("rden", [P, TILES, H, 1])
        s.on = c.sb("on", [P, TILES, C])
        s.onT = c.sb("onT", [P, T])
        s.hT_ready, s.qk_rows, s.v_rows, s.qk_sb, s.qk_sq_ready = c.sems(
            "hT_ready", "qk_rows", "v_rows", "qk_sb", "qk_sq_ready")
        s.z_ready, s.guess_ready, s.vaug_ready, s.parts_ready, s.q_turned = c.sems(
            "z_ready", "guess_ready", "vaug_ready", "parts_ready", "q_turned")
        s.k_turned, s.qp_ready, s.kp_ready, s.scores_ready, s.exp_done = c.sems(
            "k_turned", "qp_ready", "kp_ready", "scores_ready", "exp_done")
        s.pv_done, s.on_ready, s.on_turned, s.onT_ready, s.out_ready = c.sems(
            "pv_done", "on_ready", "on_turned", "onT_ready", "out_ready")
        s.x_done, s.normed, s.oT_ready, s.o_rows, s.q_high = c.sems(
            "x_done", "normed", "oT_ready", "o_rows", "q_high")
        score_bank, o_bank, misc, proj, v_banks = k.bank[0:3], k.bank[3], k.bank[4], k.bank[5], k.bank[6:8]
        sum_bank = [o_bank, misc]
        o_rows = [score_bank[t][:, :].rearrange("p (h e) -> p h e", h=H) for t in range(TILES)]

        @block.tensor
        def _(pe):
            for sem, per in ((s.v_ready, D // 2), (s.sum_ready, 1), (s.qkz_ready, 1), (s.qk_rows, 1), (s.v_rows, 1),
                             (s.q_turned, 1), (s.k_turned, 1), (s.scores_ready, H), (s.pv_done, GROUPS),
                             (s.o_rows, 1), (s.on_turned, 1), (s.out_ready, 1)):
                credit(pe, sem, per)

            def project(n):
                pe.wait_ge(s.norm_ready, n + 1)
                pe.wait_ge(s.nT_ready, before(n))
                for t in range(TILES):
                    ins = pe.transpose(misc[:, t * P:(t + 1) * P], s.norm[:, t, :], w["ident"][:])
                ins.then_inc(s.norm_used, 1)
                pe.wait_ge(s.nT_ready, of(n))
                pe.wait_ge(s.qk_sb, before(n))
                pe.matmul(proj[:, 0:T], w["mix_q"][:], s.nT[:], start=True, stop=True)
                pe.matmul(proj[:, T:2 * T], w["mix_k"][:], s.nT[:], start=True, stop=True)
                pe.matmul(score_bank[2][:, 0:T], w["mix_g"][:], s.nT[:], start=True, stop=True).then_inc(s.qkz_ready, 1)
                spread_values(pe, s, v_banks, w["mix_v"], n,
                              lambda chunk: pe.wait_ge(s.kp_ready, before(n)))

            def sum_states(n):
                pe.wait_ge(s.prod_ready, of(n, 2, 2))
                for e in range(D):
                    ins = pe.matmul(v_banks[1][:, 0:T], w["sum_d"][:, e, :], s.prod[:, e, :], start=(e == 0), stop=(e == D - 1))
                ins.then_inc(s.sum_ready, 1)

            def rows(n):
                for t in range(TILES):
                    ins = pe.matmul(v_banks[0][:, t * C:(t + 1) * C], s.nT[:, t * P:(t + 1) * P], w["v"][:], start=True, stop=True)
                ins.then_inc(s.v_rows, 1)
                pe.wait_ge(s.hT_ready, of(n))
                for t in range(TILES):
                    ins = pe.matmul(proj[:, t * 2 * C:(t + 1) * 2 * C], s.hT[:, t * P:(t + 1) * P], w["qk"][:], start=True, stop=True)
                ins.then_inc(s.qk_rows, 1)

            def turn_qk(n):
                pe.wait_ge(s.parts_ready, of(n))
                pe.wait_ge(s.vaug_ready, of(n))
                for banks, which, turned in ((score_bank, 0, s.q_turned), (v_banks, 1, s.k_turned)):
                    for g in range(GROUPS):
                        for t in range(TILES):
                            at, first = (g % 2) * T + t * P, t * H + LANES * g
                            ins = pe.transpose(banks[g // 2][:, at:at + P],
                                               s.parts[:, which, first:first + LANES].rearrange("p h s e -> p (h s e)").bitcast(F32),
                                               w["ident"][:])
                    ins.then_inc(turned, 1)

            def lane(j):
                return slice(32 * j, 32 * (j + 1))

            def scores(i, h):
                if h == 0:
                    pe.wait_ge(s.qp_ready, of(i))
                    pe.wait_ge(s.kp_ready, of(i))
                if h == 2:
                    pe.wait_ge(s.z_read, of(i + 1))
                if h >= 3:
                    pe.wait_ge(s.exp_done, of(i, h - 2, H))
                for kt in range(TILES):
                    ins = pe.matmul(score_bank[h % 3][:, kt * T:(kt + 1) * T], s.kp[lane(h % LANES), h // LANES, kt * P:(kt + 1) * P],
                                    s.qp[lane(h % LANES), h // LANES, :], start=True, stop=True)
                ins.then_inc(s.scores_ready, 1)

            def weigh(i, g):
                if g == 0:
                    pe.wait_ge(s.x_done, before(i))
                    pe.wait_ge(s.vaug_ready, of(i))
                if g >= 2:
                    pe.wait_ge(s.oT_ready, of(i, g - 1, GROUPS))
                pe.wait_ge(s.exp_done, of(i, LANES * (g + 1), H))
                for kt in range(TILES):
                    for j in range(LANES):
                        h = LANES * g + j
                        ins = pe.matmul(sum_bank[g % 2][lane(j), 0:T], k.vaug[:, kt, h, :],
                                        s.probs[:, h % (2 * LANES), kt * T:(kt + 1) * T],
                                        start=(kt == 0), stop=(kt == TILES - 1))
                ins.then_inc(s.pv_done, 1)

            def turn_back(i):
                pe.wait_ge(s.oT_ready, of(i, GROUPS, GROUPS))
                for t in range(TILES):
                    for g in range(GROUPS):
                        ins = pe.transpose(score_bank[t][:, g * P:(g + 1) * P], s.oT[:, g, t * P:(t + 1) * P], w["ident"][:])
                ins.then_inc(s.o_rows, 1)

            def turn_o(i):
                pe.wait_ge(s.on_ready, of(i))
                for t in range(TILES):
                    ins = pe.transpose(misc[:, T + t * P:T + (t + 1) * P], s.on[:, t, :], w["ident"][:])
                ins.then_inc(s.on_turned, 1)

            def output(i):
                pe.wait_ge(s.onT_ready, of(i))
                for t in range(TILES):
                    out = o_bank[:, t * C:(t + 1) * C]
                    pe.matmul(out, s.onT[:, t * P:(t + 1) * P], w["o"][:], start=True, stop=False)
                    ins = pe.matmul(out, k.ones_row[:], w["bo"][:], start=False, stop=True)
                ins.then_inc(s.out_ready, 1)

            lag = LANES + 1
            project(0)
            sum_states(0)
            rows(0)
            turn_qk(0)
            with pe.Fori(0, B) as i:
                project(i + 1)
                for h in range(H + 2):
                    if h < H:
                        scores(i, h)
                    if h >= lag and (h - lag) % LANES == 0:
                        weigh(i, (h - lag) // LANES)
                sum_states(i + 1)
                turn_back(i)
                rows(i + 1)
                turn_o(i)
                output(i)
                turn_qk(i + 1)

        @block.scalar
        def _(act):
            for sem, per in ((s.nT_ready, 1), (s.qkT_ready, 1), (s.z_read, 1), (s.z_parts, 1), (s.decay_ready, 1),
                             (s.exp_done, H), (s.hT_ready, 1), (s.onT_ready, 1), (s.qk_sq_ready, 1), (s.qp_ready, 1),
                             (s.guess_ready, 1), (s.oT_ready, GROUPS), (s.q_high, 1)):
                credit(act, sem, per)
            nc.scalar.preload_act_table_set(LOG_EXP_SET)
            chain = Chain(act, s.act_step)

            def project(n):
                chain.start(2 * n)
                act.wait_ge(s.norm_used, n + 1)
                act.activation(s.nT[:], misc[:, 0:T], ACT.Copy).then_inc(s.nT_ready, 1)
                act.wait_ge(s.qkz_ready, of(n))
                act.activation(s.kT[:], proj[:, T:2 * T], ACT.Identity, bias=w["mix_bk"][:])
                act.activation(s.qT[:], proj[:, 0:T], ACT.Identity, bias=w["mix_bq"][:]).then_inc(s.qkT_ready, 1)
                act.activation(s.z_relu[:], score_bank[2][:, 0:T], ACT.Relu, bias=w["mix_bg"][:])
                act.activation(s.z_exp[:], score_bank[2][:, 0:T], ACT.Abs, bias=w["mix_bg"][:]).then_inc(s.z_read, 1)
                act.wait_ge(s.z_read, of(n))
                chain.link(act.activation(s.z_exp[:], s.z_exp[:], ACT.Exp, scale=-1.0))
                act.activation(s.z_exp[:], s.z_exp[:], ACT.Ln, bias=1.0).then_inc(s.z_parts, 1)
                act.wait_ge(s.softplus_ready, of(n))
                act.activation(s.decay[:], s.softplus[:], ACT.Exp, scale=-1.0).then_inc(s.decay_ready, 1)

            def h_copy(n):
                act.wait_ge(s.sum_ready, of(n))
                act.activation(s.hT[:], v_banks[1][:, 0:T], ACT.Copy).then_inc(s.hT_ready, 1)

            def square(n):
                act.wait_ge(s.qk_sb, of(n))
                act.activation(s.qk_sq[:], s.qk[:], ACT.Square).then_inc(s.qk_sq_ready, 1)

            def q_high(n):
                act.wait_ge(s.normed, of(n))
                act.activation(s.parts[:, 0, :, 0:2, :], s.qk[:, 0].rearrange("p t (h e) -> p (t h) e", e=D).unsqueeze(2)
                               .broadcast_to([P, TILES * H, 2, D]), ACT.Copy).then_inc(s.q_high, 1)

            def q_copy(n):
                act.wait_ge(s.q_turned, of(n))
                for b in range(2):
                    ins = act.activation(s.qp[:, 2 * b:2 * b + 2, :].rearrange("p g t -> p (g t)"), score_bank[b][:, :], ACT.Copy)
                ins.then_inc(s.qp_ready, 1)

            def o_copy(i, g):
                act.wait_ge(s.pv_done, of(i, g + 1, GROUPS))
                act.activation(s.oT[:, g, :], sum_bank[g % 2][:, 0:T], ACT.Copy).then_inc(s.oT_ready, 1)

            project(0)
            h_copy(0)
            square(0)
            root_guess(act, chain, s, s.ss, 0)
            q_high(0)
            q_copy(0)
            with act.Fori(0, B) as i:
                project(i + 1)
                for h in range(H):
                    act.wait_ge(s.scores_ready, of(i, h + 1, H))
                    if h % LANES == 0:
                        act.wait_ge(s.pv_done, of(i, h // LANES - 1, GROUPS))
                    act.activation(s.probs[:, h % (2 * LANES), :], score_bank[h % 3][:, :], ACT.Exp,
                                   bias=k.exp_shift[:, h:h + 1]).then_inc(s.exp_done, 1)
                    if h % LANES == LANES - 1 and h > LANES:
                        o_copy(i, h // LANES - 1)
                o_copy(i, GROUPS - 1)
                h_copy(i + 1)
                square(i + 1)
                act.wait_ge(s.on_turned, of(i))
                act.activation(s.onT[:], misc[:, T:2 * T], ACT.Copy).then_inc(s.onT_ready, 1)
                root_guess(act, chain, s, s.ss, i + 1)
                q_high(i + 1)
                q_copy(i + 1)

        @block.gpsimd
        def _(pool):
            forget(pool, k, "ffn")
            for sem, per in ((s.softplus_ready, 1), (s.prod_ready, 2)):
                credit(pool, sem, per)

            def front(n):
                pool.wait_ge(s.z_parts, of(n))
                pool.tensor_tensor(s.softplus[:], s.z_relu[:], s.z_exp[:], ALU.add).then_inc(s.softplus_ready, 1)
                query_states(pool, s, n)

            ln_power(pool, s, TILES, 0)
            front(0)
            ln_power(pool, s, TILES, 1)
            with pool.Fori(0, B) as i:
                front(i + 1)
                ln_power(pool, s, TILES, i + 2)

        @block.vector
        def _(dve):
            for sem, per in ((s.kv_done, D), (s.scan_done, D), (s.qk_sb, 1), (s.vaug_ready, 1), (s.z_ready, 1),
                             (s.normed, 1), (s.parts_ready, 1), (s.kp_ready, 1), (s.on_ready, 1), (s.x_done, 1)):
                credit(dve, sem, per)
            chain = Chain(dve, s.dve_step)

            def norm_rows(n):
                ln_stats(dve, chain, s, x_tile(k, n), TILES)
                ln_apply(dve, s, x_tile(k, n), TILES, n)

            def qk_rows(n):
                dve.wait_ge(s.qk_rows, of(n))
                dve.tensor_tensor(s.qk[:].rearrange("p w t c -> p t w c"), proj[:, :].rearrange("p (t w c) -> p t w c", w=2, c=C),
                                  k.bqk_rows[:].rearrange("p t (w c) -> p t w c", w=2), ALU.add).then_inc(s.qk_sb, 1)
                dve.wait_ge(s.v_rows, of(n))
                dve.tensor_tensor(k.vaug[:, :, :, 0:D].rearrange("p t h e -> p (t h) e"),
                                  v_banks[0][:, 0:TILES * C].rearrange("p (g e) -> p g e", e=D),
                                  k.bv_rows[:].rearrange("p t (h e) -> p (t h) e", e=D), ALU.add).then_inc(s.vaug_ready, 1)
                heads = s.qk[:].rearrange("p w t (h e) -> p (w t h) e", e=D)
                dve.wait_ge(s.qk_sq_ready, of(n))
                chain.link(dve.tensor_reduce(s.ss[:], s.qk_sq[:].rearrange("p w t (h e) -> p (w t h) e", e=D), AX_X, ALU.add))
                dve.tensor_scalar(s.ss[:], s.ss[:], L2_FLOOR, ROOT_SCALE, ALU.max, ALU.mult).then_inc(s.z_ready, 1)
                chain.link(refine_root(dve, chain, s, s.ss, n))
                chain.link(dve.tensor_tensor(s.rs[:], s.rs[:], k.l2_scale[:].rearrange("p w t h -> p (w t h)"), ALU.mult))
                dve.tensor_tensor(heads, heads, s.rs[:].unsqueeze(2).broadcast_to([P, 2 * TILES * H, D]),
                                  ALU.mult).then_inc(s.normed, 1)
                half = [P, TILES * H, 2, D]
                q, kk = [s.qk[:, which].rearrange("p t (h e) -> p (t h) e", e=D).unsqueeze(2).broadcast_to(half)
                         for which in range(2)]
                dve.wait_ge(s.normed, of(n))
                chain.link(dve.tensor_copy(s.parts[:, 1, :, 0:SPLIT:2, :], kk))
                dve.tensor_tensor(s.parts[:, 1, :, 1:SPLIT:2, :], kk, s.parts[:, 1, :, 0:SPLIT:2, :].bitcast(F32), ALU.subtract)
                dve.wait_ge(s.q_high, of(n))
                dve.tensor_tensor(s.parts[:, 0, :, 2:SPLIT, :], q, s.parts[:, 0, :, 0:2, :].bitcast(F32),
                                  ALU.subtract).then_inc(s.parts_ready, 1)

            def k_copy(n):
                dve.wait_ge(s.k_turned, of(n))
                for b in range(2):
                    ins = dve.tensor_copy(s.kp[:, 2 * b:2 * b + 2, :].rearrange("p g t -> p (g t)"), v_banks[b][:, :])
                ins.then_inc(s.kp_ready, 1)

            def weighted(i):
                dve.wait_ge(s.o_rows, of(i))
                for t in range(TILES):
                    ins = dve.reciprocal(s.rden[:, t], o_rows[t][:, :, D:D + 1])
                chain.link(ins)
                for t in range(TILES):
                    ins = dve.tensor_tensor(s.on[:, t, :].rearrange("p (h e) -> p h e", e=D), o_rows[t][:, :, 0:D],
                                            s.rden[:, t].broadcast_to([P, H, D]), ALU.mult)
                ins.then_inc(s.on_ready, 1)

            norm_rows(0)
            outer_and_scan(dve, s, v_banks, w["mix_bv"], 0)
            norm_rows(1)
            qk_rows(0)
            k_copy(0)
            first = chain.n
            with dve.Fori(0, B) as i:
                chain.start(9 * i + first)
                outer_and_scan(dve, s, v_banks, w["mix_bv"], i + 1)
                norm_rows(i + 2)
                weighted(i)
                qk_rows(i + 1)
                dve.wait_ge(s.out_ready, of(i))
                dve.tensor_tensor(x_seq(k, i), x_seq(k, i), o_bank[:, 0:TILES * C], ALU.add).then_inc(s.x_done, 1)
                k_copy(i + 1)
                assert chain.n == 9, chain.n



def phase_moe(nc, k, name, kind="moe"):
    w = k.w
    CAUSAL = BLOCKS * P
    SEL = TILES * NE
    SPREADS = PAIRS * NE // 2
    with Ctx(nc, k, name, kind) as c, nc.Block() as block:
        s = Stage()
        s.minus_half = k.minus_half
        ln_buffers(s, c, TILES)
        s.nT = c.sb("nT", [P, T])
        s.nV = c.sb("nV", [P, T])
        s.qT = c.sb("qT", [P, PAIRS, T])
        s.kT = c.sb("kT", [P, PAIRS, T])
        s.gates = c.sb("gates", [P, TILES * EH, NE])
        s.ranked = c.sb("ranked", [P, TILES * EH, NE])
        s.best = c.sb("best", [P, TILES * EH])
        s.top_gate = c.sb("top_gate", [P, TILES * EH])
        s.onehot = c.sb("onehot", [P, TILES, EH, NE])
        s.block_max = c.sb("block_max", [P, EH, BLOCKS])
        s.max1 = c.sb("max1", [P, EH])
        s.shift = c.sb("shift", [P, TILES, EH])
        s.part_bf = c.sb("part_bf", [P, TILES, EH], BF16)
        s.parts = c.sb("parts", [P, TILES, PARTS * EH])
        s.partsT = c.sb("partsT", [PARTS * EH, T], BF16)
        s.onehotT = c.sb("onehotT", [EH * NE, T], BF16)
        s.probs = c.sb("probs", [P, EH, CAUSAL])
        s.coef = c.sb("coef", [P, TILES * EH])
        s.o = c.sb("o", [P, TILES * EH, EK])
        s.oT = c.sb("oT", [P, PAIRS, T])
        s.picked = c.sb("picked", [P, 3, 2, T])
        s.taken = c.sb("taken", [P, SEL])
        s.nT_ready, s.q_psum, s.q_ready, s.k_psum, s.k_ready = c.sems(
            "nT_ready", "q_psum", "q_ready", "k_psum", "k_ready")
        s.logits_psum, s.gate_exp_ready, s.onehot_ready, s.rows_ready, s.max_done = c.sems(
            "logits_psum", "gate_exp_ready", "onehot_ready", "rows_ready", "max_done")
        s.parts_ready, s.small_turned, s.small_ready, s.experts_ready, s.selected = c.sems(
            "parts_ready", "small_turned", "small_ready", "experts_ready", "selected")
        s.gated, s.scores_ready, s.exp_done, s.o_psum, s.o_ready = c.sems(
            "gated", "scores_ready", "exp_done", "o_psum", "o_ready")
        s.o_turned, s.oT_ready, s.spread_ready, s.picked_ready, s.picked_used = c.sems(
            "o_turned", "oT_ready", "spread_ready", "picked_ready", "picked_used")
        s.x_done, s.dve_step, s.nV_ready = c.sems(
            "x_done", "dve_step", "nV_ready")
        two, experts, misc, o_banks = k.bank[0:2], k.bank[2:4], k.bank[4], k.bank[5:8]
        acc = [o_banks[t][:, 0:C] for t in range(TILES)]
        oT_banks = [o_banks[2], misc]
        results = TILES * EH

        def o_of(r, last):
            return o_banks[r // OBANK][:, (r % OBANK) * (EK + 1):(r % OBANK) * (EK + 1) + last]

        def o_group(b):
            first, count = b * OBANK, min(OBANK, results - b * OBANK)
            return first, count, o_banks[b][:, 0:count * (EK + 1)].rearrange("p (r e) -> p r e", e=EK + 1)

        @block.tensor
        def _(pe):
            for sem, per in ((s.q_psum, 2), (s.k_psum, 2), (s.logits_psum, 1), (s.rows_ready, EH), (s.small_turned, 1),
                             (s.experts_ready, SEL), (s.scores_ready, EH), (s.o_psum, len(o_banks)), (s.o_turned, 2),
                             (s.spread_ready, SPREADS), (s.picked_used, SPREADS)):
                credit(pe, sem, per)

            def turn_norm(n):
                pe.wait_ge(s.norm_ready, n + 1)
                for t in range(TILES):
                    ins = pe.transpose(misc[:, t * P:(t + 1) * P], s.norm[:, t, :], w["ident"][:])
                ins.then_inc(s.norm_used, 1)

            def project(b, weight, ready):
                for p in (2 * b, 2 * b + 1):
                    ins = pe.matmul(experts[b][:, (p % 2) * T:(p % 2 + 1) * T], weight[:, p * P:(p + 1) * P], s.nT[:],
                                    start=True, stop=True)
                ins.then_inc(ready, 1)

            def project_q(n):
                pe.wait_ge(s.nT_ready, of(n))
                pe.wait_ge(s.selected, before(n, SEL, SEL))
                for b in range(2):
                    project(b, w["moe_q"], s.q_psum)

            def project_k(n, b):
                pe.wait_ge(s.q_ready, of(n, b + 1, 2))
                project(b, w["moe_k"], s.k_psum)

            def logits(n):
                for t in range(TILES):
                    ins = pe.matmul(misc[:, T + t * EH * NE:T + (t + 1) * EH * NE], s.nT[:, t * P:(t + 1) * P], w["moe_gate"][:],
                                    start=True, stop=True)
                ins.then_inc(s.logits_psum, 1)

            def head(tensor, h, at, size):
                return tensor[EK * (h % 2):EK * (h % 2 + 1), h // 2, at:at + size]

            def score_rows(i, h):
                if h == 0:
                    pe.wait_ge(s.q_ready, of(i, 2, 2))
                    pe.wait_ge(s.k_ready, of(i, 2, 2))
                if h >= 2:
                    pe.wait_ge(s.max_done, of(i, h - 1, EH))
                b = two[h % 2]
                pe.matmul(b[:, 0:P], head(s.qT, h, 0, P), head(s.kT, h, 0, P), start=True, stop=False)
                pe.matmul(b[:, 0:P], w["ident_bf"][:], w["mask_rows"][:], start=False, stop=True)
                pe.matmul(b[:, P:CAUSAL], head(s.qT, h, P, P), head(s.kT, h, 0, T), start=True, stop=False, skip_group_check=True)
                pe.matmul(b[:, 2 * P:CAUSAL], w["ident_bf"][:], w["mask_rows"][:], start=False, stop=True,
                          skip_group_check=True).then_inc(s.rows_ready, 1)

            def scores(i, h):
                if h == 0:
                    pe.wait_ge(s.small_ready, of(i))
                if h >= 2:
                    pe.wait_ge(s.exp_done, of(i, h - 1, EH))
                b = two[h % 2]
                for at, key, query, size in ((0, 0, 0, T), (T, P, P, P)):
                    pe.matmul(b[:, at:at + size], head(s.kT, h, key, P), head(s.qT, h, query, size), start=True, stop=False,
                              skip_group_check=True)
                    pe.matmul(b[:, at:at + size], w["shift_sel"][:, h, :], s.partsT[:, query:query + size], start=False, stop=False,
                              skip_group_check=True)
                    ins = pe.matmul(b[:, at:at + P], w["ident_bf"][:], w["mask_T"][:], start=False, stop=True,
                                    skip_group_check=True)
                ins.then_inc(s.scores_ready, 1)

            def expert_values(i, t, experts_of):
                for e in experts_of:
                    j = t * NE + e
                    if j >= 2:
                        pe.wait_ge(s.selected, of(i, j - 1, SEL))
                    pe.matmul(experts[j % 2][:, :], s.nV[:, t * P:(t + 1) * P], w["moe_v"][:, e, :], start=True, stop=True) \
                      .then_inc(s.experts_ready, 1)

            def turn_small(i):
                pe.wait_ge(s.onehot_ready, of(i))
                pe.wait_ge(s.parts_ready, of(i))
                for t in range(TILES):
                    pe.transpose(misc[0:PARTS * EH, t * P:(t + 1) * P], s.parts[:, t, :], w["ident"][:])
                for t in range(TILES):
                    ins = pe.transpose(misc[0:EH * NE, T + t * P:T + (t + 1) * P],
                                       s.onehot[:, t, :, :].rearrange("p h e -> p (h e)"), w["ident"][:])
                ins.then_inc(s.small_turned, 1)

            def weigh(i):
                pe.wait_ge(s.gated, of(i, 2, 2))
                pe.wait_ge(s.exp_done, of(i, EH, EH))
                pe.wait_ge(s.x_done, before(i))
                for r in range(results):
                    t, h = r // EH, r % EH
                    for kt in range(t + 1):
                        at = (t + kt) * P
                        ins = pe.matmul(o_of(r, EK + 1), s.probs[:, h, at:at + P], k.values[:, kt, h, :], start=(kt == 0), stop=(kt == t))
                    if r % OBANK == OBANK - 1 or r == results - 1:
                        ins.then_inc(s.o_psum, 1)

            def turn_o(i):
                pe.wait_ge(s.o_ready, of(i))
                pe.wait_ge(s.gate_exp_ready, of(i + 1))
                for p in range(PAIRS):
                    for t in range(TILES):
                        at = (p % 2) * T + t * P
                        r = t * EH + 2 * p
                        ins = pe.transpose(oT_banks[p // 2][:, at:at + P], s.o[:, r:r + 2, :].rearrange("p r e -> p (r e)"),
                                           w["ident"][:])
                    if p % 2 == 1:
                        ins.then_inc(s.o_turned, 1)

            def spread(i, g):
                if g >= 2:
                    pe.wait_ge(s.picked_ready, of(i, g - 1, SPREADS))
                p, e = g // (NE // 2), 2 * (g % (NE // 2))
                for j in range(2):
                    ins = pe.matmul(two[g % 2][:, j * T:(j + 1) * T], w["spread"][:, p, e + j, :], s.onehotT[:], start=True, stop=True)
                ins.then_inc(s.spread_ready, 1)

            def expert_outputs(i, g):
                pe.wait_ge(s.picked_ready, of(i, g + 1, SPREADS))
                p, e = g // (NE // 2), 2 * (g % (NE // 2))
                for j in range(2):
                    for t in range(TILES):
                        ins = pe.matmul(acc[t], s.picked[:, g % 3, j, t * P:(t + 1) * P], w["moe_o"][:, p, e + j, :],
                                        start=(g == 0 and j == 0), stop=(g == SPREADS - 1 and j == 1))
                ins.then_inc(s.picked_used, 1)

            early = range(NE - 2)
            late = range(NE - 2, NE)
            turn_norm(0)
            project_q(0)
            project_k(0, 0)
            project_k(0, 1)
            logits(0)
            with pe.Fori(0, B) as i:
                for h in range(EH):
                    score_rows(i, h)
                pe.wait_ge(s.nV_ready, of(i))
                expert_values(i, 0, early)
                turn_small(i)
                expert_values(i, 0, late)
                for h in range(EH):
                    scores(i, h)
                expert_values(i, 1, early)
                turn_norm(i + 1)
                expert_values(i, 1, late)
                project_q(i + 1)
                weigh(i)
                project_k(i + 1, 0)
                logits(i + 1)
                spread(i, 0)
                spread(i, 1)
                turn_o(i)
                project_k(i + 1, 1)
                expert_outputs(i, 0)
                for g in range(2, SPREADS):
                    spread(i, g)
                    expert_outputs(i, g - 1)
                expert_outputs(i, SPREADS - 1)

        @block.scalar
        def _(act):
            for sem, per in ((s.nT_ready, 1), (s.q_ready, 2), (s.k_ready, 2), (s.gate_exp_ready, 1), (s.small_ready, 1),
                             (s.exp_done, EH), (s.oT_ready, 2), (s.nV_ready, 1)):
                credit(act, sem, per)

            def norm_copy(n):
                act.wait_ge(s.norm_used, n + 1)
                act.activation(s.nT[:], misc[:, 0:T], ACT.Copy).then_inc(s.nT_ready, 1)

            def projected(n, b, psum, dst, ready, scale):
                act.wait_ge(psum, of(n, b + 1, 2))
                act.activation(dst[:, 2 * b:2 * b + 2, :].rearrange("p g t -> p (g t)"), experts[b][:, :], ACT.Copy,
                               scale=scale).then_inc(ready, 1)

            def q_copies(n):
                for b in range(2):
                    projected(n, b, s.q_psum, s.qT, s.q_ready, EK ** -0.5)

            def k_copy(n, b):
                projected(n, b, s.k_psum, s.kT, s.k_ready, 1.0)

            def gate_exp(n):
                act.wait_ge(s.logits_psum, of(n))
                act.activation(s.gates[:].rearrange("p r e -> p (r e)"), misc[:, T:T + TILES * EH * NE], ACT.Exp,
                               scale=-1.0).then_inc(s.gate_exp_ready, 1)

            norm_copy(0)
            q_copies(0)
            k_copy(0, 0)
            k_copy(0, 1)
            gate_exp(0)
            with act.Fori(0, B) as i:
                act.wait_ge(s.nT_ready, of(i))
                act.activation(s.nV[:], s.nT[:], ACT.Copy).then_inc(s.nV_ready, 1)
                act.wait_ge(s.small_turned, of(i))
                act.activation(s.partsT[:], misc[0:PARTS * EH, 0:T], ACT.Copy)
                act.activation(s.onehotT[:], misc[0:EH * NE, T:2 * T], ACT.Copy).then_inc(s.small_ready, 1)
                for h in range(EH):
                    act.wait_ge(s.scores_ready, of(i, h + 1, EH))
                    act.activation(s.probs[:, h, :], two[h % 2][:, 0:CAUSAL], ACT.Exp).then_inc(s.exp_done, 1)
                norm_copy(i + 1)
                q_copies(i + 1)
                k_copy(i + 1, 0)
                gate_exp(i + 1)
                for b in range(2):
                    act.wait_ge(s.o_turned, of(i, b + 1, 2))
                    act.activation(s.oT[:, 2 * b:2 * b + 2, :].rearrange("p g t -> p (g t)"), oT_banks[b][:, :], ACT.Copy).then_inc(s.oT_ready, 1)
                k_copy(i + 1, 1)

        @block.gpsimd
        def _(pool):
            credit(pool, s.gated, TILES)
            ln_power(pool, s, TILES, 0)
            with pool.Fori(0, B) as i:
                ln_power(pool, s, TILES, i + 1)
                for t in range(TILES):
                    pool.wait_ge(s.selected, of(i, NE * (t + 1), SEL))
                    pool.tensor_tensor(k.values[:, t, :, 0:EK], k.values[:, t, :, 0:EK],
                                       s.top_gate[:, t * EH:(t + 1) * EH].unsqueeze(2).broadcast_to([P, EH, EK]),
                                       ALU.mult).then_inc(s.gated, 1)

        @block.vector
        def _(dve):
            for sem, per in ((s.max_done, EH), (s.parts_ready, 1), (s.selected, SEL), (s.o_ready, 1), (s.picked_ready, SPREADS),
                             (s.x_done, 1), (s.onehot_ready, 1)):
                credit(dve, sem, per)
            chain = Chain(dve, s.dve_step)

            def norm_rows(n):
                ln_stats(dve, chain, s, x_tile(k, n), TILES)
                ln_apply(dve, s, x_tile(k, n), TILES, n)

            wide = [P, TILES * EH, NE]

            def sigmoid(n):
                dve.wait_ge(s.gate_exp_ready, of(n))
                chain.link(dve.tensor_scalar(s.gates[:], s.gates[:], 1.0, None, ALU.add))
                chain.link(dve.reciprocal(s.gates[:], s.gates[:]))

            def top(n):
                chain.link(dve.tensor_reduce(s.top_gate[:], s.gates[:], AX_X, ALU.max))
                chain.link(dve.tensor_tensor(s.ranked[:], s.gates[:], s.top_gate[:].unsqueeze(2).broadcast_to(wide), ALU.is_equal))
                chain.link(dve.tensor_tensor(s.ranked[:], s.ranked[:], w["rank"][:], ALU.mult))

            def first_top(n):
                chain.link(dve.tensor_reduce(s.best[:], s.ranked[:], AX_X, ALU.max))
                dve.tensor_tensor(s.onehot[:].rearrange("p t h e -> p (t h) e"), w["rank"][:],
                                  s.best[:].unsqueeze(2).broadcast_to(wide), ALU.is_equal).then_inc(s.onehot_ready, 1)

            def select(i, t):
                for e in range(NE):
                    dve.wait_ge(s.experts_ready, of(i, t * NE + e + 1, SEL))
                    if e > 0:
                        dve.wait_ge(s.selected, of(i, t * NE + e, SEL))
                    dve.memset(s.taken[:, t * NE + e:t * NE + e + 1], 0.0)
                    dve.copy_predicated(k.values[:, t, :, 0:EK],
                                        s.onehot[:, t, :, e:e + 1].bitcast(U32).broadcast_to([P, EH, EK]),
                                        experts[e % 2][:, :].rearrange("p (h e) -> p h e", e=EK)).then_inc(s.selected, 1)

            norm_rows(0)
            for step in (sigmoid, top, first_top):
                step(0)
            first = chain.n
            with dve.Fori(0, B) as i:
                chain.start(20 * i + first)
                for h in range(EH):
                    dve.wait_ge(s.rows_ready, of(i, h + 1, EH))
                    dve.tensor_reduce(s.block_max[:, h, :], two[h % 2][:, 0:CAUSAL].rearrange("p (b k) -> p b k", k=P), AX_X,
                                      ALU.max).then_inc(s.max_done, 1)
                dve.wait_ge(s.max_done, of(i, EH, EH))
                dve.tensor_scalar(s.shift[:, 0, :], s.block_max[:, :, 0], -1.0, None, ALU.mult)
                chain.link(dve.tensor_tensor(s.max1[:], s.block_max[:, :, 1], s.block_max[:, :, 2], ALU.max))
                chain.link(dve.tensor_scalar(s.shift[:, 1, :], s.max1[:], -1.0, None, ALU.mult))
                for part in range(PARTS - 1):
                    chain.link(dve.tensor_copy(s.part_bf[:], s.shift[:]))
                    dve.tensor_copy(s.parts[:, :, part * EH:(part + 1) * EH], s.part_bf[:])
                    chain.link(dve.tensor_tensor(s.shift[:], s.shift[:], s.part_bf[:], ALU.subtract))
                dve.tensor_copy(s.parts[:, :, (PARTS - 1) * EH:PARTS * EH], s.shift[:]).then_inc(s.parts_ready, 1)
                dve.wait_ge(s.onehot_ready, of(i))
                select(i, 0)
                norm_rows(i + 1)
                select(i, 1)
                for b in range(len(o_banks)):
                    first_r, count, view = o_group(b)
                    coef = s.coef[:, first_r:first_r + count]
                    dve.wait_ge(s.o_psum, of(i, b + 1, len(o_banks)))
                    chain.link(dve.reciprocal(coef.unsqueeze(2), view[:, :, EK:EK + 1]))
                    chain.link(dve.tensor_tensor(coef, coef, s.top_gate[:, first_r:first_r + count], ALU.mult))
                    ins = dve.tensor_tensor(s.o[:, first_r:first_r + count, :], view[:, :, 0:EK],
                                            coef.unsqueeze(2).broadcast_to([P, count, EK]), ALU.mult)
                ins.then_inc(s.o_ready, 1)
                between = {SPREADS // 4: sigmoid, SPREADS // 2: top, 3 * SPREADS // 4: first_top}
                for g in range(SPREADS):
                    if g % (SPREADS // 2) == 0:
                        dve.wait_ge(s.oT_ready, of(i, g // (SPREADS // 2) + 1, 2))
                    dve.wait_ge(s.spread_ready, of(i, g + 1, SPREADS))
                    dve.wait_ge(s.picked_used, of(i, g - 2, SPREADS))
                    dve.tensor_tensor(s.picked[:, g % 3], two[g % 2][:, :].rearrange("p (j t) -> p j t", t=T),
                                      s.oT[:, g // (NE // 2), :].unsqueeze(1).broadcast_to([P, 2, T]), ALU.mult).then_inc(s.picked_ready, 1)
                    if g in between:
                        between[g](i + 1)
                dve.wait_ge(s.picked_used, of(i, SPREADS, SPREADS))
                for t in range(TILES):
                    ins = dve.scalar_tensor_tensor(x_tile(k, i)(t), acc[t], 0.5, x_tile(k, i)(t), ALU.mult, ALU.add)
                ins.then_inc(s.x_done, 1)
                assert chain.n == 20, chain.n



def phase_gla(nc, k, name, kind="gla"):
    w = k.w
    with Ctx(nc, k, name, kind) as c, nc.Block() as block:
        s = Stage()
        s.minus_half = k.minus_half
        ln_buffers(s, c, TILES)
        recurrence_buffers(s, c)
        s.low = c.sb("low", [GLA_RANK, T])
        s.gate_exp = c.sb("gate_exp", [P, TILES * C])
        s.gate = c.sb("gate", [P, TILES * C])
        s.o_sq = c.sb("o_sq", [P, TILES, D, H])
        s.ms = c.sb("ms", [P, TILES * H])
        s.guess = c.sb("guess", [P, TILES * H])
        s.rs = c.sb("rs", [P, TILES * H])
        s.on = c.sb("on", [P, TILES, C])
        s.gated = c.sb("gated", [P, TILES, C])
        s.onT = c.sb("onT", [P, T])
        s.low_psum, s.low_ready, s.gate_psum, s.gate_exp_ready, s.gate_ready = c.sems(
            "low_psum", "low_ready", "gate_psum", "gate_exp_ready", "gate_ready")
        s.o_sq_ready, s.z_ready, s.guess_ready, s.on_ready, s.gated_ready = c.sems(
            "o_sq_ready", "z_ready", "guess_ready", "on_ready", "gated_ready")
        s.on_turned, s.onT_ready, s.out_ready, s.x_done = c.sems(
            "on_turned", "onT_ready", "out_ready", "x_done")
        o_bank, out_bank, gate_bank, z_bank, misc, proj, v_banks = *k.bank[0:6], k.bank[6:8]
        o_heads = o_bank[:, 0:TILES * C].rearrange("p (t e h) -> p t h e", t=TILES, e=D)

        @block.tensor
        def _(pe):
            for sem, per in ((s.v_ready, D // 2), (s.sum_ready, 1), (s.qkz_ready, 1), (s.low_psum, 1),
                             (s.gate_psum, 1), (s.on_turned, 1), (s.out_ready, 1)):
                credit(pe, sem, per)

            def project(n):
                pe.wait_ge(s.norm_ready, n + 1)
                pe.wait_ge(s.nT_ready, before(n))
                for t in range(TILES):
                    ins = pe.transpose(misc[:, t * P:(t + 1) * P], s.norm[:, t, :], w["ident"][:])
                ins.then_inc(s.norm_used, 1)
                pe.wait_ge(s.nT_ready, of(n))
                pe.wait_ge(s.qkT_ready, before(n))
                pe.wait_ge(s.z_read, before(n))
                pe.matmul(z_bank[0:GLA_RANK, 0:T], w["gla_g1"][:], s.nT[:], start=True, stop=True).then_inc(s.low_psum, 1)
                pe.matmul(proj[:, 0:T], w["gla_q"][:], s.nT[:], start=True, stop=True)
                pe.matmul(proj[:, T:2 * T], w["gla_k"][:], s.nT[:], start=True, stop=True)
                pe.wait_ge(s.low_ready, of(n))
                pe.matmul(z_bank[:, T:2 * T], w["gla_g2"][:], s.low[:], start=True, stop=True).then_inc(s.qkz_ready, 1)
                spread_values(pe, s, v_banks, w["gla_v"], n,
                              lambda chunk: pe.wait_ge(s.kv_done, before(n, D // 2 + 2 * (chunk + 1), D)))
                pe.wait_ge(s.gate_ready, before(n))
                for t in range(TILES):
                    ins = pe.matmul(gate_bank[:, t * C:(t + 1) * C], s.nT[:, t * P:(t + 1) * P], w["gla_gate"][:], start=True, stop=True)
                ins.then_inc(s.gate_psum, 1)

            def sum_states(n):
                pe.wait_ge(s.prod_ready, of(n, 2, 2))
                pe.wait_ge(s.on_ready, before(n))
                for t in range(TILES):
                    for e in range(D):
                        at = t * C + e * H
                        ins = pe.matmul(o_bank[:, at:at + H], s.prod[:, e, t * P:(t + 1) * P], w["sum_dh"][:], start=True, stop=True)
                ins.then_inc(s.sum_ready, 1)

            def output(i):
                pe.wait_ge(s.gated_ready, of(i))
                for t in range(TILES):
                    ins = pe.transpose(misc[:, T + t * P:T + (t + 1) * P], s.gated[:, t, :], w["ident"][:])
                ins.then_inc(s.on_turned, 1)
                pe.wait_ge(s.onT_ready, of(i))
                pe.wait_ge(s.x_done, before(i))
                for t in range(TILES):
                    ins = pe.matmul(out_bank[:, t * C:(t + 1) * C], s.onT[:, t * P:(t + 1) * P], w["gla_o"][:], start=True, stop=True)
                ins.then_inc(s.out_ready, 1)

            project(0)
            sum_states(0)
            with pe.Fori(0, B) as i:
                project(i + 1)
                output(i)
                sum_states(i + 1)

        @block.scalar
        def _(act):
            for sem, per in ((s.nT_ready, 1), (s.qkT_ready, 1), (s.z_read, 1), (s.z_parts, 1), (s.decay_ready, 1),
                             (s.low_ready, 1), (s.gate_exp_ready, 1), (s.o_sq_ready, 1), (s.onT_ready, 1),
                             (s.guess_ready, 1)):
                credit(act, sem, per)
            nc.scalar.preload_act_table_set(LOG_EXP_SET)
            chain = Chain(act, s.act_step)

            def project(n):
                chain.start(2 * n)
                act.wait_ge(s.norm_used, n + 1)
                act.activation(s.nT[:], misc[:, 0:T], ACT.Copy).then_inc(s.nT_ready, 1)
                act.wait_ge(s.low_psum, of(n))
                act.activation(s.low[:], z_bank[0:GLA_RANK, 0:T], ACT.Copy).then_inc(s.low_ready, 1)
                act.wait_ge(s.qkz_ready, of(n))
                act.activation(s.kT[:], proj[:, T:2 * T], ACT.Copy)
                act.activation(s.qT[:], proj[:, 0:T], ACT.Copy).then_inc(s.qkT_ready, 1)
                act.activation(s.z_relu[:], z_bank[:, T:2 * T], ACT.Relu, bias=k.minus_bg[:], scale=-1.0)
                act.activation(s.z_exp[:], z_bank[:, T:2 * T], ACT.Abs, bias=w["gla_bg"][:]).then_inc(s.z_read, 1)
                act.wait_ge(s.z_read, of(n))
                chain.link(act.activation(s.z_exp[:], s.z_exp[:], ACT.Exp, scale=-1.0))
                act.activation(s.z_exp[:], s.z_exp[:], ACT.Ln, bias=1.0).then_inc(s.z_parts, 1)
                act.wait_ge(s.softplus_ready, of(n))
                act.activation(s.decay[:], s.softplus[:], ACT.Exp, scale=-1.0 / GLA_NORM).then_inc(s.decay_ready, 1)
                act.wait_ge(s.gate_psum, of(n))
                act.activation(s.gate_exp[:], gate_bank[:, 0:TILES * C], ACT.Exp, scale=-1.0).then_inc(s.gate_exp_ready, 1)

            def square(n):
                act.wait_ge(s.sum_ready, of(n))
                act.activation(s.o_sq[:].rearrange("p t e h -> p (t e h)"), o_bank[:, 0:TILES * C], ACT.Square).then_inc(s.o_sq_ready, 1)

            project(0)
            square(0)
            root_guess(act, chain, s, s.ms, 0)
            with act.Fori(0, B) as i:
                project(i + 1)
                act.wait_ge(s.on_turned, of(i))
                act.activation(s.onT[:], misc[:, T:2 * T], ACT.Copy).then_inc(s.onT_ready, 1)
                square(i + 1)
                root_guess(act, chain, s, s.ms, i + 1)

        @block.gpsimd
        def _(pool):
            forget(pool, k, "moe")
            for sem, per in ((s.softplus_ready, 1), (s.prod_ready, 2), (s.gated_ready, 1)):
                credit(pool, sem, per)

            def softplus(n):
                pool.wait_ge(s.z_parts, of(n))
                pool.tensor_tensor(s.softplus[:], s.z_relu[:], s.z_exp[:], ALU.add).then_inc(s.softplus_ready, 1)

            ln_power(pool, s, TILES, 0)
            softplus(0)
            query_states(pool, s, 0)
            ln_power(pool, s, TILES, 1)
            with pool.Fori(0, B) as i:
                pool.wait_ge(s.on_ready, of(i))
                pool.tensor_tensor(s.gated[:].rearrange("p t c -> p (t c)"), s.on[:].rearrange("p t c -> p (t c)"), s.gate[:],
                                   ALU.mult).then_inc(s.gated_ready, 1)
                softplus(i + 1)
                query_states(pool, s, i + 1)
                ln_power(pool, s, TILES, i + 2)

        @block.vector
        def _(dve):
            for sem, per in ((s.kv_done, D), (s.scan_done, D), (s.gate_ready, 1), (s.z_ready, 1), (s.on_ready, 1),
                             (s.x_done, 1)):
                credit(dve, sem, per)
            chain = Chain(dve, s.dve_step)

            def norm_rows(n):
                ln_stats(dve, chain, s, x_tile(k, n), TILES)
                ln_apply(dve, s, x_tile(k, n), TILES, n)

            def mean_square(n):
                dve.wait_ge(s.o_sq_ready, of(n))
                chain.link(dve.tensor_reduce(s.ms[:].rearrange("p (t h) -> p t h", h=H),
                                             s.o_sq[:].rearrange("p t e h -> p t h e"), AX_X, ALU.add))
                dve.tensor_scalar(s.ms[:], s.ms[:], 1.0 / D, RMS_EPS, ALU.mult, ALU.add).then_inc(s.z_ready, 1)

            norm_rows(0)
            outer_and_scan(dve, s, v_banks, None, 0)
            norm_rows(1)
            mean_square(0)
            first = chain.n
            with dve.Fori(0, B) as i:
                chain.start(9 * i + first)
                dve.wait_ge(s.gate_exp_ready, of(i))
                chain.link(dve.tensor_scalar(s.gate[:], s.gate_exp[:], 1.0, None, ALU.add))
                chain.link(dve.reciprocal(s.gate[:], s.gate[:]))
                chain.link(dve.tensor_tensor(s.gate[:], gate_bank[:, 0:TILES * C], s.gate[:], ALU.mult))
                dve.tensor_tensor(s.gate[:], s.gate[:], k.gnorm_rows[:].rearrange("p t c -> p (t c)"), ALU.mult).then_inc(s.gate_ready, 1)
                chain.link(refine_root(dve, chain, s, s.ms, i))
                for t in range(TILES):
                    ins = dve.tensor_tensor(s.on[:, t, :].rearrange("p (h e) -> p h e", e=D), o_heads[:, t],
                                            s.rs[:, t * H:(t + 1) * H].unsqueeze(2).broadcast_to([P, H, D]), ALU.mult)
                ins.then_inc(s.on_ready, 1)
                outer_and_scan(dve, s, v_banks, None, i + 1)
                norm_rows(i + 2)
                dve.wait_ge(s.out_ready, of(i))
                dve.tensor_tensor(x_seq(k, i), x_seq(k, i), out_bank[:, 0:TILES * C], ALU.add).then_inc(s.x_done, 1)
                mean_square(i + 1)
                assert chain.n == 9, chain.n



def phase_store(nc, k, out):
    with Ctx(nc, k, "store") as c, nc.Block() as block:
        stored = c.sem("stored")

        @block.sync
        def _(sp):
            sp.dma_start(out.rearrange("b (t p) c -> p (b t) c", p=P), k.x[:, 0:B * TILES, :]).then_inc(stored, 16)
            sp.wait_ge(stored, 16)


def build(nc, dram, out):
    k = Stage()
    k.sems, k.stack = {}, ExitStack()
    with k.stack, Ctx(nc, k, "all") as c:
        k.bank = [c.stack.enter_context(nc.psum_tensor(f"bank{i}", [P, 512], F32)) for i in range(8)]
        k.x = c.sb("x", [P, B * TILES + FFN_TILES, C])
        k.w = {n: c.sb("w_" + n, list(a.shape), a.dtype) for n, a in dram.items() if n != "x"}
        k.minus_half = c.sb("minus_half", [P, 64])
        k.ones_row = c.sb("ones_row", [1, P])
        k.w_ffn = c.sb("w_ffn", [P, C])
        k.b_ffn = c.sb("b_ffn", [1, C])
        k.bqk_rows = c.sb("bqk_rows", [P, TILES, 2 * C])
        k.bv_rows = c.sb("bv_rows", [P, TILES, C])
        k.gnorm_rows = c.sb("gnorm_rows", [P, TILES, C])
        k.l2_scale = c.sb("l2_scale", [P, 2, TILES, H])
        k.exp_shift = c.sb("exp_shift", [P, H])
        k.minus_bg = c.sb("minus_bg", [P, 1])
        k.vaug = c.sb("vaug", [P, TILES, H, 32])
        k.values = c.sb("values", [P, TILES, EH, EK + 1])
        phase_load(nc, k, dram)
        phase_ffn(nc, k, "ffn_a")
        phase_mixer(nc, k, "mixer")
        phase_ffn(nc, k, "ffn_b")
        phase_moe(nc, k, "moe_a")
        phase_gla(nc, k, "gla")
        phase_moe(nc, k, "moe_b")
        phase_store(nc, k, out)


def layouts(a):
    def recur_v(w):
        return np.repeat(w.reshape(C, H, D).transpose(0, 2, 1), D, axis=2)

    w = {
        "ffn_WT": a["L0_ffn_W"].T, "ffn_b": a["L0_ffn_b"][None],
        "lora_downT": a["L0_ffn_lora_down"].T, "down_aux": a["L0_ffn_down_aux"],
        "lora_upT": a["L0_ffn_lora_up"].T, "up_auxT": a["L0_ffn_up_aux"].T,
        "mix_q": a["L0_attn_Wsq"].T, "mix_k": a["L0_attn_Wsk"].T,
        "mix_bq": a["L0_attn_bsq"][:, None], "mix_bk": a["L0_attn_bsk"][:, None],
        "mix_g": np.repeat(a["L0_attn_Wg"].T, D, axis=1), "mix_bg": np.repeat(a["L0_attn_bg"], D)[:, None],
        "mix_v": recur_v(a["L0_attn_Wsv"].T),
        "mix_bv": np.repeat(a["L0_attn_bsv"].reshape(H, D), D, axis=0),
        "qk": np.concatenate([a["L0_attn_Wq"].T, a["L0_attn_Wk"].T], axis=1),
        "bqk": np.concatenate([a["L0_attn_bq"], a["L0_attn_bk"]])[None],
        "v": a["L0_attn_Wv"].T, "bv": a["L0_attn_bv"][None],
        "o": a["L0_attn_Wo"].T, "bo": a["L0_attn_bo"][None],
        "temp": a["L0_attn_temp"].reshape(1, H),
        "gla_q": a["L1_attn_Wq"], "gla_k": a["L1_attn_Wk"], "gla_v": recur_v(a["L1_attn_Wv"]),
        "gla_g1": a["L1_attn_Wg1"], "gla_g2": a["L1_attn_Wg2"], "gla_bg": a["L1_attn_bg2"][:, None],
        "gla_gate": a["L1_attn_Wg"], "gnorm": np.tile(a["L1_attn_g_norm_w"], H)[None], "gla_o": a["L1_attn_Wo"],
        "moe_q": a["L1_ffn_w_q"], "moe_k": a["L1_ffn_w_k"], "moe_gate": a["L1_ffn_w_gate"],
        "moe_v": a["L1_ffn_value_experts"].transpose(2, 0, 1, 3).reshape(P, NE, EH * EK),
        "moe_o": a["L1_ffn_output_experts"].transpose(1, 2, 0, 3).reshape(PAIRS, P, NE, C).transpose(1, 0, 2, 3),
    }
    w = {n: np.ascontiguousarray(v) for n, v in w.items()}
    w["ident"] = np.eye(P, dtype=np.float32)
    ch = np.arange(P)
    same_head = ch[:, None] // D == ch[None, :] // D
    w["sum_d"] = np.stack([same_head & (ch[None, :] % D == e) for e in range(D)], 1).astype(np.float32)
    w["sum_dh"] = ((ch[:, None] // D == np.arange(H)[None]) * np.float32(D ** -0.5)).astype(np.float32)
    return w


def kernel(**inputs):
    import ml_dtypes
    import concourse.bacc as _bacc
    from concourse.bass_utils import run_bass_kernel_spmd as _run

    a = {n: np.asarray(v) for n, v in inputs.items()}
    w = layouts(a)
    bf = ml_dtypes.bfloat16
    w["ident_bf"] = np.eye(P, dtype=bf)
    i = np.arange(P)
    w["mask_rows"] = np.where(i[None, :] > i[:, None], MASKED, 0.0).astype(bf)
    w["mask_T"] = np.where(i[:, None] > i[None, :], MASKED, 0.0).astype(bf)
    part = np.arange(PARTS * EH)
    w["shift_sel"] = np.broadcast_to((part[:, None] % EH == np.arange(EH)[None])[:, :, None],
                                     (PARTS * EH, EH, P)).astype(bf)
    he = np.arange(EH * NE)
    pair, e, m = np.meshgrid(np.arange(PAIRS), np.arange(NE), np.arange(P), indexing="ij")
    w["spread"] = (he[:, None, None, None] == ((2 * pair + m // EK) * NE + e)[None]).astype(bf)
    w["rank"] = np.broadcast_to(NE - np.arange(NE, dtype=np.float32), (P, TILES * EH, NE))
    w = {n: np.ascontiguousarray(v) for n, v in w.items()}

    nc = _bacc.Bacc("TRN2", target_bir_lowering=False, num_devices=1)
    w["x"] = np.ascontiguousarray(a["L0_attn_x"])
    dram = {n: nc.dram_tensor("in_" + n, v.shape, mybir.dt.from_np(v.dtype), kind="ExternalInput").ap()
            for n, v in w.items()}
    out = nc.dram_tensor("out", (B, T, C), F32, kind="ExternalOutput").ap()
    build(nc, dram, out)
    r = _run(nc, [{"in_" + n: v for n, v in w.items()}], core_ids=[0])
    return r.results[0]["out"]
```

```python
from contextlib import ExitStack

import numpy as np

import concourse.bass as bass
from concourse import mybir

ALU = mybir.AluOpType
ACT = mybir.ActivationFunctionType
F32 = mybir.dt.float32
F32R = mybir.dt.float32r
BF16 = mybir.dt.bfloat16
U32 = mybir.dt.uint32
AX_X = mybir.AxisListType.X

P = 128
B, T, C = 16, 256, 128
TILES = T // P
LN_EPS = 1e-5

H, D = 16, 8
GLA_RANK = 16
GLA_NORM = 16.0
RMS_EPS = 1e-5
L2_FLOOR = 1e-24
ROOT_SCALE = 2.0 ** 18
LANES = P // 32
GROUPS = H // LANES
SPLIT = 4
EXP_SAFE = 80.0

EH, EK, NE = 8, 64, 8
PAIRS = EH // 2
BLOCKS = 3
MASKED = -1e30

FFN_TILES = 4
AHEAD = 4

LOG_EXP_SET = "natural_log_exp_and_others"


def wait(eng, sem, value):
    if not (isinstance(value, int) and value <= 0):
        eng.wait_ge(sem, value)


class Chain:

    def __init__(self, eng, sem):
        self.eng, self.sem, self.base, self.n = eng, sem, 0, 0

    def link(self, ins, static=False):
        self.n += 1
        ins.then_inc(self.sem, 1)
        self.eng.wait_ge(self.sem, self.base + self.n)
        if static is not False:
            self.eng.memset(static[:], 0.0)

    def start(self, base):
        self.base, self.n = base, 0



def of(i, n=1, per=1):
    return (i + 1) * per + n


def before(i, n=1, per=1):
    return i * per + n


def credit(eng, sem, per=1):
    for _ in range(per):
        eng.nop().then_inc(sem, 1)



def ln_stats(dve, chain, s, x_tiles, tiles):
    for t in range(tiles):
        ins = dve.bn_stats(s.stats[:, t, :], x_tiles(t))
    chain.link(ins, static=s.scratch)
    for t in range(tiles):
        ins = dve.bn_aggr(s.mean_var[:, t, :], s.stats[:, t, :])
    chain.link(ins)
    dve.tensor_scalar(s.var_eps[:, 0:tiles], s.mean_var[:, 0:tiles, 1], LN_EPS, None,
                      ALU.add).then_inc(s.var_ready, 1)


def ln_apply(dve, s, x_tiles, tiles, n):
    wait(dve, s.rstd_ready, n + 1)
    wait(dve, s.norm_used, n)
    for t in range(tiles):
        ins = dve.tensor_scalar(s.norm[:, t, :], x_tiles(t), s.mean_var[:, t, 0:1], s.rstd[:, t:t + 1],
                                ALU.subtract, ALU.mult)
    ins.then_inc(s.norm_ready, 1)


def ln_power(pool, s, tiles, n):
    wait(pool, s.var_ready, n + 1)
    wait(pool, s.norm_ready, n)
    pool.tensor_tensor(s.rstd[:, 0:tiles], s.var_eps[:, 0:tiles], s.minus_half[:, 0:tiles],
                       ALU.pow).then_inc(s.rstd_ready, 1)


def root_guess(act, chain, s, z, n):
    act.wait_ge(s.z_ready, of(n))
    chain.link(act.activation(s.guess[:], z[:], ACT.Ln))
    act.activation(s.guess[:], s.guess[:], ACT.Exp, scale=-0.5).then_inc(s.guess_ready, 1)


def refine_root(dve, chain, s, z, n):
    dve.wait_ge(s.guess_ready, of(n))
    chain.link(dve.tensor_tensor(s.rs[:], s.guess[:], z[:], ALU.mult))
    chain.link(dve.scalar_tensor_tensor(s.rs[:], s.rs[:], -0.5, s.guess[:], ALU.mult, ALU.mult))
    return dve.scalar_tensor_tensor(s.rs[:], s.rs[:], 1.5, s.guess[:], ALU.add, ALU.mult)


def ln_buffers(s, c, tiles):
    s.stats = c.sb("stats", [P, tiles, 6])
    s.mean_var = c.sb("mean_var", [P, tiles, 2])
    s.var_eps = c.sb("var_eps", [P, tiles])
    s.rstd = c.sb("rstd", [P, tiles])
    s.norm = c.sb("norm", [P, tiles, C])
    s.scratch = c.sb("scratch", [P, 1])
    s.var_ready, s.rstd_ready, s.norm_ready, s.norm_used = c.sems(
        "var_ready", "rstd_ready", "norm_ready", "norm_used")


class Stage:
    pass


class Ctx:

    def __init__(self, nc, k, phase, kind=None):
        self.nc, self.k, self.phase, self.kind, self.stack = nc, k, phase, kind or phase, ExitStack()

    def __enter__(self):
        self.stack.__enter__()
        return self

    def __exit__(self, *a):
        return self.stack.__exit__(*a)

    def sb(self, name, shape, dt=F32):
        return self.stack.enter_context(self.nc.sbuf_tensor(f"{self.phase}_{name}", shape, dt))

    def sem(self, name):
        kept = self.k.sems.setdefault(self.kind, {})
        if name not in kept:
            kept[name] = self.k.stack.enter_context(self.nc.semaphore(f"{self.kind}_{name}"))
        return kept[name]

    def sems(self, *names):
        return [self.sem(name) for name in names]


def forget(pool, k, kind):
    for sem in k.sems[kind].values():
        pool.sem_clear(sem)


EARLY_WEIGHTS = ("ffn_WT", "ffn_b", "lora_downT", "down_aux", "lora_upT", "up_auxT", "bqk", "bv", "gnorm", "temp",
                 "gla_bg", "ident")



def phase_load(nc, k, dram):
    with Ctx(nc, k, "load") as c, nc.Block() as block:
        loaded = c.sem("loaded")
        made = c.sem("made")
        lora1 = c.sem("lora1")
        lora1_sb = c.sem("lora1_sb")
        lora2 = c.sem("lora2")
        lora2_sb = c.sem("lora2_sb")
        lora3 = c.sem("lora3")
        bias_rows = c.sem("bias_rows")
        temp_rows = c.sem("temp_rows")
        act_step = c.sem("act_step")
        dve_step = c.sem("dve_step")
        w = k.w
        a1 = c.sb("a1", [4, C])
        a2 = c.sb("a2", [50, C])
        t1 = c.sb("t1", [P, H])
        t2 = c.sb("t2", [P, H])
        t3 = c.sb("t3", [P, H])
        x_loaded = c.sem("x_loaded")

        @block.sync
        def _(sp):
            for name in EARLY_WEIGHTS:
                sp.dma_start(w[name][:], dram[name]).then_inc(loaded, 16)
            sp.dma_start(k.x[:, 0:B * TILES, :], dram["x"].rearrange("b (t p) c -> p (b t) c", p=P)) \
              .then_inc(x_loaded, 16)
            sp.wait_ge(loaded, 16 * len(EARLY_WEIGHTS))
            sp.wait_ge(x_loaded, 16)

        @block.gpsimd
        def _(pool):
            pool.memset(k.minus_half[:], -0.5)
            pool.memset(k.x[:, B * TILES:, :], 0.0)
            pool.memset(k.vaug[:], 1.0)
            pool.memset(k.values[:], 1.0)
            pool.memset(k.ones_row[:], 1.0).then_inc(made, 1)

        @block.tensor
        def _(pe):
            pe.wait_ge(loaded, 16 * len(EARLY_WEIGHTS))
            pe.wait_ge(made, 1)
            pe.matmul(k.bank[0][0:4, 0:C], w["lora_downT"][:], w["down_aux"][:], start=True, stop=True).then_inc(lora1, 1)
            pe.matmul(k.bank[3][:, 0:2 * C], k.ones_row[:], w["bqk"][:], start=True, stop=True)
            pe.matmul(k.bank[4][:, 0:C], k.ones_row[:], w["bv"][:], start=True, stop=True)
            pe.matmul(k.bank[7][:, 0:C], k.ones_row[:], w["ffn_b"][:], start=True, stop=True)
            pe.matmul(k.bank[5][:, 0:C], k.ones_row[:], w["gnorm"][:], start=True, stop=True).then_inc(bias_rows, 1)
            pe.matmul(k.bank[6][:, 0:H], k.ones_row[:], w["temp"][:], start=True, stop=True).then_inc(temp_rows, 1)
            pe.wait_ge(lora1_sb, 1)
            pe.matmul(k.bank[1][0:50, 0:C], w["lora_upT"][:], a1[:], start=True, stop=True).then_inc(lora2, 1)
            pe.wait_ge(lora2_sb, 1)
            pe.matmul(k.bank[2][:, 0:C], a2[:], w["up_auxT"][:], start=True, stop=True).then_inc(lora3, 1)

        @block.vector
        def _(dve):
            chain = Chain(dve, dve_step)
            dve.wait_ge(lora1, 1)
            dve.tensor_copy(a1[:], k.bank[0][0:4, 0:C]).then_inc(lora1_sb, 1)
            dve.wait_ge(bias_rows, 1)
            for t in range(TILES):
                dve.tensor_copy(k.bqk_rows[:, t, :], k.bank[3][:, 0:2 * C])
                dve.tensor_copy(k.bv_rows[:, t, :], k.bank[4][:, 0:C])
                dve.tensor_copy(k.gnorm_rows[:, t, :], k.bank[5][:, 0:C])
            dve.wait_ge(lora2, 1)
            dve.tensor_copy(a2[:], k.bank[1][0:50, 0:C]).then_inc(lora2_sb, 1)
            dve.wait_ge(lora3, 1)
            chain.link(dve.tensor_tensor(k.w_ffn[:], k.bank[2][:, 0:C], w["ffn_WT"][:], ALU.add))
            dve.tensor_scalar(k.w_ffn[:], k.w_ffn[:], 0.5, None, ALU.mult)
            for t in range(FFN_TILES):
                dve.tensor_scalar(k.b_ffn[:, t, :], k.bank[7][:, 0:C], 0.5, None, ALU.mult)
            dve.tensor_scalar(k.minus_bg[:], w["gla_bg"][:], -1.0, None, ALU.mult)
            dve.wait_ge(act_step, 4)
            chain.link(dve.tensor_tensor(t3[:], t2[:], t1[:], ALU.add))
            dve.tensor_scalar(k.exp_shift[:], t3[:], EXP_SAFE, 0.0, ALU.subtract, ALU.max)
            for t in range(TILES):
                dve.memset(k.l2_scale[:, 1, t, :], ROOT_SCALE ** 0.5)
                ins = dve.tensor_scalar(k.l2_scale[:, 0, t, :], t3[:], ROOT_SCALE ** 0.5, None, ALU.mult)
            chain.link(ins)
            chain.link(dve.tensor_scalar(k.exp_shift[:], k.exp_shift[:], -1.0, None, ALU.mult))

        @block.scalar
        def _(act):
            act.wait_ge(temp_rows, 1)
            act.activation(t1[:], k.bank[6][:, 0:H], ACT.Relu).then_inc(act_step, 1)
            act.activation(t2[:], k.bank[6][:, 0:H], ACT.Abs).then_inc(act_step, 1)
            act.wait_ge(act_step, 2)
            act.activation(t2[:], t2[:], ACT.Exp, scale=-1.0).then_inc(act_step, 1)
            act.wait_ge(act_step, 3)
            act.activation(t2[:], t2[:], ACT.Ln, bias=1.0).then_inc(act_step, 1)



def phase_ffn(nc, k, name, late=None, split=None, split_whole=(), kind="ffn"):
    steps = B * TILES // FFN_TILES
    with Ctx(nc, k, name, kind) as c, nc.Block() as block:
        s = Stage()
        s.minus_half = k.minus_half
        ln_buffers(s, c, FFN_TILES)
        nT = c.sb("nT", [P, FFN_TILES, P])
        nT_ready, y_ready, x_done, biased = (c.sem(n) for n in ("nT_ready", "y_ready", "x_done", "biased"))
        dve_step = c.sem("dve_step")
        late_loaded = c.sem("late_loaded")
        high_made, whole_made = c.sems("high_made", "whole_made")
        turned, y = k.bank[0], k.bank[1]

        def x_at(step):
            return lambda t: k.x[:, bass.ds(step * FFN_TILES + t, 1), :].rearrange("p a c -> p (a c)")

        def x_step(i):
            return k.x[:, bass.ds(i * FFN_TILES, FFN_TILES), :].rearrange("p a c -> p (a c)")

        if split:
            assert split[0].shape[1] == steps

        def part(tensor, i):
            return tensor[:, bass.ds(i, 1), :].rearrange("p a c -> p (a c)")

        if late:
            @block.sync
            def _(sp):
                for weight, src in late.items():
                    sp.dma_start(k.w[weight][:], src).then_inc(late_loaded, 16)
                sp.wait_ge(late_loaded, 16 * len(late))

        @block.vector
        def _(dve):
            credit(dve, x_done)
            chain = Chain(dve, dve_step)
            ln_stats(dve, chain, s, x_at(0), FFN_TILES)
            ln_apply(dve, s, x_at(0), FFN_TILES, 0)
            ln_stats(dve, chain, s, x_at(1), FFN_TILES)
            first = chain.n
            with dve.Fori(0, steps) as i:
                chain.start(2 * i + first)
                ln_apply(dve, s, x_at(i + 1), FFN_TILES, i + 1)
                ln_stats(dve, chain, s, x_at(i + 2), FFN_TILES)
                dve.wait_ge(y_ready, of(i))
                dve.wait_ge(biased, of(i))
                dve.tensor_tensor(x_step(i), x_step(i), y[:, :], ALU.add).then_inc(x_done, 1)

        @block.gpsimd
        def _(pool):
            credit(pool, biased)
            ln_power(pool, s, FFN_TILES, 0)
            ln_power(pool, s, FFN_TILES, 1)
            for n, (weight, high, low) in enumerate(split_whole):
                pool.wait_ge(whole_made, n + 1)
                pool.tensor_tensor(low[:], weight[:], high[:].bitcast(F32), ALU.subtract)
            with pool.Fori(0, steps) as i:
                pool.wait_ge(s.norm_ready, i + 1)
                pool.tensor_tensor(x_step(i), x_step(i), k.b_ffn[:].rearrange("p a c -> p (a c)"), ALU.add).then_inc(biased, 1)
                ln_power(pool, s, FFN_TILES, i + 2)
                if split:
                    pool.wait_ge(high_made, i + 1)
                    pool.tensor_tensor(part(split[2], i), part(split[0], i), part(split[1], i).bitcast(F32), ALU.subtract)

        @block.tensor
        def _(pe):
            credit(pe, y_ready)

            def turn_norm(n):
                pe.wait_ge(s.norm_ready, n + 1)
                pe.wait_ge(nT_ready, before(n))
                for t in range(FFN_TILES):
                    ins = pe.transpose(turned[:, t * P:(t + 1) * P], s.norm[:, t, :], k.w["ident"][:])
                ins.then_inc(s.norm_used, 1)

            turn_norm(0)
            with pe.Fori(0, steps) as i:
                pe.wait_ge(nT_ready, of(i))
                pe.wait_ge(x_done, before(i))
                for t in range(FFN_TILES):
                    ins = pe.matmul(y[:, t * C:(t + 1) * C], nT[:, t, :], k.w_ffn[:], start=True, stop=True)
                ins.then_inc(y_ready, 1)
                turn_norm(i + 1)

        @block.scalar
        def _(act):
            credit(act, nT_ready)

            def norm_copy(n):
                act.wait_ge(s.norm_used, n + 1)
                act.wait_ge(y_ready, before(n))
                act.activation(nT[:].rearrange("p a c -> p (a c)"), turned[:, :], ACT.Copy).then_inc(nT_ready, 1)

            for weight, high, low in split_whole:
                act.activation(high[:], weight[:], ACT.Copy).then_inc(whole_made, 1)
            norm_copy(0)
            with act.Fori(0, steps) as i:
                norm_copy(i + 1)
                if split:
                    act.activation(part(split[1], i), part(split[0], i), ACT.Copy).then_inc(high_made, 1)



def outer_and_scan(dve, s, v_banks, v_bias, n):
    dve.wait_ge(s.qkT_ready, of(n))
    dve.wait_ge(s.prod_ready, before(n, 2, 2))
    for chunk in range(D // 2):
        dve.wait_ge(s.v_ready, of(n, chunk + 1, D // 2))
        for e in (2 * chunk, 2 * chunk + 1):
            v = v_banks[chunk % 2][:, (e % 2) * T:(e % 2 + 1) * T]
            if v_bias is None:
                ins = dve.tensor_tensor(s.kv[:, e, :], v, s.kT[:], ALU.mult)
            else:
                ins = dve.scalar_tensor_tensor(s.kv[:, e, :], v, v_bias[:, e:e + 1], s.kT[:], ALU.add, ALU.mult)
            ins.then_inc(s.kv_done, 1)
        if chunk == 0:
            dve.wait_ge(s.decay_ready, of(n))
        for e in (2 * chunk, 2 * chunk + 1):
            dve.wait_ge(s.kv_done, of(n, e + 1, D))
            dve.tensor_tensor_scan(s.M[:, e, :], s.decay[:], s.kv[:, e, :], 0.0, ALU.mult, ALU.add) \
               .then_inc(s.scan_done, 1)


def query_states(pool, s, n):
    half = D // 2
    pool.wait_ge(s.sum_ready, before(n))
    for j in range(2):
        pool.wait_ge(s.scan_done, of(n, half * (j + 1), D))
        e = slice(half * j, half * (j + 1))
        pool.tensor_tensor(s.prod[:, e, :], s.M[:, e, :], s.qT[:].unsqueeze(1).broadcast_to([P, half, T]),
                           ALU.mult).then_inc(s.prod_ready, 1)


def spread_values(pe, s, v_banks, w_v, n, chunk):
    if chunk >= 2:
        pe.wait_ge(s.kv_done, of(n, 2 * (chunk - 1), D))
    for e in (2 * chunk, 2 * chunk + 1):
        ins = pe.matmul(v_banks[chunk % 2][:, (e % 2) * T:(e % 2 + 1) * T], w_v[:, e, :], s.nT[:],
                        start=True, stop=True)
    ins.then_inc(s.v_ready, 1)


def recurrence_buffers(s, c):
    s.nT = c.sb("nT", [P, T])
    s.qT = c.sb("qT", [P, T])
    s.kT = c.sb("kT", [P, T])
    s.decay = c.sb("decay", [P, T])
    s.kv = c.sb("kv", [P, D, T])
    s.M = c.sb("M", [P, D, T])
    s.prod = c.sb("prod", [P, D, T])
    s.z_relu = c.sb("z_relu", [P, T])
    s.z_exp = c.sb("z_exp", [P, T])
    s.softplus = c.sb("softplus", [P, T])
    s.nT_ready, s.qkz_ready, s.qkT_ready, s.z_read, s.z_parts = c.sems(
        "nT_ready", "qkz_ready", "qkT_ready", "z_read", "z_parts")
    s.softplus_ready, s.decay_ready, s.v_ready, s.kv_done, s.scan_done = c.sems(
        "softplus_ready", "decay_ready", "v_ready", "kv_done", "scan_done")
    s.prod_ready, s.sum_ready, s.act_step, s.dve_step = c.sems(
        "prod_ready", "sum_ready", "act_step", "dve_step")


def x_tile(k, seq):
    return lambda t: k.x[:, bass.ds(seq * TILES + t, 1), :].rearrange("p a c -> p (a c)")


def x_seq(k, seq):
    return k.x[:, bass.ds(seq * TILES, TILES), :].rearrange("p a c -> p (a c)")



def phase_mixer(nc, k, name, kind="mixer"):
    w = k.w
    with Ctx(nc, k, name, kind) as c, nc.Block() as block:
        s = Stage()
        s.minus_half = k.minus_half
        ln_buffers(s, c, TILES)
        recurrence_buffers(s, c)
        s.hT = c.sb("hT", [P, T])
        s.qk = c.sb("qk", [P, 2, TILES, C])
        s.qk_sq = c.sb("qk_sq", [P, 2, TILES, C])
        s.v = c.sb("v", [P, TILES * H, D])
        s.ss = c.sb("ss", [P, 2 * TILES * H])
        s.guess = c.sb("guess", [P, 2 * TILES * H])
        s.rs = c.sb("rs", [P, 2 * TILES * H])
        s.parts = c.sb("parts", [P, 2, TILES * H, SPLIT, D], F32R)
        s.qp = c.sb("qp", [P, GROUPS, T], F32R)
        s.kp = c.sb("kp", [P, GROUPS, T], F32R)
        s.probs = c.sb("probs", [P, 2 * LANES, 2 * T])
        s.oT = c.sb("oT", [P, GROUPS, T])
        s.rden = c.sb("rden", [P, TILES, H, 1])
        s.on = c.sb("on", [P, TILES, C])
        s.onT = c.sb("onT", [P, T])
        s.hT_ready, s.qk_rows, s.v_rows, s.qk_sb, s.qk_sq_ready = c.sems(
            "hT_ready", "qk_rows", "v_rows", "qk_sb", "qk_sq_ready")
        s.z_ready, s.guess_ready, s.vaug_ready, s.parts_ready, s.q_turned = c.sems(
            "z_ready", "guess_ready", "vaug_ready", "parts_ready", "q_turned")
        s.k_turned, s.qp_ready, s.kp_ready, s.scores_ready, s.exp_done = c.sems(
            "k_turned", "qp_ready", "kp_ready", "scores_ready", "exp_done")
        s.pv_done, s.on_ready, s.on_turned, s.onT_ready, s.out_ready = c.sems(
            "pv_done", "on_ready", "on_turned", "onT_ready", "out_ready")
        s.x_done, s.normed, s.oT_ready, s.o_rows, s.q_high = c.sems(
            "x_done", "normed", "oT_ready", "o_rows", "q_high")
        s.v_read = c.sem("v_read")
        k_banks = [k.bank[2], k.bank[5]]
        score_bank, o_bank, misc, proj, v_banks = k.bank[0:3], k.bank[3], k.bank[4], k.bank[5], k.bank[6:8]
        sum_bank = [o_bank, misc]
        o_rows = [v_banks[t][:, :].rearrange("p (h e) -> p h e", h=H) for t in range(TILES)]

        @block.tensor
        def _(pe):
            for sem, per in ((s.v_ready, D // 2), (s.sum_ready, 1), (s.qkz_ready, 1), (s.qk_rows, 1), (s.v_rows, 1),
                             (s.q_turned, 1), (s.k_turned, 1), (s.scores_ready, H), (s.pv_done, GROUPS),
                             (s.o_rows, 1), (s.on_turned, 1), (s.out_ready, 1)):
                credit(pe, sem, per)

            def project(n):
                pe.wait_ge(s.norm_ready, n + 1)
                pe.wait_ge(s.nT_ready, before(n))
                for t in range(TILES):
                    ins = pe.transpose(misc[:, t * P:(t + 1) * P], s.norm[:, t, :], w["ident"][:])
                ins.then_inc(s.norm_used, 1)
                pe.wait_ge(s.nT_ready, of(n))
                pe.wait_ge(s.qk_sb, before(n))
                pe.matmul(proj[:, 0:T], w["mix_q"][:], s.nT[:], start=True, stop=True)
                pe.matmul(proj[:, T:2 * T], w["mix_k"][:], s.nT[:], start=True, stop=True)
                pe.matmul(score_bank[2][:, 0:T], w["mix_g"][:], s.nT[:], start=True, stop=True).then_inc(s.qkz_ready, 1)
                pe.wait_ge(s.v_read, before(n))
                for chunk in range(2):
                    spread_values(pe, s, v_banks, w["mix_v"], n, chunk)

            def spread_rest(n, chunk):
                spread_values(pe, s, v_banks, w["mix_v"], n, chunk)

            def sum_states(n, half):
                pe.wait_ge(s.prod_ready, of(n, half + 1, 2))
                if half == 0:
                    pe.wait_ge(s.kv_done, of(n, D, D))
                for e in range(half * D // 2, (half + 1) * D // 2):
                    ins = pe.matmul(v_banks[1][:, 0:T], w["sum_d"][:, e, :], s.prod[:, e, :], start=(e == 0), stop=(e == D - 1))
                if half == 1:
                    ins.then_inc(s.sum_ready, 1)

            def rows(n):
                for t in range(TILES):
                    ins = pe.matmul(v_banks[0][:, t * C:(t + 1) * C], s.nT[:, t * P:(t + 1) * P], w["v"][:], start=True, stop=True)
                ins.then_inc(s.v_rows, 1)
                pe.wait_ge(s.hT_ready, of(n))
                pe.wait_ge(s.kp_ready, before(n))
                for t in range(TILES):
                    ins = pe.matmul(proj[:, t * 2 * C:(t + 1) * 2 * C], s.hT[:, t * P:(t + 1) * P], w["qk"][:], start=True, stop=True)
                ins.then_inc(s.qk_rows, 1)

            def turn_qk(n):
                pe.wait_ge(s.parts_ready, of(n))
                pe.wait_ge(s.qkT_ready, of(n + 1))
                pe.wait_ge(s.z_read, of(n + 1))
                for banks, which, turned in ((score_bank, 0, s.q_turned), (k_banks, 1, s.k_turned)):
                    for g in range(GROUPS):
                        for t in range(TILES):
                            at, first = (g % 2) * T + t * P, t * H + LANES * g
                            ins = pe.transpose(banks[g // 2][:, at:at + P],
                                               s.parts[:, which, first:first + LANES].rearrange("p h s e -> p (h s e)").bitcast(F32),
                                               w["ident"][:])
                    ins.then_inc(turned, 1)

            def lane(j):
                return slice(32 * j, 32 * (j + 1))

            def scores(i, h):
                if h == 0:
                    pe.wait_ge(s.qp_ready, of(i))
                    pe.wait_ge(s.kp_ready, of(i))
                if h == 2:
                    pe.wait_ge(s.z_read, of(i + 2))
                if h >= 3:
                    pe.wait_ge(s.exp_done, of(i, h - 2, H))
                for kt in range(TILES):
                    ins = pe.matmul(score_bank[h % 3][:, kt * T:(kt + 1) * T], s.kp[lane(h % LANES), h // LANES, kt * P:(kt + 1) * P],
                                    s.qp[lane(h % LANES), h // LANES, :], start=True, stop=True)
                ins.then_inc(s.scores_ready, 1)

            def weigh(i, g):
                if g == 0:
                    pe.wait_ge(s.x_done, before(i))
                    pe.wait_ge(s.vaug_ready, of(i))
                if g >= 2:
                    pe.wait_ge(s.oT_ready, of(i, g - 1, GROUPS))
                pe.wait_ge(s.exp_done, of(i, LANES * (g + 1), H))
                for kt in range(TILES):
                    for j in range(LANES):
                        h = LANES * g + j
                        ins = pe.matmul(sum_bank[g % 2][lane(j), 0:T], k.vaug[:, kt, h, :],
                                        s.probs[:, h % (2 * LANES), kt * T:(kt + 1) * T],
                                        start=(kt == 0), stop=(kt == TILES - 1))
                ins.then_inc(s.pv_done, 1)

            def turn_back(i):
                pe.wait_ge(s.oT_ready, of(i, GROUPS, GROUPS))
                pe.wait_ge(s.hT_ready, of(i + 2))
                for t in range(TILES):
                    for g in range(GROUPS):
                        ins = pe.transpose(v_banks[t][:, g * P:(g + 1) * P], s.oT[:, g, t * P:(t + 1) * P], w["ident"][:])
                ins.then_inc(s.o_rows, 1)

            def turn_o(i):
                pe.wait_ge(s.on_ready, of(i))
                for t in range(TILES):
                    ins = pe.transpose(misc[:, T + t * P:T + (t + 1) * P], s.on[:, t, :], w["ident"][:])
                ins.then_inc(s.on_turned, 1)

            def output(i):
                pe.wait_ge(s.onT_ready, of(i))
                for t in range(TILES):
                    out = o_bank[:, t * C:(t + 1) * C]
                    pe.matmul(out, s.onT[:, t * P:(t + 1) * P], w["o"][:], start=True, stop=False)
                    ins = pe.matmul(out, k.ones_row[:], w["bo"][:], start=False, stop=True)
                ins.then_inc(s.out_ready, 1)

            sum_at = {11: 0, 15: 1}
            rest_at = {2: 2, 4: 3}
            lag = LANES + 1
            project(0)
            for chunk in range(2, D // 2):
                spread_rest(0, chunk)
            sum_states(0, 0)
            sum_states(0, 1)
            rows(0)
            project(1)
            for chunk in range(2, D // 2):
                spread_rest(1, chunk)
            sum_states(1, 0)
            sum_states(1, 1)
            turn_qk(0)
            with pe.Fori(0, B) as i:
                rows(i + 1)
                project(i + 2)
                for h in range(H + 2):
                    if h < H:
                        scores(i, h)
                    if h in rest_at:
                        spread_rest(i + 2, rest_at[h])
                    if h in sum_at:
                        sum_states(i + 2, sum_at[h])
                    if h >= lag and (h - lag) % LANES == 0:
                        weigh(i, (h - lag) // LANES)
                turn_back(i)
                turn_qk(i + 1)
                turn_o(i)
                output(i)

        @block.scalar
        def _(act):
            for sem, per in ((s.nT_ready, 1), (s.qkT_ready, 1), (s.z_read, 1), (s.z_parts, 1), (s.decay_ready, 1),
                             (s.exp_done, H), (s.hT_ready, 1), (s.onT_ready, 1), (s.qk_sq_ready, 1), (s.qp_ready, 1),
                             (s.guess_ready, 1), (s.oT_ready, GROUPS), (s.q_high, 1)):
                credit(act, sem, per)
            nc.scalar.preload_act_table_set(LOG_EXP_SET)
            chain = Chain(act, s.act_step)

            def norm_copy(n):
                act.wait_ge(s.norm_used, n + 1)
                act.activation(s.nT[:], misc[:, 0:T], ACT.Copy).then_inc(s.nT_ready, 1)

            def softplus_parts(n):
                act.wait_ge(s.qkz_ready, of(n))
                act.activation(s.z_relu[:], score_bank[2][:, 0:T], ACT.Relu, bias=w["mix_bg"][:])
                act.activation(s.z_exp[:], score_bank[2][:, 0:T], ACT.Abs, bias=w["mix_bg"][:]).then_inc(s.z_read, 1)
                act.wait_ge(s.z_read, of(n))
                chain.link(act.activation(s.z_exp[:], s.z_exp[:], ACT.Exp, scale=-1.0))
                act.activation(s.z_exp[:], s.z_exp[:], ACT.Ln, bias=1.0).then_inc(s.z_parts, 1)

            def qk_copies(n):
                act.activation(s.kT[:], proj[:, T:2 * T], ACT.Identity, bias=w["mix_bk"][:])
                act.activation(s.qT[:], proj[:, 0:T], ACT.Identity, bias=w["mix_bq"][:]).then_inc(s.qkT_ready, 1)

            def decay(n):
                act.wait_ge(s.softplus_ready, of(n))
                act.activation(s.decay[:], s.softplus[:], ACT.Exp, scale=-1.0).then_inc(s.decay_ready, 1)

            def front(n):
                norm_copy(n)
                softplus_parts(n)
                qk_copies(n)
                decay(n)

            def h_copy(n):
                act.wait_ge(s.sum_ready, of(n))
                act.activation(s.hT[:], v_banks[1][:, 0:T], ACT.Copy).then_inc(s.hT_ready, 1)

            def square(n):
                act.wait_ge(s.qk_sb, of(n))
                act.activation(s.qk_sq[:], s.qk[:], ACT.Square).then_inc(s.qk_sq_ready, 1)

            def q_high(n):
                act.wait_ge(s.normed, of(n))
                act.activation(s.parts[:, 0, :, 0:2, :], s.qk[:, 0].rearrange("p t (h e) -> p (t h) e", e=D).unsqueeze(2)
                               .broadcast_to([P, TILES * H, 2, D]), ACT.Copy).then_inc(s.q_high, 1)

            def q_copy(n):
                act.wait_ge(s.q_turned, of(n))
                for b in range(2):
                    ins = act.activation(s.qp[:, 2 * b:2 * b + 2, :].rearrange("p g t -> p (g t)"), score_bank[b][:, :], ACT.Copy)
                ins.then_inc(s.qp_ready, 1)

            def o_copy(i, g):
                act.wait_ge(s.pv_done, of(i, g + 1, GROUPS))
                act.activation(s.oT[:, g, :], sum_bank[g % 2][:, 0:T], ACT.Copy).then_inc(s.oT_ready, 1)

            front(0)
            h_copy(0)
            square(0)
            root_guess(act, chain, s, s.ss, 0)
            q_high(0)
            front(1)
            h_copy(1)
            q_copy(0)
            first = chain.n
            with act.Fori(0, B) as i:
                chain.start(2 * i + first)
                norm_copy(i + 2)
                square(i + 1)
                softplus_parts(i + 2)
                qk_copies(i + 2)
                for h in range(H):
                    act.wait_ge(s.scores_ready, of(i, h + 1, H))
                    if h % LANES == 0:
                        act.wait_ge(s.pv_done, of(i, h // LANES - 1, GROUPS))
                    act.activation(s.probs[:, h % (2 * LANES), :], score_bank[h % 3][:, :], ACT.Exp,
                                   bias=k.exp_shift[:, h:h + 1]).then_inc(s.exp_done, 1)
                    if h == 0:
                        decay(i + 2)
                        root_guess(act, chain, s, s.ss, i + 1)
                    if h == 11:
                        q_high(i + 1)
                    if h % LANES == LANES - 1 and h > LANES:
                        o_copy(i, h // LANES - 1)
                h_copy(i + 2)
                o_copy(i, GROUPS - 1)
                q_copy(i + 1)
                act.wait_ge(s.on_turned, of(i))
                act.activation(s.onT[:], misc[:, T:2 * T], ACT.Copy).then_inc(s.onT_ready, 1)
                assert chain.n == 2

        @block.gpsimd
        def _(pool):
            forget(pool, k, "ffn")
            for sem, per in ((s.softplus_ready, 1), (s.prod_ready, 2)):
                credit(pool, sem, per)

            def front(n):
                pool.wait_ge(s.z_parts, of(n))
                pool.tensor_tensor(s.softplus[:], s.z_relu[:], s.z_exp[:], ALU.add).then_inc(s.softplus_ready, 1)
                ln_power(pool, s, TILES, n + 1)
                query_states(pool, s, n)

            ln_power(pool, s, TILES, 0)
            front(0)
            front(1)
            with pool.Fori(0, B) as i:
                front(i + 2)

        @block.vector
        def _(dve):
            for sem, per in ((s.kv_done, D), (s.scan_done, D), (s.qk_sb, 1), (s.vaug_ready, 1), (s.z_ready, 1),
                             (s.normed, 1), (s.parts_ready, 1), (s.kp_ready, 1), (s.on_ready, 1), (s.x_done, 1),
                             (s.v_read, 1)):
                credit(dve, sem, per)
            chain = Chain(dve, s.dve_step)

            def norm_stats(n):
                ln_stats(dve, chain, s, x_tile(k, n), TILES)

            def norm_apply(n):
                ln_apply(dve, s, x_tile(k, n), TILES, n)

            def qk_rows(n):
                dve.wait_ge(s.qk_rows, of(n))
                dve.tensor_tensor(s.qk[:].rearrange("p w t c -> p t w c"), proj[:, :].rearrange("p (t w c) -> p t w c", w=2, c=C),
                                  k.bqk_rows[:].rearrange("p t (w c) -> p t w c", w=2), ALU.add).then_inc(s.qk_sb, 1)
                dve.wait_ge(s.v_rows, of(n))
                dve.tensor_tensor(s.v[:], v_banks[0][:, 0:TILES * C].rearrange("p (g e) -> p g e", e=D),
                                  k.bv_rows[:].rearrange("p t (h e) -> p (t h) e", e=D), ALU.add).then_inc(s.v_read, 1)
                dve.wait_ge(s.qk_sq_ready, of(n))
                chain.link(dve.tensor_reduce(s.ss[:], s.qk_sq[:].rearrange("p w t (h e) -> p (w t h) e", e=D), AX_X, ALU.add))
                dve.tensor_scalar(s.ss[:], s.ss[:], L2_FLOOR, ROOT_SCALE, ALU.max, ALU.mult).then_inc(s.z_ready, 1)

            def split_parts(n):
                heads = s.qk[:].rearrange("p w t (h e) -> p (w t h) e", e=D)
                chain.link(refine_root(dve, chain, s, s.ss, n))
                chain.link(dve.tensor_tensor(s.rs[:], s.rs[:], k.l2_scale[:].rearrange("p w t h -> p (w t h)"), ALU.mult))
                dve.tensor_tensor(heads, heads, s.rs[:].unsqueeze(2).broadcast_to([P, 2 * TILES * H, D]),
                                  ALU.mult).then_inc(s.normed, 1)
                half = [P, TILES * H, 2, D]
                q, kk = [s.qk[:, which].rearrange("p t (h e) -> p (t h) e", e=D).unsqueeze(2).broadcast_to(half)
                         for which in range(2)]
                dve.wait_ge(s.normed, of(n))
                chain.link(dve.tensor_copy(s.parts[:, 1, :, 0:SPLIT:2, :], kk))
                dve.tensor_tensor(s.parts[:, 1, :, 1:SPLIT:2, :], kk, s.parts[:, 1, :, 0:SPLIT:2, :].bitcast(F32), ALU.subtract)
                dve.wait_ge(s.q_high, of(n))
                dve.tensor_tensor(s.parts[:, 0, :, 2:SPLIT, :], q, s.parts[:, 0, :, 0:2, :].bitcast(F32),
                                  ALU.subtract).then_inc(s.parts_ready, 1)

            def v_copy(n):
                dve.wait_ge(s.v_read, of(n))
                dve.wait_ge(s.pv_done, before(n, GROUPS, GROUPS))
                dve.tensor_copy(k.vaug[:, :, :, 0:D].rearrange("p t h e -> p (t h) e"), s.v[:]).then_inc(s.vaug_ready, 1)

            def k_copy(n):
                dve.wait_ge(s.k_turned, of(n))
                for b in range(2):
                    ins = dve.tensor_copy(s.kp[:, 2 * b:2 * b + 2, :].rearrange("p g t -> p (g t)"), k_banks[b][:, :])
                ins.then_inc(s.kp_ready, 1)

            def weighted(i):
                dve.wait_ge(s.o_rows, of(i))
                for t in range(TILES):
                    ins = dve.reciprocal(s.rden[:, t], o_rows[t][:, :, D:D + 1])
                chain.link(ins)
                for t in range(TILES):
                    ins = dve.tensor_tensor(s.on[:, t, :].rearrange("p (h e) -> p h e", e=D), o_rows[t][:, :, 0:D],
                                            s.rden[:, t].broadcast_to([P, H, D]), ALU.mult)
                ins.then_inc(s.on_ready, 1)

            norm_stats(0)
            norm_apply(0)
            norm_stats(1)
            outer_and_scan(dve, s, v_banks, w["mix_bv"], 0)
            norm_apply(1)
            qk_rows(0)
            split_parts(0)
            norm_stats(2)
            outer_and_scan(dve, s, v_banks, w["mix_bv"], 1)
            norm_apply(2)
            v_copy(0)
            k_copy(0)
            first = chain.n
            with dve.Fori(0, B) as i:
                chain.start(9 * i + first)
                qk_rows(i + 1)
                norm_stats(i + 3)
                outer_and_scan(dve, s, v_banks, w["mix_bv"], i + 2)
                split_parts(i + 1)
                norm_apply(i + 3)
                weighted(i)
                v_copy(i + 1)
                k_copy(i + 1)
                dve.wait_ge(s.out_ready, of(i))
                dve.tensor_tensor(x_seq(k, i), x_seq(k, i), o_bank[:, 0:TILES * C], ALU.add).then_inc(s.x_done, 1)
                assert chain.n == 9, chain.n



def phase_moe(nc, k, name, kind="moe"):
    w = k.w
    CAUSAL = BLOCKS * P
    SEL = TILES * NE
    SPREADS = PAIRS * NE // 2
    ORDER = [(t, e) for e in range(NE) for t in range(TILES)]
    last_of = [max(j for j, (t, _) in enumerate(ORDER) if t == tile) for tile in range(TILES)]
    with Ctx(nc, k, name, kind) as c, nc.Block() as block:
        s = Stage()
        s.minus_half = k.minus_half
        ln_buffers(s, c, TILES)
        s.nT = c.sb("nT", [P, T])
        s.next_high = c.sb("next_high", [P, T], F32R)
        s.next_low = c.sb("next_low", [P, T], F32R)
        s.n_high = c.sb("n_high", [P, T], F32R)
        s.n_low = c.sb("n_low", [P, T], F32R)
        s.qT = c.sb("qT", [P, PAIRS, T])
        s.kT = c.sb("kT", [P, PAIRS, T])
        s.gates = c.sb("gates", [P, TILES * EH, NE])
        s.ranked = c.sb("ranked", [P, TILES * EH, NE])
        s.best = c.sb("best", [P, TILES * EH])
        s.top_gate = c.sb("top_gate", [P, TILES * EH])
        s.onehot = c.sb("onehot", [P, TILES, EH, NE])
        s.minus_max = c.sb("minus_max", [P, EH, TILES])
        s.sums = c.sb("sums", [P, TILES * EH])
        s.onehotT = c.sb("onehotT", [EH * NE, T], BF16)
        s.probs = c.sb("probs", [P, EH, CAUSAL])
        s.probsT = c.sb("probsT", [P, EH, CAUSAL])
        s.coef = c.sb("coef", [P, TILES * EH])
        s.oT = c.sb("oT", [P, PAIRS, T])
        s.picked = c.sb("picked", [P, 3, 2, T])
        s.taken = c.sb("taken", [P, SEL])
        s.nT_ready, s.q_psum, s.q_ready, s.k_psum, s.k_ready = c.sems(
            "nT_ready", "q_psum", "q_ready", "k_psum", "k_ready")
        s.logits_psum, s.gate_exp_ready, s.onehot_ready, s.rows_ready, s.max_done = c.sems(
            "logits_psum", "gate_exp_ready", "onehot_ready", "rows_ready", "max_done")
        s.onehot_turned, s.onehotT_ready, s.experts_ready, s.selected, s.gated = c.sems(
            "onehot_turned", "onehotT_ready", "experts_ready", "selected", "gated")
        s.gated_late, s.exp_done, s.coef_ready, s.scaled, s.probs_turned = c.sems(
            "gated_late", "exp_done", "coef_ready", "scaled", "probs_turned")
        s.probsT_ready, s.o_ready, s.oT_ready, s.spread_ready, s.picked_ready = c.sems(
            "probsT_ready", "o_ready", "oT_ready", "spread_ready", "picked_ready")
        s.picked_used, s.x_done, s.dve_step, s.high_ready, s.low_ready = c.sems(
            "picked_used", "x_done", "dve_step", "high_ready", "low_ready")
        s.scaled_first, s.next_low_ready = c.sems("scaled_first", "next_low_ready")
        two, experts, misc, acc_banks = k.bank[0:2], k.bank[2:4], k.bank[4], k.bank[5:7]
        acc = [acc_banks[t][:, 0:C] for t in range(TILES)]
        turned_banks = acc_banks
        logit_bank = acc_banks[1][:, T:T + TILES * EH * NE]
        row_banks = [*two, k.bank[7]]
        oT_banks = [k.bank[7], misc]

        @block.tensor
        def _(pe):
            for sem, per in ((s.q_psum, 2), (s.k_psum, 2), (s.logits_psum, 1), (s.rows_ready, EH), (s.onehot_turned, 1),
                             (s.experts_ready, SEL), (s.probs_turned, EH), (s.o_ready, 2),
                             (s.spread_ready, SPREADS), (s.picked_used, SPREADS)):
                credit(pe, sem, per)

            def turn_norm(n):
                pe.wait_ge(s.norm_ready, n + 1)
                pe.wait_ge(s.onehotT_ready, before(n))
                for t in range(TILES):
                    ins = pe.transpose(misc[:, t * P:(t + 1) * P], s.norm[:, t, :], w["ident"][:])
                ins.then_inc(s.norm_used, 1)

            def project(b, weight, ready):
                for p in (2 * b, 2 * b + 1):
                    out = experts[b][:, (p % 2) * T:(p % 2 + 1) * T]
                    high, low = (part[:, p * P:(p + 1) * P] for part in weight)
                    pe.matmul(out, high, s.next_high[:], start=True, stop=False)
                    pe.matmul(out, low, s.next_high[:], start=False, stop=False)
                    ins = pe.matmul(out, high, s.next_low[:], start=False, stop=True)
                ins.then_inc(ready, 1)

            def project_q(n):
                pe.wait_ge(s.next_low_ready, of(n))
                for b in range(2):
                    pe.wait_ge(s.selected, before(n, SEL - 1 + b, SEL))
                    project(b, k.query_parts, s.q_psum)

            def project_k(n, b):
                pe.wait_ge(s.q_ready, of(n, b + 1, 2))
                project(b, k.key_parts, s.k_psum)

            def logits(n):
                for t in range(TILES):
                    ins = pe.matmul(logit_bank[:, t * EH * NE:(t + 1) * EH * NE], s.nT[:, t * P:(t + 1) * P], w["moe_gate"][:],
                                    start=True, stop=True)
                ins.then_inc(s.logits_psum, 1)

            def head(tensor, h, at, size):
                return tensor[EK * (h % 2):EK * (h % 2 + 1), h // 2, at:at + size]

            def score_rows(i, h):
                if h == 0:
                    pe.wait_ge(s.q_ready, of(i, 2, 2))
                    pe.wait_ge(s.k_ready, of(i, 2, 2))
                if h >= len(row_banks):
                    pe.wait_ge(s.exp_done, of(i, h - len(row_banks) + 1, EH))
                b = row_banks[h % len(row_banks)]
                pe.matmul(b[:, 0:P], head(s.qT, h, 0, P), head(s.kT, h, 0, P), start=True, stop=False)
                pe.matmul(b[:, 0:P], w["ident_bf"][:], w["mask_rows"][:], start=False, stop=True)
                pe.matmul(b[:, P:CAUSAL], head(s.qT, h, P, P), head(s.kT, h, 0, T), start=True, stop=False, skip_group_check=True)
                pe.matmul(b[:, 2 * P:CAUSAL], w["ident_bf"][:], w["mask_rows"][:], start=False, stop=True,
                          skip_group_check=True).then_inc(s.rows_ready, 1)

            def expert_values(i, steps):
                for j in steps:
                    t, e = ORDER[j]
                    if j >= 2:
                        pe.wait_ge(s.selected, of(i, j - 1, SEL))
                    tokens = slice(t * P, (t + 1) * P)
                    out = experts[j % 2][:, :]
                    pe.matmul(out, s.n_high[:, tokens], k.experts_high[:, e, :], start=True, stop=False)
                    pe.matmul(out, s.n_high[:, tokens], k.experts_low[:, e, :], start=False, stop=False)
                    pe.matmul(out, s.n_low[:, tokens], k.experts_high[:, e, :], start=False, stop=True).then_inc(s.experts_ready, 1)

            def turn_onehot(i):
                for t in range(TILES):
                    ins = pe.transpose(misc[0:EH * NE, T + t * P:T + (t + 1) * P],
                                       s.onehot[:, t, :, :].rearrange("p h e -> p (h e)"), w["ident"][:])
                ins.then_inc(s.onehot_turned, 1)

            def turn_probs(i, h):
                if h == 0:
                    pe.wait_ge(s.x_done, before(i))
                if h >= 2:
                    pe.wait_ge(s.probsT_ready, of(i, h - 1, EH))
                pe.wait_ge(s.scaled, of(i, h + 1, EH))
                pe.wait_ge(s.scaled_first, of(i, h + 1, EH))
                for b in range(BLOCKS):
                    ins = pe.transpose(turned_banks[h % 2][:, b * P:(b + 1) * P], s.probs[:, h, b * P:(b + 1) * P], w["ident"][:])
                ins.then_inc(s.probs_turned, 1)

            def weigh(i):
                pe.wait_ge(s.gated, of(i))
                pe.wait_ge(s.gated_late, of(i))
                pe.wait_ge(s.probsT_ready, of(i, EH, EH))
                pe.wait_ge(s.onehotT_ready, of(i))
                for p in range(PAIRS):
                    at = (p % 2) * T
                    for kt in range(TILES):
                        for j in range(2):
                            h = 2 * p + j
                            ins = pe.matmul(oT_banks[p // 2][EK * j:EK * (j + 1), at + kt * P:at + T], k.values[:, kt, h, :],
                                            s.probsT[:, h, kt * T:kt * T + T - kt * P], start=(kt == 0), stop=(kt == TILES - 1),
                                            skip_group_check=True)
                    if p % 2 == 1:
                        ins.then_inc(s.o_ready, 1)

            def spread(i, g):
                if g >= 2:
                    pe.wait_ge(s.picked_ready, of(i, g - 1, SPREADS))
                p, e = g // (NE // 2), 2 * (g % (NE // 2))
                for j in range(2):
                    ins = pe.matmul(two[g % 2][:, j * T:(j + 1) * T], w["spread"][:, p, e + j, :], s.onehotT[:], start=True, stop=True)
                ins.then_inc(s.spread_ready, 1)

            def expert_outputs(i, g):
                pe.wait_ge(s.picked_ready, of(i, g + 1, SPREADS))
                p, e = g // (NE // 2), 2 * (g % (NE // 2))
                for j in range(2):
                    for t in range(TILES):
                        ins = pe.matmul(acc[t], s.picked[:, g % 3, j, t * P:(t + 1) * P], w["moe_o"][:, p, e + j, :],
                                        start=(g == 0 and j == 0), stop=(g == SPREADS - 1 and j == 1))
                ins.then_inc(s.picked_used, 1)

            turn_norm(0)
            project_q(0)
            project_k(0, 0)
            project_k(0, 1)
            logits(0)
            with pe.Fori(0, B) as i:
                pe.wait_ge(s.low_ready, of(i))
                pe.wait_ge(s.onehot_ready, of(i))
                for h in range(EH):
                    score_rows(i, h)
                    expert_values(i, [h])
                turn_onehot(i)
                for h in range(EH + 1):
                    if h < EH:
                        expert_values(i, [EH + h])
                    if h >= 1:
                        turn_probs(i, h - 1)
                    if h == EH - 4:
                        turn_norm(i + 1)
                project_q(i + 1)
                weigh(i)
                project_k(i + 1, 0)
                logits(i + 1)
                spread(i, 0)
                project_k(i + 1, 1)
                spread(i, 1)
                pe.wait_ge(s.gate_exp_ready, of(i + 1))
                for g in range(SPREADS):
                    if g + 2 < SPREADS:
                        spread(i, g + 2)
                    expert_outputs(i, g)

        @block.scalar
        def _(act):
            for sem, per in ((s.nT_ready, 1), (s.q_ready, 2), (s.k_ready, 2), (s.gate_exp_ready, 1), (s.onehotT_ready, 1),
                             (s.exp_done, EH), (s.scaled, EH), (s.probsT_ready, EH), (s.oT_ready, 2), (s.high_ready, 1)):
                credit(act, sem, per)

            def norm_copy(n):
                act.wait_ge(s.norm_used, n + 1)
                act.activation(s.nT[:], misc[:, 0:T], ACT.Copy)
                act.activation(s.next_high[:], misc[:, 0:T], ACT.Copy).then_inc(s.nT_ready, 1)

            def projected(n, b, psum, dst, ready, scale):
                act.wait_ge(psum, of(n, b + 1, 2))
                act.activation(dst[:, 2 * b:2 * b + 2, :].rearrange("p g t -> p (g t)"), experts[b][:, :], ACT.Copy,
                               scale=scale).then_inc(ready, 1)

            def q_copies(n):
                for b in range(2):
                    projected(n, b, s.q_psum, s.qT, s.q_ready, EK ** -0.5)

            def k_copy(n, b):
                projected(n, b, s.k_psum, s.kT, s.k_ready, 1.0)

            def gate_exp(n):
                act.wait_ge(s.logits_psum, of(n))
                act.activation(s.gates[:].rearrange("p r e -> p (r e)"), logit_bank, ACT.Exp,
                               scale=-1.0).then_inc(s.gate_exp_ready, 1)

            norm_copy(0)
            q_copies(0)
            k_copy(0, 0)
            k_copy(0, 1)
            gate_exp(0)
            with act.Fori(0, B) as i:
                act.wait_ge(s.nT_ready, of(i))
                act.activation(s.n_high[:], s.nT[:], ACT.Copy).then_inc(s.high_ready, 1)
                for h in range(EH):
                    act.wait_ge(s.max_done, of(i, h + 1, EH))
                    for t in range(TILES):
                        at = slice(t * P, t * T + P)
                        ins = act.activation(s.probs[:, h, at], row_banks[h % len(row_banks)][:, at], ACT.Exp,
                                             bias=s.minus_max[:, h, t:t + 1], accum_out=s.sums[:, t * EH + h:t * EH + h + 1])
                    ins.then_inc(s.exp_done, 1)
                act.wait_ge(s.onehot_turned, of(i))
                act.activation(s.onehotT[:], misc[0:EH * NE, T:2 * T], ACT.Copy).then_inc(s.onehotT_ready, 1)
                act.wait_ge(s.coef_ready, of(i))
                for h in range(EH + 2):
                    if h < EH:
                        act.activation(s.probs[:, h, P:CAUSAL], s.probs[:, h, P:CAUSAL], ACT.Copy,
                                       scale=s.coef[:, EH + h:EH + h + 1]).then_inc(s.scaled, 1)
                    if h >= 2:
                        act.wait_ge(s.probs_turned, of(i, h - 1, EH))
                        act.activation(s.probsT[:, h - 2, :], turned_banks[h % 2][:, 0:CAUSAL], ACT.Copy).then_inc(s.probsT_ready, 1)
                    if h == EH - 3:
                        norm_copy(i + 1)
                q_copies(i + 1)
                for b in range(2):
                    act.wait_ge(s.o_ready, of(i, b + 1, 2))
                    act.activation(s.oT[:, 2 * b:2 * b + 2, :].rearrange("p g t -> p (g t)"), oT_banks[b][:, :], ACT.Copy).then_inc(s.oT_ready, 1)
                k_copy(i + 1, 0)
                gate_exp(i + 1)
                k_copy(i + 1, 1)

        def gate_values(eng, t, gated):
            eng.tensor_tensor(k.values[:, t, :, :], k.values[:, t, :, :],
                              s.top_gate[:, t * EH:(t + 1) * EH].unsqueeze(2).broadcast_to([P, EH, EK]),
                              ALU.mult).then_inc(gated, 1)

        @block.gpsimd
        def _(pool):
            credit(pool, s.gated)
            credit(pool, s.low_ready)
            credit(pool, s.next_low_ready)

            def low_part(n):
                pool.wait_ge(s.nT_ready, of(n))
                pool.tensor_tensor(s.next_low[:], s.nT[:], s.next_high[:].bitcast(F32), ALU.subtract).then_inc(s.next_low_ready, 1)

            credit(pool, s.scaled_first, EH)

            ln_power(pool, s, TILES, 0)
            low_part(0)
            with pool.Fori(0, B) as i:
                pool.wait_ge(s.high_ready, of(i))
                pool.tensor_tensor(s.n_low[:], s.nT[:], s.n_high[:].bitcast(F32), ALU.subtract).then_inc(s.low_ready, 1)
                ln_power(pool, s, TILES, i + 1)
                pool.wait_ge(s.coef_ready, of(i))
                for h in range(EH):
                    pool.tensor_tensor(s.probs[:, h, 0:P], s.probs[:, h, 0:P], s.coef[:, h:h + 1].broadcast_to([P, P]),
                                       ALU.mult).then_inc(s.scaled_first, 1)
                low_part(i + 1)
                pool.wait_ge(s.selected, of(i, last_of[0] + 1, SEL))
                gate_values(pool, 0, s.gated)

        @block.vector
        def _(dve):
            for sem, per in ((s.max_done, EH), (s.gated_late, 1), (s.coef_ready, 1), (s.selected, SEL), (s.picked_ready, SPREADS),
                             (s.x_done, 1), (s.onehot_ready, 1)):
                credit(dve, sem, per)
            chain = Chain(dve, s.dve_step)

            wide = [P, TILES * EH, NE]

            def sigmoid(n):
                dve.wait_ge(s.gate_exp_ready, of(n))
                chain.link(dve.tensor_scalar(s.gates[:], s.gates[:], 1.0, None, ALU.add))
                chain.link(dve.reciprocal(s.gates[:], s.gates[:]))

            def top(n):
                chain.link(dve.tensor_reduce(s.top_gate[:], s.gates[:], AX_X, ALU.max))
                chain.link(dve.tensor_tensor(s.ranked[:], s.gates[:], s.top_gate[:].unsqueeze(2).broadcast_to(wide), ALU.is_equal))
                chain.link(dve.tensor_tensor(s.ranked[:], s.ranked[:], w["rank"][:], ALU.mult))

            def first_top(n):
                chain.link(dve.tensor_reduce(s.best[:], s.ranked[:], AX_X, ALU.max))
                dve.tensor_tensor(s.onehot[:].rearrange("p t h e -> p (t h) e"), w["rank"][:],
                                  s.best[:].unsqueeze(2).broadcast_to(wide), ALU.is_equal).then_inc(s.onehot_ready, 1)

            def select(i, steps):
                for j in steps:
                    t, e = ORDER[j]
                    dve.wait_ge(s.experts_ready, of(i, j + 1, SEL))
                    if j >= TILES:
                        dve.wait_ge(s.selected, of(i, j - TILES + 1, SEL))
                    dve.memset(s.taken[:, j:j + 1], 0.0)
                    dve.copy_predicated(k.values[:, t, :, :],
                                        s.onehot[:, t, :, e:e + 1].bitcast(U32).broadcast_to([P, EH, EK]),
                                        experts[j % 2][:, :].rearrange("p (h e) -> p h e", e=EK)).then_inc(s.selected, 1)

            ln_stats(dve, chain, s, x_tile(k, 0), TILES)
            ln_apply(dve, s, x_tile(k, 0), TILES, 0)
            for step in (sigmoid, top, first_top):
                step(0)
            first = chain.n
            with dve.Fori(0, B) as i:
                chain.start(9 * i + first)
                dve.wait_ge(s.onehot_ready, of(i))
                for h in range(EH):
                    dve.wait_ge(s.rows_ready, of(i, h + 1, EH))
                    for t in range(TILES):
                        ins = dve.tensor_reduce(s.minus_max[:, h, t:t + 1], row_banks[h % len(row_banks)][:, t * P:t * T + P], AX_X,
                                                ALU.max, negate=True)
                    ins.then_inc(s.max_done, 1)
                    select(i, [h])
                    if h == 1:
                        ln_stats(dve, chain, s, x_tile(k, i + 1), TILES)
                dve.wait_ge(s.exp_done, of(i, EH, EH))
                chain.link(dve.reciprocal(s.coef[:], s.sums[:]))
                dve.tensor_tensor(s.coef[:], s.coef[:], s.top_gate[:], ALU.mult).then_inc(s.coef_ready, 1)
                select(i, range(EH, EH + 3))
                ln_apply(dve, s, x_tile(k, i + 1), TILES, i + 1)
                select(i, range(EH + 3, SEL))
                dve.wait_ge(s.selected, of(i, SEL, SEL))
                gate_values(dve, TILES - 1, s.gated_late)
                between = {SPREADS // 4: sigmoid, SPREADS // 2: top, 3 * SPREADS // 4: first_top}
                for g in range(SPREADS):
                    if g % (SPREADS // 2) == 0:
                        dve.wait_ge(s.oT_ready, of(i, g // (SPREADS // 2) + 1, 2))
                    dve.wait_ge(s.spread_ready, of(i, g + 1, SPREADS))
                    dve.wait_ge(s.picked_used, of(i, g - 2, SPREADS))
                    dve.tensor_tensor(s.picked[:, g % 3], two[g % 2][:, :].rearrange("p (j t) -> p j t", t=T),
                                      s.oT[:, g // (NE // 2), :].unsqueeze(1).broadcast_to([P, 2, T]), ALU.mult).then_inc(s.picked_ready, 1)
                    if g in between:
                        between[g](i + 1)
                dve.wait_ge(s.picked_used, of(i, SPREADS, SPREADS))
                for t in range(TILES):
                    ins = dve.scalar_tensor_tensor(x_tile(k, i)(t), acc[t], 0.5, x_tile(k, i)(t), ALU.mult, ALU.add)
                ins.then_inc(s.x_done, 1)
                assert chain.n == 9, chain.n



def phase_gla(nc, k, name, kind="gla"):
    w = k.w
    with Ctx(nc, k, name, kind) as c, nc.Block() as block:
        s = Stage()
        s.minus_half = k.minus_half
        ln_buffers(s, c, TILES)
        recurrence_buffers(s, c)
        s.low = c.sb("low", [GLA_RANK, T])
        s.gate_exp = c.sb("gate_exp", [P, TILES * C])
        s.gate = c.sb("gate", [P, TILES * C])
        s.oT = c.sb("oT", [P, T])
        s.o_sq = c.sb("o_sq", [P, TILES * C])
        s.ms = c.sb("ms", [P, TILES * H])
        s.guess = c.sb("guess", [P, TILES * H])
        s.rs = c.sb("rs", [P, TILES * H])
        s.on = c.sb("on", [P, TILES, C])
        s.gated = c.sb("gated", [P, TILES, C])
        s.onT = c.sb("onT", [P, T])
        s.low_psum, s.low_ready, s.gate_psum, s.gate_exp_ready, s.gate_ready = c.sems(
            "low_psum", "low_ready", "gate_psum", "gate_exp_ready", "gate_ready")
        s.o_sq_ready, s.z_ready, s.guess_ready, s.on_ready, s.gated_ready = c.sems(
            "o_sq_ready", "z_ready", "guess_ready", "on_ready", "gated_ready")
        s.on_turned, s.onT_ready, s.out_ready, s.x_done, s.oT_ready = c.sems(
            "on_turned", "onT_ready", "out_ready", "x_done", "oT_ready")
        s.o_rows = c.sem("o_rows")
        o_bank, out_bank, gate_bank, z_bank, misc, proj, v_banks = *k.bank[0:6], k.bank[6:8]
        o_heads = o_bank[:, 0:TILES * C].rearrange("p (g e) -> p g e", e=D)

        @block.tensor
        def _(pe):
            for sem, per in ((s.v_ready, D // 2), (s.sum_ready, 1), (s.qkz_ready, 1), (s.low_psum, 1),
                             (s.gate_psum, 1), (s.on_turned, 1), (s.out_ready, 1), (s.o_rows, 1)):
                credit(pe, sem, per)

            def turn_norm(n):
                pe.wait_ge(s.norm_ready, n + 1)
                pe.wait_ge(s.nT_ready, before(n))
                for t in range(TILES):
                    ins = pe.transpose(misc[:, t * P:(t + 1) * P], s.norm[:, t, :], w["ident"][:])
                ins.then_inc(s.norm_used, 1)

            def project(n):
                pe.wait_ge(s.nT_ready, of(n))
                pe.wait_ge(s.qkT_ready, before(n))
                pe.wait_ge(s.z_read, before(n))
                pe.matmul(z_bank[0:GLA_RANK, 0:T], w["gla_g1"][:], s.nT[:], start=True, stop=True).then_inc(s.low_psum, 1)
                pe.matmul(proj[:, 0:T], w["gla_q"][:], s.nT[:], start=True, stop=True)
                pe.matmul(proj[:, T:2 * T], w["gla_k"][:], s.nT[:], start=True, stop=True)
                pe.wait_ge(s.low_ready, of(n))
                pe.matmul(z_bank[:, T:2 * T], w["gla_g2"][:], s.low[:], start=True, stop=True).then_inc(s.qkz_ready, 1)
                pe.wait_ge(s.kv_done, before(n, D, D))
                for chunk in range(2):
                    spread_values(pe, s, v_banks, w["gla_v"], n, chunk)

            def project_gate(n):
                pe.wait_ge(s.gate_ready, before(n))
                for t in range(TILES):
                    ins = pe.matmul(gate_bank[:, t * C:(t + 1) * C], s.nT[:, t * P:(t + 1) * P], w["gla_gate"][:], start=True, stop=True)
                ins.then_inc(s.gate_psum, 1)

            def spread_rest(n):
                for chunk in range(2, D // 2):
                    spread_values(pe, s, v_banks, w["gla_v"], n, chunk)

            def sum_states(n):
                pe.wait_ge(s.on_ready, before(n))
                pe.wait_ge(s.prod_ready, of(n, 2, 2))
                for e in range(D):
                    ins = pe.matmul(o_bank[:, T:2 * T], w["sum_d"][:, e, :], s.prod[:, e, :], start=(e == 0), stop=(e == D - 1))
                ins.then_inc(s.sum_ready, 1)

            def turn_rows(n):
                pe.wait_ge(s.oT_ready, of(n))
                for t in range(TILES):
                    ins = pe.transpose(o_bank[:, t * C:(t + 1) * C], s.oT[:, t * P:(t + 1) * P], w["ident"][:])
                ins.then_inc(s.o_rows, 1)

            def output(i):
                pe.wait_ge(s.gated_ready, of(i))
                for t in range(TILES):
                    ins = pe.transpose(misc[:, T + t * P:T + (t + 1) * P], s.gated[:, t, :], w["ident"][:])
                ins.then_inc(s.on_turned, 1)
                pe.wait_ge(s.onT_ready, of(i))
                pe.wait_ge(s.x_done, before(i))
                for t in range(TILES):
                    ins = pe.matmul(out_bank[:, t * C:(t + 1) * C], s.onT[:, t * P:(t + 1) * P], w["gla_o"][:], start=True, stop=True)
                ins.then_inc(s.out_ready, 1)

            turn_norm(0)
            project(0)
            spread_rest(0)
            project_gate(0)
            turn_norm(1)
            project(1)
            with pe.Fori(0, B) as i:
                sum_states(i)
                spread_rest(i + 1)
                project_gate(i + 1)
                turn_rows(i)
                turn_norm(i + 2)
                project(i + 2)
                output(i)

        @block.scalar
        def _(act):
            for sem, per in ((s.nT_ready, 1), (s.qkT_ready, 1), (s.z_read, 1), (s.z_parts, 1), (s.decay_ready, 1),
                             (s.low_ready, 1), (s.gate_exp_ready, 1), (s.o_sq_ready, 1), (s.onT_ready, 1),
                             (s.guess_ready, 1), (s.oT_ready, 1)):
                credit(act, sem, per)
            nc.scalar.preload_act_table_set(LOG_EXP_SET)
            chain = Chain(act, s.act_step)

            def norm_copy(n):
                act.wait_ge(s.norm_used, n + 1)
                act.activation(s.nT[:], misc[:, 0:T], ACT.Copy).then_inc(s.nT_ready, 1)

            def low_copy(n):
                act.wait_ge(s.low_psum, of(n))
                act.activation(s.low[:], z_bank[0:GLA_RANK, 0:T], ACT.Copy).then_inc(s.low_ready, 1)

            def project(n):
                act.wait_ge(s.qkz_ready, of(n))
                act.activation(s.z_relu[:], z_bank[:, T:2 * T], ACT.Relu, bias=k.minus_bg[:], scale=-1.0)
                act.activation(s.z_exp[:], z_bank[:, T:2 * T], ACT.Abs, bias=w["gla_bg"][:]).then_inc(s.z_read, 1)
                act.wait_ge(s.z_read, of(n))
                chain.link(act.activation(s.z_exp[:], s.z_exp[:], ACT.Exp, scale=-1.0))
                act.activation(s.z_exp[:], s.z_exp[:], ACT.Ln, bias=1.0).then_inc(s.z_parts, 1)
                act.wait_ge(s.kv_done, before(n, D, D))
                act.activation(s.kT[:], proj[:, T:2 * T], ACT.Copy)

            def q_and_decay(n):
                act.wait_ge(s.prod_ready, before(n, 2, 2))
                act.activation(s.qT[:], proj[:, 0:T], ACT.Copy).then_inc(s.qkT_ready, 1)
                act.wait_ge(s.softplus_ready, of(n))
                act.activation(s.decay[:], s.softplus[:], ACT.Exp, scale=-1.0 / GLA_NORM).then_inc(s.decay_ready, 1)

            def gate_exp(n):
                act.wait_ge(s.gate_psum, of(n))
                act.activation(s.gate_exp[:], gate_bank[:, 0:TILES * C], ACT.Exp, scale=-1.0).then_inc(s.gate_exp_ready, 1)

            norm_copy(0)
            low_copy(0)
            project(0)
            q_and_decay(0)
            gate_exp(0)
            norm_copy(1)
            low_copy(1)
            project(1)
            q_and_decay(1)
            first = chain.n
            with act.Fori(0, B) as i:
                chain.start(2 * i + first)
                act.wait_ge(s.sum_ready, of(i))
                act.activation(s.oT[:], o_bank[:, T:2 * T], ACT.Copy, scale=D ** -0.5).then_inc(s.oT_ready, 1)
                act.wait_ge(s.o_rows, of(i))
                act.activation(s.o_sq[:], o_bank[:, 0:TILES * C], ACT.Square).then_inc(s.o_sq_ready, 1)
                root_guess(act, chain, s, s.ms, i)
                gate_exp(i + 1)
                norm_copy(i + 2)
                low_copy(i + 2)
                project(i + 2)
                act.wait_ge(s.on_turned, of(i))
                act.activation(s.onT[:], misc[:, T:2 * T], ACT.Copy).then_inc(s.onT_ready, 1)
                q_and_decay(i + 2)
                assert chain.n == 2

        @block.gpsimd
        def _(pool):
            forget(pool, k, "moe")
            for sem, per in ((s.softplus_ready, 1), (s.prod_ready, 2), (s.gated_ready, 1)):
                credit(pool, sem, per)

            def softplus(n):
                pool.wait_ge(s.z_parts, of(n))
                pool.tensor_tensor(s.softplus[:], s.z_relu[:], s.z_exp[:], ALU.add).then_inc(s.softplus_ready, 1)

            ln_power(pool, s, TILES, 0)
            softplus(0)
            query_states(pool, s, 0)
            ln_power(pool, s, TILES, 1)
            softplus(1)
            with pool.Fori(0, B) as i:
                ln_power(pool, s, TILES, i + 2)
                query_states(pool, s, i + 1)
                pool.wait_ge(s.on_ready, of(i))
                pool.wait_ge(s.gate_ready, of(i))
                pool.tensor_tensor(s.gated[:].rearrange("p t c -> p (t c)"), s.on[:].rearrange("p t c -> p (t c)"), s.gate[:],
                                   ALU.mult).then_inc(s.gated_ready, 1)
                softplus(i + 2)

        @block.vector
        def _(dve):
            for sem, per in ((s.kv_done, D), (s.scan_done, D), (s.gate_ready, 1), (s.z_ready, 1), (s.on_ready, 1),
                             (s.x_done, 1)):
                credit(dve, sem, per)
            chain = Chain(dve, s.dve_step)

            def norm_stats(n):
                ln_stats(dve, chain, s, x_tile(k, n), TILES)

            def norm_apply(n):
                ln_apply(dve, s, x_tile(k, n), TILES, n)

            def make_gate(n):
                dve.wait_ge(s.gate_exp_ready, of(n))
                chain.link(dve.tensor_scalar(s.gate_exp[:], s.gate_exp[:], 1.0, None, ALU.add))
                chain.link(dve.reciprocal(s.gate_exp[:], s.gate_exp[:]))
                dve.wait_ge(s.gated_ready, before(n))
                chain.link(dve.tensor_tensor(s.gate[:], gate_bank[:, 0:TILES * C], s.gate_exp[:], ALU.mult))
                dve.tensor_tensor(s.gate[:], s.gate[:], k.gnorm_rows[:].rearrange("p t c -> p (t c)"), ALU.mult).then_inc(s.gate_ready, 1)

            norm_stats(0)
            norm_apply(0)
            outer_and_scan(dve, s, v_banks, None, 0)
            norm_stats(1)
            norm_apply(1)
            make_gate(0)
            first = chain.n
            with dve.Fori(0, B) as i:
                chain.start(9 * i + first)
                norm_stats(i + 2)
                norm_apply(i + 2)
                outer_and_scan(dve, s, v_banks, None, i + 1)
                dve.wait_ge(s.o_sq_ready, of(i))
                chain.link(dve.tensor_reduce(s.ms[:], s.o_sq[:].rearrange("p (g e) -> p g e", e=D), AX_X, ALU.add))
                dve.tensor_scalar(s.ms[:], s.ms[:], 1.0 / D, RMS_EPS, ALU.mult, ALU.add).then_inc(s.z_ready, 1)
                chain.link(refine_root(dve, chain, s, s.ms, i))
                dve.tensor_tensor(s.on[:].rearrange("p t (h e) -> p (t h) e", e=D), o_heads,
                                  s.rs[:].unsqueeze(2).broadcast_to([P, TILES * H, D]), ALU.mult).then_inc(s.on_ready, 1)
                make_gate(i + 1)
                dve.wait_ge(s.out_ready, of(i))
                dve.tensor_tensor(x_seq(k, i), x_seq(k, i), out_bank[:, 0:TILES * C], ALU.add).then_inc(s.x_done, 1)
                assert chain.n == 9, chain.n



def phase_store(nc, k, out):
    with Ctx(nc, k, "store") as c, nc.Block() as block:
        stored = c.sem("stored")

        @block.sync
        def _(sp):
            sp.dma_start(out.rearrange("b (t p) c -> p (b t) c", p=P), k.x[:, 0:B * TILES, :]).then_inc(stored, 16)
            sp.wait_ge(stored, 16)


def build(nc, dram, out):
    k = Stage()
    k.sems, k.stack = {}, ExitStack()
    with k.stack, Ctx(nc, k, "all") as c:
        k.bank = [c.stack.enter_context(nc.psum_tensor(f"bank{i}", [P, 512], F32)) for i in range(8)]
        k.x = c.sb("x", [P, B * TILES + AHEAD * TILES, C])
        k.w = {n: c.sb("w_" + n, list(a.shape), a.dtype) for n, a in dram.items() if n != "x"}
        k.minus_half = c.sb("minus_half", [P, 64])
        k.ones_row = c.sb("ones_row", [1, P])
        k.w_ffn = c.sb("w_ffn", [P, C])
        k.b_ffn = c.sb("b_ffn", [P, FFN_TILES, C])
        k.bqk_rows = c.sb("bqk_rows", [P, TILES, 2 * C])
        k.bv_rows = c.sb("bv_rows", [P, TILES, C])
        k.gnorm_rows = c.sb("gnorm_rows", [P, TILES, C])
        k.l2_scale = c.sb("l2_scale", [P, 2, TILES, H])
        k.exp_shift = c.sb("exp_shift", [P, H])
        k.minus_bg = c.sb("minus_bg", [P, 1])
        k.vaug = c.sb("vaug", [P, TILES, H, 32])
        k.values = c.sb("values", [P, TILES, EH, EK])
        phase_load(nc, k, dram)
        phase_ffn(nc, k, "ffn_a", late={n: a for n, a in dram.items() if n != "x" and n not in EARLY_WEIGHTS})
        phase_mixer(nc, k, "mixer")
        k.experts_high = c.sb("experts_high", [P, NE, EH * EK], F32R)
        k.experts_low = c.sb("experts_low", [P, NE, EH * EK], F32R)
        k.query_parts, k.key_parts = ([c.sb(f"{n}_{part}", [P, EH * EK], F32R) for part in ("high", "low")]
                                      for n in ("query", "key"))
        phase_ffn(nc, k, "ffn_b", split=(k.w["moe_v"], k.experts_high, k.experts_low),
                  split_whole=((k.w["moe_q"], *k.query_parts), (k.w["moe_k"], *k.key_parts)))
        phase_moe(nc, k, "moe_a")
        phase_gla(nc, k, "gla")
        phase_moe(nc, k, "moe_b")
        phase_store(nc, k, out)


def layouts(a):
    def recur_v(w):
        return np.repeat(w.reshape(C, H, D).transpose(0, 2, 1), D, axis=2)

    w = {
        "ffn_WT": a["L0_ffn_W"].T, "ffn_b": a["L0_ffn_b"][None],
        "lora_downT": a["L0_ffn_lora_down"].T, "down_aux": a["L0_ffn_down_aux"],
        "lora_upT": a["L0_ffn_lora_up"].T, "up_auxT": a["L0_ffn_up_aux"].T,
        "mix_q": a["L0_attn_Wsq"].T, "mix_k": a["L0_attn_Wsk"].T,
        "mix_bq": a["L0_attn_bsq"][:, None], "mix_bk": a["L0_attn_bsk"][:, None],
        "mix_g": np.repeat(a["L0_attn_Wg"].T, D, axis=1), "mix_bg": np.repeat(a["L0_attn_bg"], D)[:, None],
        "mix_v": recur_v(a["L0_attn_Wsv"].T),
        "mix_bv": np.repeat(a["L0_attn_bsv"].reshape(H, D), D, axis=0),
        "qk": np.concatenate([a["L0_attn_Wq"].T, a["L0_attn_Wk"].T], axis=1),
        "bqk": np.concatenate([a["L0_attn_bq"], a["L0_attn_bk"]])[None],
        "v": a["L0_attn_Wv"].T, "bv": a["L0_attn_bv"][None],
        "o": a["L0_attn_Wo"].T, "bo": a["L0_attn_bo"][None],
        "temp": a["L0_attn_temp"].reshape(1, H),
        "gla_q": a["L1_attn_Wq"], "gla_k": a["L1_attn_Wk"], "gla_v": recur_v(a["L1_attn_Wv"]),
        "gla_g1": a["L1_attn_Wg1"], "gla_g2": a["L1_attn_Wg2"], "gla_bg": a["L1_attn_bg2"][:, None],
        "gla_gate": a["L1_attn_Wg"], "gnorm": np.tile(a["L1_attn_g_norm_w"], H)[None], "gla_o": a["L1_attn_Wo"],
        "moe_q": a["L1_ffn_w_q"], "moe_k": a["L1_ffn_w_k"], "moe_gate": a["L1_ffn_w_gate"],
        "moe_v": a["L1_ffn_value_experts"].transpose(2, 0, 1, 3).reshape(P, NE, EH * EK),
        "moe_o": a["L1_ffn_output_experts"].transpose(1, 2, 0, 3).reshape(PAIRS, P, NE, C).transpose(1, 0, 2, 3),
    }
    w = {n: np.ascontiguousarray(v) for n, v in w.items()}
    w["ident"] = np.eye(P, dtype=np.float32)
    ch = np.arange(P)
    same_head = ch[:, None] // D == ch[None, :] // D
    w["sum_d"] = np.stack([same_head & (ch[None, :] % D == e) for e in range(D)], 1).astype(np.float32)
    return w


def kernel(**inputs):
    import ml_dtypes
    import concourse.bacc as _bacc
    from concourse.bass_utils import run_bass_kernel_spmd as _run

    a = {n: np.asarray(v) for n, v in inputs.items()}
    w = layouts(a)
    bf = ml_dtypes.bfloat16
    w["ident_bf"] = np.eye(P, dtype=bf)
    i = np.arange(P)
    w["mask_rows"] = np.where(i[None, :] > i[:, None], MASKED, 0.0).astype(bf)
    he = np.arange(EH * NE)
    pair, e, m = np.meshgrid(np.arange(PAIRS), np.arange(NE), np.arange(P), indexing="ij")
    w["spread"] = (he[:, None, None, None] == ((2 * pair + m // EK) * NE + e)[None]).astype(bf)
    w["rank"] = np.broadcast_to(NE - np.arange(NE, dtype=np.float32), (P, TILES * EH, NE))
    w = {n: np.ascontiguousarray(v) for n, v in w.items()}

    nc = _bacc.Bacc("TRN2", target_bir_lowering=False, num_devices=1)
    w["x"] = np.ascontiguousarray(a["L0_attn_x"])
    dram = {n: nc.dram_tensor("in_" + n, v.shape, mybir.dt.from_np(v.dtype), kind="ExternalInput").ap()
            for n, v in w.items()}
    out = nc.dram_tensor("out", (B, T, C), F32, kind="ExternalOutput").ap()
    build(nc, dram, out)
    r = _run(nc, [{"in_" + n: v for n, v in w.items()}], core_ids=[0])
    return r.results[0]["out"]
```
